# Optimizing a Trainium2 kernel written in Bass

```python
import numpy as np
import jax
import jax.numpy as jnp

def _softmax(x, axis=-1):
    return jax.nn.softmax(x, axis=axis)

def _gelu(x):
    return jax.nn.gelu(x, approximate=True)

def _silu(x):
    return jax.nn.silu(x)

def _sigmoid(x):
    return jax.nn.sigmoid(x)

def _layernorm(x, axis=-1, eps=1e-05):
    m = jnp.mean(x, axis=axis, keepdims=True)
    v = jnp.var(x, axis=axis, keepdims=True)
    return (x - m) / jnp.sqrt(v + eps)

def _scatter_add(tgt, idx, src, axis=0):
    return tgt.at[idx].add(src)

def _segment_sum(src, seg, n):
    return jax.ops.segment_sum(src, seg, n)
kernel_name = 'mk_gnn_ffn_d1_gnn_r32_6e684d'

def setup_inputs(seed: int=0):
    np.random.seed(seed)
    _w = jnp.asarray

    def _rec_inputs():
        import jax
        import jax.numpy as jnp
        _gk = jax.random.key(seed)
        x = -0.0003713 + 1 * jax.random.normal(jax.random.fold_in(_gk, 1), (3125, 256), jnp.float32)
        src = jax.random.randint(jax.random.fold_in(_gk, 2), (50000,), 0, 3125, jnp.int32)
        dst = jax.random.randint(jax.random.fold_in(_gk, 3), (50000,), 0, 3125, jnp.int32)
        _o = jnp.argsort(dst, stable=True)
        src = src[_o]
        dst = dst[_o]
        edge_attr_18 = 0.00023367 + 0.999922 * jax.random.normal(jax.random.fold_in(_gk, 11), (50000, 18), jnp.float32)
        return (x, src, dst, edge_attr_18)
    x, src, dst, edge_attr_18 = _rec_inputs()

    def _L0_gnn_setup():
        import jax, jax.numpy as jnp
        import numpy as np
        N, E = (50000, 25000)
        DIM, H, D = (256, 16, 8)
        DH = D * H
        IN_RPE = 18
        SCALE = D ** (-0.5)
        EPS = 1e-16

        def _segment_softmax(compat, s, num_nodes):
            m = jax.ops.segment_max(compat, s, num_segments=num_nodes)
            ex = jnp.exp(compat - m[s])
            den = jax.ops.segment_sum(ex, s, num_segments=num_nodes)
            return ex / (den[s] + EPS)
        key = jax.random.key(seed)
        ks = jax.random.split(key, 10)
        x = jax.random.normal(ks[0], (N, DIM), dtype=jnp.float32)
        edge_index = jax.random.randint(ks[1], (2, E), 0, N, dtype=jnp.int64)
        edge_attr = jax.random.normal(ks[2], (E, IN_RPE), dtype=jnp.float32)
        Wqkv = jax.random.normal(ks[3], (DIM, 2 * DH + DIM), dtype=jnp.float32) * DIM ** (-0.5)
        bqkv = jnp.zeros((2 * DH + DIM,), dtype=jnp.float32)
        Wk_rpe = jax.random.normal(ks[4], (IN_RPE, DH), dtype=jnp.float32) * IN_RPE ** (-0.5)
        bk_rpe = jnp.zeros((DH,), dtype=jnp.float32)
        Wq_rpe = jax.random.normal(ks[5], (IN_RPE, DH), dtype=jnp.float32) * IN_RPE ** (-0.5)
        bq_rpe = jnp.zeros((DH,), dtype=jnp.float32)
        return {'x': x, 'edge_index': edge_index, 'edge_attr': edge_attr, 'Wqkv': Wqkv, 'bqkv': bqkv, 'Wk_rpe': Wk_rpe, 'bk_rpe': bk_rpe, 'Wq_rpe': Wq_rpe, 'bq_rpe': bq_rpe}
    _L0_gnn_all = _L0_gnn_setup()
    _L0_gnn_in = {k: v for k, v in _L0_gnn_all.items() if k in ('Wqkv', 'bqkv', 'Wk_rpe', 'bk_rpe', 'Wq_rpe', 'bq_rpe')}
    del _L0_gnn_all

    def _L0_ffn_setup():
        import jax, jax.numpy as jnp
        import numpy as np
        B, S, D = (8, 128, 256)
        H = 4 * D
        CAPACITY = 0.5
        key = jax.random.key(seed)
        ks = jax.random.split(key, 6)
        x = jax.random.normal(ks[0], (B, S, D), dtype=jnp.float32)
        attention_mask = jnp.zeros((B, 1, 1, S), dtype=jnp.float32)
        wr = jax.random.normal(ks[1], (D, 1), dtype=jnp.float32) * 0.02
        br = jnp.zeros((1,), dtype=jnp.float32)
        w1 = jax.random.normal(ks[2], (D, H), dtype=jnp.float32) * 0.02
        b1 = jnp.zeros((H,), dtype=jnp.float32)
        w2 = jax.random.normal(ks[3], (H, D), dtype=jnp.float32) * 0.02
        b2 = jnp.zeros((D,), dtype=jnp.float32)
        return {'x': x, 'attention_mask': attention_mask, 'wr': wr, 'br': br, 'w1': w1, 'b1': b1, 'w2': w2, 'b2': b2}
    _L0_ffn_all = _L0_ffn_setup()
    _L0_ffn_in = {k: v for k, v in _L0_ffn_all.items() if k in ('attention_mask', 'wr', 'br', 'w1', 'b1', 'w2', 'b2')}
    del _L0_ffn_all
    return {'x': x, 'src': src, 'dst': dst, 'edge_attr_18': edge_attr_18, 'L0_gnn_Wqkv': _L0_gnn_in['Wqkv'], 'L0_gnn_bqkv': _L0_gnn_in['bqkv'], 'L0_gnn_Wk_rpe': _L0_gnn_in['Wk_rpe'], 'L0_gnn_bk_rpe': _L0_gnn_in['bk_rpe'], 'L0_gnn_Wq_rpe': _L0_gnn_in['Wq_rpe'], 'L0_gnn_bq_rpe': _L0_gnn_in['bq_rpe'], 'L0_ffn_attention_mask': _L0_ffn_in['attention_mask'], 'L0_ffn_wr': _L0_ffn_in['wr'], 'L0_ffn_br': _L0_ffn_in['br'], 'L0_ffn_w1': _L0_ffn_in['w1'], 'L0_ffn_b1': _L0_ffn_in['b1'], 'L0_ffn_w2': _L0_ffn_in['w2'], 'L0_ffn_b2': _L0_ffn_in['b2']}

def reference(x, src, dst, edge_attr_18, L0_gnn_Wqkv, L0_gnn_bqkv, L0_gnn_Wk_rpe, L0_gnn_bk_rpe, L0_gnn_Wq_rpe, L0_gnn_bq_rpe, L0_ffn_attention_mask, L0_ffn_wr, L0_ffn_br, L0_ffn_w1, L0_ffn_b1, L0_ffn_w2, L0_ffn_b2):
    import jax
    import jax.numpy as jnp

    def _L0_gnn_ref(x, edge_index, edge_attr, Wqkv, bqkv, Wk_rpe, bk_rpe, Wq_rpe, bq_rpe):
        import jax, jax.numpy as jnp
        import numpy as np
        N, E = (50000, 25000)
        DIM, H, D = (256, 16, 8)
        DH = D * H
        IN_RPE = 18
        SCALE = D ** (-0.5)
        EPS = 1e-16

        def _segment_softmax(compat, s, num_nodes):
            m = jax.ops.segment_max(compat, s, num_segments=num_nodes)
            ex = jnp.exp(compat - m[s])
            den = jax.ops.segment_sum(ex, s, num_segments=num_nodes)
            return ex / (den[s] + EPS)
        n = x.shape[0]
        e = edge_index.shape[1]
        qkv = x @ Wqkv + bqkv
        q = qkv[:, :DH].reshape(n, H, D)
        k = qkv[:, DH:2 * DH].reshape(n, H, D)
        v = qkv[:, 2 * DH:].reshape(n, H, DIM // H)
        s, t = (edge_index[0], edge_index[1])
        qe = q[s] * SCALE
        ke = k[t]
        ke = ke + (edge_attr @ Wk_rpe + bk_rpe).reshape(e, H, D)
        qe = qe + (edge_attr @ Wq_rpe + bq_rpe).reshape(e, H, D)
        compat = jnp.einsum('ehd,ehd->eh', qe, ke)
        attn = _segment_softmax(compat, s, n)
        msg = (v[t] * attn[..., None]).reshape(e, DIM)
        out = jax.ops.segment_sum(msg, s, num_segments=n)
        return out

    def _L0_ffn_ref(x, attention_mask, wr, br, w1, b1, w2, b2):
        import jax, jax.numpy as jnp
        import numpy as np
        B, S, D = (8, 128, 256)
        H = 4 * D
        CAPACITY = 0.5
        b, s, d = x.shape
        weights = (jnp.einsum('bsd,do->bso', x, wr) + br)[..., 0]
        k = max(1, int(CAPACITY * s))
        kk = k - 1 if k > 1 else 1
        _, idx = jax.lax.top_k(weights, k)
        sel_idx = idx[:, :kk]
        sel = jnp.take_along_axis(x, sel_idx[:, :, None], axis=1)
        h = jax.nn.gelu(jnp.einsum('bkd,dh->bkh', sel, w1) + b1)
        y = jnp.einsum('bkh,hd->bkd', h, w2) + b2
        w_sel = jnp.take_along_axis(weights, sel_idx, axis=1)
        y = y * w_sel[..., None]
        batch_idx = jnp.arange(b)[:, None]
        processed = jnp.zeros_like(x).at[batch_idx, sel_idx].set(y)
        return processed + x
    edge_index = jnp.stack([src, dst])
    x = x + _L0_gnn_ref(_layernorm(x, axis=-1), edge_index, edge_attr_18, L0_gnn_Wqkv, L0_gnn_bqkv, L0_gnn_Wk_rpe, L0_gnn_bk_rpe, L0_gnn_Wq_rpe, L0_gnn_bq_rpe)
    x = x + _L0_ffn_ref(_layernorm(x, axis=-1)[None], L0_ffn_attention_mask, L0_ffn_wr, L0_ffn_br, L0_ffn_w1, L0_ffn_b1, L0_ffn_w2, L0_ffn_b2)[0]
    return x

_drawn_inputs = setup_inputs


def setup_inputs(seed=0):
    import zlib

    import numpy as np

    out = dict(_drawn_inputs(seed))
    spreads = {'L0_gnn_bqkv': (0.0, 0.1),
     'L0_gnn_bk_rpe': (0.0, 0.1),
     'L0_gnn_bq_rpe': (0.0, 0.1),
     'L0_ffn_b1': (0.0, 0.8),
     'L0_ffn_b2': (0.0, 0.8)}
    factors = {'L0_ffn_wr': 4.344, 'L0_ffn_w1': 5.089, 'L0_ffn_w2': 4.731}
    for name, (base, spread) in spreads.items():
        noise = np.random.default_rng([zlib.crc32(name.encode()), seed]).standard_normal(out[name].shape)
        drawn = base * np.exp(spread * noise) if base else spread * noise
        out[name] = jnp.asarray(drawn.astype(out[name].dtype))
    for name, factor in factors.items():
        out[name] = (out[name] * factor).astype(out[name].dtype)
    return out
```

```python
from contextlib import ExitStack

import concourse.bass as bass
from concourse import mybir

F32 = mybir.dt.float32
BF16 = mybir.dt.bfloat16
I32 = mybir.dt.int32
ALU = mybir.AluOpType
ACT = mybir.ActivationFunctionType
AX = mybir.AxisListType
PE_ENGINE = mybir.EngineType.PE
DVE_ENGINE = mybir.EngineType.DVE

NODES, DIM, EDGES, ATTRS = 3125, 256, 50000, 18
HEADS, QK = 16, 128
HEAD_QK = QK // HEADS
HEAD_V = DIM // HEADS
QKV = 2 * QK + DIM
KV = QK + DIM
HIDDEN = 1024
KEPT = NODES // 2 - 1
SCALE = HEAD_QK**-0.5
EPS_LN, EPS_DEN = 1e-5, 1e-16
BIG = 1e30

BN = 125
NB = NODES // BN
EP, EC = 125, EDGES // 125
HALF = 8
STEPS = EC // (2 * HALF)
TILE = 128
SC = 16
NSC = -(-(EDGES // TILE + NB) // SC)
NT = NSC * SC
PARTS = 8
PT = SC // PARTS
BATCH = 4
NBATCH = SC // BATCH
ONE, SRC, LOW, DST, WIDE = ATTRS, ATTRS + 1, ATTRS + 2, ATTRS + 3, ATTRS + 4
VD = HEAD_V + 1
ACCW = HEADS * VD
GCOL = NT // 4

assert NB * BN == NODES and STEPS * 2 * HALF == EC and STEPS == NB and NT == 4 * GCOL
assert PARTS * HEADS == 128


def gnn_ffn_kernel(nc, x, src, dst, attrs, Wqkv, bqkv, Wk, bk, Wq, bq, mask, wr, br, w1, b1, w2, b2, out):
    records = nc.dram_tensor("edge_records", [NT * TILE, WIDE], F32, kind="Internal").ap()
    kv_rows = nc.dram_tensor("kv_rows", [NODES, KV], F32, kind="Internal").ap()
    route_dram = nc.dram_tensor("route_dram", [NODES], F32, kind="Internal").ap()

    with ExitStack() as keep:
        def lasting(name, shape, dt=F32):
            return keep.enter_context(nc.sbuf_tensor(name, shape, dt))

        c = {
            "x": lasting("x_sb", [BN, NB, DIM]),
            "q": lasting("q_sb", [BN, NB, QK]),
            "bucket_of_tile": lasting("bucket_of_tile", [1, NT], I32),
            "ident": lasting("ident", [128, 128]),
            "iota": lasting("iota_row", [128, 128]),
            "below": lasting("below", [128, 128]),
            "above": lasting("above", [128, 128]),
            "ones": lasting("ones", [128, 128]),
        }
        order_edges(nc, c, x, src, dst, attrs, Wqkv, bqkv, records, kv_rows)
        c["acc"] = lasting("acc", [BN, NB, ACCW])
        attend(nc, c, records, kv_rows, Wk, bk, Wq, bq)
        feed_forward(nc, c, wr, br, w1, b1, w2, b2, route_dram, out)


def order_edges(nc, c, x, src, dst, attrs, Wqkv, bqkv, records, kv_rows):
    with ExitStack() as ctx:
        def sb(name, shape, dt=F32):
            return ctx.enter_context(nc.sbuf_tensor(name, shape, dt))

        def sem(name):
            return ctx.enter_context(nc.semaphore(name))

        src_i = sb("src_i", [EP, EC], I32)
        dst_i = sb("dst_i", [EP, EC], I32)
        src_f = sb("src_f", [EP, EC])
        low_f = sb("low_f", [EP, EC])
        high_f = sb("high_f", [EP, EC])
        fix = sb("fix", [EP, EC])
        high_i = sb("high_i", [EP, EC], I32)
        attr_sb = sb("attr_sb", [EP, EC * ATTRS])
        table = sb("table", [BN, NB, EC + 1])
        total_i = sb("total_i", [BN, NB], I32)
        tiles_i = sb("tiles_i", [BN, NB], I32)
        tiles_f = sb("tiles_f", [BN, NB])
        tile_end = sb("tile_end", [BN, NB])
        tile_start = sb("tile_start", [BN, NB])
        base = sb("base", [BN, NB])
        tile_no_i = sb("tile_no_i", [GCOL, 4], I32)
        tile_no = sb("tile_no", [GCOL, 4])
        passed = sb("passed", [GCOL, 4, NB])
        bucket_col = sb("bucket_col", [GCOL, 4])
        iota_i = sb("iota_i", [128, 128], I32)
        iota_b = sb("iota_b", [128, 128], BF16)
        empty = sb("empty", [128, NT // 16, WIDE])
        bqkv_sb = sb("bqkv_sb", [BN, QKV])
        wqkv_sb = sb("wqkv_sb", [128, 2, QKV])

        ps = [ctx.enter_context(nc.psum_tensor(f"ps_a{i}", [128, 512], F32)) for i in range(8)]

        with ExitStack() as first:
            def sb1(name, shape, dt=F32):
                return first.enter_context(nc.sbuf_tensor(name, shape, dt))

            def sem1(name):
                return first.enter_context(nc.semaphore(name))

            low_hot = sb1("low_hot", [EP, 2, HALF, BN], BF16)
            high_hot = sb1("high_hot", [EP, 2, HALF, NB], BF16)
            edges_in = sem1("edges_in")
            nodes_in = sem1("nodes_in")
            prefilled = sem1("prefilled")
            made = sem1("made")
            digits = sem1("digits")
            hot_ready = sem1("hot_ready")
            counts_ready = sem1("counts_ready")
            table_filled = sem1("table_filled")
            summed = sem1("summed")
            totals_ready = sem1("totals_ready")
            layout_step = sem1("layout_step")
            buckets_ready = sem1("buckets_ready")
            block = first.enter_context(nc.Block())

            @block.sync
            def _(sp):
                sp.dma_start(src_i[:], src.rearrange("(p c) -> p c", c=EC)).then_inc(edges_in, 16)
                sp.dma_start(c["x"][:], x.rearrange("(b p) d -> p b d", p=BN)).then_inc(nodes_in, 16)
                sp.dma_start(dst_i[:], dst.rearrange("(p c) -> p c", c=EC)).then_inc(nodes_in, 16)
                sp.dma_start(attr_sb[:], attrs.rearrange("(p c) a -> p (c a)", c=EC)).then_inc(nodes_in, 16)
                sp.dma_start(wqkv_sb[:], Wqkv.rearrange("(k p) n -> p k n", p=128)).then_inc(nodes_in, 16)
                sp.dma_start(bqkv_sb[:], bqkv.rearrange("(a n) -> a n", a=1).broadcast_to([BN, QKV])).then_inc(nodes_in, 16)
                sp.wait_ge(made, 10)
                records_v = records.rearrange("(p a r) w -> a p (r w)", p=128, a=16)
                for a in range(16):
                    sp.dma_start(records_v[a], empty[:].rearrange("p r w -> p (r w)")).then_inc(prefilled, 16)
                sp.wait_ge(nodes_in, 16 * 5)
                sp.wait_ge(prefilled, 16 * 16)

            @block.gpsimd
            def _(pool):
                nc.gpsimd.iota(iota_i[:], pattern=[[1, 128]], base=0, channel_multiplier=0).then_inc(made, 1)
                nc.gpsimd.iota(tile_no_i[:], pattern=[[GCOL, 4]], base=0, channel_multiplier=1).then_inc(made, 1)
                nc.gpsimd.memset(c["ident"][:], 0.0).then_inc(made, 1)
                nc.gpsimd.memset(c["ones"][:], 1.0).then_inc(made, 1)
                pool.wait_ge(made, 4)
                nc.gpsimd.affine_select(out=c["ident"][:], in_=c["ident"][:], compare_op=ALU.not_equal, fill=1.0,
                                        base=0, pattern=[[-1, 128]], channel_multiplier=1).then_inc(made, 1)
                nc.gpsimd.affine_select(out=c["below"][:], in_=c["ones"][:], compare_op=ALU.is_gt, fill=0.0,
                                        base=0, pattern=[[-1, 128]], channel_multiplier=1).then_inc(made, 1)
                nc.gpsimd.affine_select(out=c["above"][:], in_=c["ones"][:], compare_op=ALU.is_gt, fill=0.0,
                                        base=0, pattern=[[1, 128]], channel_multiplier=-1).then_inc(made, 1)
                nc.gpsimd.memset(empty[:], 0.0).then_inc(made, 1)
                pool.wait_ge(made, 8)
                nc.gpsimd.memset(empty[:, :, SRC], -1.0).then_inc(made, 1)
                nc.gpsimd.memset(empty[:, :, LOW], -1.0).then_inc(made, 1)

            @block.vector
            def _(dve):
                dve.wait_ge(made, 2)
                nc.vector.tensor_copy(c["iota"][:], iota_i[:]).then_inc(digits, 1)
                nc.vector.tensor_copy(iota_b[:], iota_i[:]).then_inc(digits, 1)
                nc.vector.tensor_copy(tile_no[:], tile_no_i[:]).then_inc(digits, 1)
                nc.vector.memset(table[:, :, 0:1], 0.0).then_inc(digits, 1)
                dve.wait_ge(edges_in, 16)
                nc.vector.tensor_copy(src_f[:], src_i[:]).then_inc(digits, 1)
                dve.wait_ge(digits, 5)
                nc.vector.tensor_scalar(high_i[:], src_f[:], 1.0 / BN, None, ALU.mult).then_inc(digits, 1)
                dve.wait_ge(digits, 6)
                nc.vector.tensor_copy(high_f[:], high_i[:]).then_inc(digits, 1)
                dve.wait_ge(digits, 7)
                nc.vector.scalar_tensor_tensor(low_f[:], high_f[:], -float(BN), src_f[:], ALU.mult, ALU.add).then_inc(digits, 1)
                dve.wait_ge(digits, 8)
                nc.vector.tensor_scalar(fix[:], low_f[:], 0.0, None, ALU.is_lt).then_inc(digits, 1)
                dve.wait_ge(digits, 9)
                nc.vector.tensor_tensor(high_f[:], high_f[:], fix[:], ALU.subtract).then_inc(digits, 1)
                nc.vector.scalar_tensor_tensor(low_f[:], fix[:], float(BN), low_f[:], ALU.mult, ALU.add).then_inc(digits, 1)
                dve.wait_ge(digits, 11)
                nc.vector.tensor_scalar(fix[:], low_f[:], float(BN), None, ALU.is_ge).then_inc(digits, 1)
                dve.wait_ge(digits, 12)
                nc.vector.tensor_tensor(high_f[:], high_f[:], fix[:], ALU.add).then_inc(digits, 1)
                nc.vector.scalar_tensor_tensor(low_f[:], fix[:], -float(BN), low_f[:], ALU.mult, ALU.add).then_inc(digits, 1)
                dve.wait_ge(digits, 14)

                with dve.Fori(0, STEPS) as i:
                    for u in range(2):
                        col = bass.ds(i * (2 * HALF) + u * HALF, HALF)
                        dve.wait_ge(counts_ready, i * 2 + (u + 1))
                        nc.vector.tensor_tensor(low_hot[:, u], iota_b[0:EP, None, 0:BN].broadcast_to([EP, HALF, BN]),
                                                low_f[:, col].unsqueeze(2).broadcast_to([EP, HALF, BN]), ALU.is_equal)
                        nc.vector.tensor_tensor(high_hot[:, u], iota_b[0:EP, None, 0:NB].broadcast_to([EP, HALF, NB]),
                                                high_f[:, col].unsqueeze(2).broadcast_to([EP, HALF, NB]), ALU.is_equal).then_inc(hot_ready, 1)

                dve.wait_ge(table_filled, 2 + 2 * STEPS)
                for b in range(NB):
                    nc.vector.tensor_tensor_scan(table[:, b, 1:], table[:, b, 1:], table[:, b, 1:], 0.0, ALU.add, ALU.max).then_inc(summed, 1)

                dve.wait_ge(totals_ready, 2)
                nc.vector.tensor_scalar(total_i[:], ps[0][0:BN, 0:NB], float(TILE - 1), None, ALU.add).then_inc(layout_step, 1)
                dve.wait_ge(layout_step, 1)
                nc.vector.tensor_scalar(tiles_i[:], total_i[:], 7, None, ALU.logical_shift_right).then_inc(layout_step, 1)
                dve.wait_ge(layout_step, 2)
                nc.vector.tensor_copy(tiles_f[:], tiles_i[:]).then_inc(layout_step, 1)
                dve.wait_ge(layout_step, 3)
                nc.vector.tensor_tensor_scan(tile_end[:], tiles_f[:], tiles_f[:], 0.0, ALU.add, ALU.max).then_inc(layout_step, 1)
                dve.wait_ge(layout_step, 4)
                nc.vector.tensor_tensor(tile_start[:], tile_end[:], tiles_f[:], ALU.subtract).then_inc(layout_step, 1)
                nc.vector.tensor_tensor(passed[:], tile_end[0:GCOL, None, :].broadcast_to([GCOL, 4, NB]),
                                        tile_no[:].unsqueeze(2).broadcast_to([GCOL, 4, NB]), ALU.is_le).then_inc(layout_step, 1)
                dve.wait_ge(layout_step, 6)
                nc.vector.scalar_tensor_tensor(base[:], tile_start[:], float(TILE), ps[1][0:BN, 0:NB], ALU.mult, ALU.add).then_inc(layout_step, 1)
                nc.vector.tensor_reduce(bucket_col[:], passed[:], AX.X, ALU.add).then_inc(layout_step, 1)
                dve.wait_ge(layout_step, 8)
                nc.vector.tensor_scalar(bucket_col[:], bucket_col[:], float(NB - 1), None, ALU.min).then_inc(layout_step, 1)
                dve.wait_ge(buckets_ready, 1)
                nc.vector.tensor_copy(c["bucket_of_tile"][:], ps[2][0:1, 0:NT])

            @block.tensor
            def _(pe):
                pe.sem_inc(counts_ready, 2)
                with pe.Fori(0, STEPS) as i:
                    for u in range(2):
                        pe.wait_ge(hot_ready, i * 2 + (u + 1))
                        pe.wait_ge(table_filled, i * 2 + (u + 1))
                        for k in range(HALF):
                            last = nc.tensor.matmul(ps[u][0:BN, k * NB:(k + 1) * NB], low_hot[:, u, k], high_hot[:, u, k], start=True, stop=True)
                        last.then_inc(counts_ready, 1)
                pe.wait_ge(summed, NB)
                pe.wait_ge(made, 7)
                pe.wait_ge(table_filled, 2 + 2 * STEPS)
                nc.tensor.matmul(ps[0][0:BN, 0:NB], c["ones"][0:BN, 0:BN], table[:, :, EC], start=True, stop=True).then_inc(totals_ready, 1)
                nc.tensor.matmul(ps[1][0:BN, 0:NB], c["above"][0:BN, 0:BN], table[:, :, EC], start=True, stop=True).then_inc(totals_ready, 1)
                pe.wait_ge(layout_step, 9)
                for k in range(4):
                    last = nc.tensor.matmul(ps[2][0:1, k * GCOL:(k + 1) * GCOL], bucket_col[:, k:k + 1], c["ident"][0:GCOL, 0:GCOL], start=True, stop=True)
                last.then_inc(buckets_ready, 1)

            @block.scalar
            def _(act):
                act.sem_inc(table_filled, 2)
                with act.Fori(0, STEPS) as i:
                    for u in range(2):
                        act.wait_ge(counts_ready, i * 2 + (u + 3))
                        nc.scalar.activation(table[:, :, bass.ds(i * (2 * HALF) + (u * HALF + 1), HALF)],
                                             ps[u][0:BN, 0:HALF * NB].rearrange("p (k b) -> p b k", b=NB), ACT.Copy).then_inc(table_filled, 1)

        place_edges(nc, c, ps, src_f, low_f, high_f, dst_i, attr_sb, table, base, wqkv_sb, bqkv_sb, records, kv_rows)


def place_edges(nc, c, ps, src_f, low_f, high_f, dst_i, attr_sb, table, base, wqkv_sb, bqkv_sb, records, kv_rows):
    with ExitStack() as ctx:
        def sb(name, shape, dt=F32):
            return ctx.enter_context(nc.sbuf_tensor(name, shape, dt))

        def sem(name):
            return ctx.enter_context(nc.semaphore(name))

        low_hot = sb("low_hot_f", [EP, 2, HALF, BN])
        low_rows = sb("low_rows", [BN, 2, HALF, EP])
        src_diag = sb("src_diag", [EP, 2, HALF, EP])
        high_hot = sb("high_hot_f", [EP, HALF, NB])
        same_before = sb("same_before", [EP, HALF, EP])
        rank = sb("rank", [EP, HALF])
        picked = sb("picked", [EP, HALF, NB])
        offset = sb("offset", [EP, HALF])
        slot = sb("slot", [EP, 2, HALF], I32)
        record = sb("record", [EP, 2, HALF, WIDE])
        stats = sb("stats", [BN, 6])
        mean_var = sb("mean_var", [BN, 2])
        spread = sb("spread", [BN, 3])
        normed = sb("normed", [BN, DIM])
        normed_t = sb("normed_t", [128, 2, BN])
        kv_out = sb("kv_out", [BN, KV])
        bq_scaled = sb("bq_scaled", [BN, QK])

        low_onehot = sem("low_onehot")
        diag_ready = sem("diag_ready")
        low_transposed = sem("low_transposed")
        low_rows_ready = sem("low_rows_ready")
        src_rows_ready = sem("src_rows_ready")
        ranks_ready = sem("ranks_ready")
        high_ready = sem("high_ready")
        looked_up = sem("looked_up")
        picked_ready = sem("picked_ready")
        offset_ready = sem("offset_ready")
        slots_ready = sem("slots_ready")
        records_built = sem("records_built")
        scattered = [sem(f"scattered{u}") for u in range(2)]
        ln_step = sem("ln_step")
        root_ready = sem("root_ready")
        normed_ready = sem("normed_ready")
        node_transposed = sem("node_transposed")
        normed_rows = sem("normed_rows")
        qkv_ready = sem("qkv_ready")
        q_ready = sem("q_ready")
        kv_ready = sem("kv_ready")
        kv_stored = sem("kv_stored")
        bias_ready = sem("bias_ready")
        ones_set = sem("ones_set")
        records_free = sem("records_free")
        kv_out_free = sem("kv_out_free")
        scatters_begun = sem("scatters_begun")
        block = ctx.enter_context(nc.Block())
        T0, S0, L0, X0, W0 = ps[0:2], ps[2:4], ps[4], ps[5], ps[6]

        @block.sync
        def _(sp):
            with sp.Fori(0, STEPS) as i:
                sp.wait_ge(scattered[0], (i + 1) * (16 * HALF))
                sp.sem_inc(records_free, 1)
                sp.wait_ge(kv_ready, i + 1)
                sp.dma_start(kv_rows[bass.ds(i * BN, BN), :], kv_out[:]).then_inc(kv_stored, 16)
                sp.wait_ge(scattered[1], (i + 1) * (16 * HALF))
                sp.sem_inc(records_free, 1)
                sp.wait_ge(kv_stored, (i + 1) * 16)
                sp.sem_inc(kv_out_free, 1)

        @block.gpsimd
        def _(pool):
            nc.gpsimd.memset(record[:, :, :, ONE], 1.0).then_inc(ones_set, 1)
            with pool.Fori(0, STEPS) as i:
                for u in range(2):
                    pool.wait_ge(records_built, i * 2 + (u + 1))
                    pool.wait_ge(slots_ready, i * 2 + (u + 1))
                    pool.sem_inc(scatters_begun, 1)
                    for k in range(HALF):
                        nc.gpsimd.indirect_dma_start(
                            out=records, out_offset=bass.IndirectOffsetOnAxis(ap=slot[:, u, k:k + 1], axis=0),
                            in_=record[:, u, k, :], in_offset=None).then_inc(scattered[u], 16)
            for u in range(2):
                pool.wait_ge(scattered[u], 16 * HALF * STEPS)

        @block.scalar
        def _(act):
            act.sem_inc(low_rows_ready, 1)
            act.wait_ge(ones_set, 1)
            with act.Fori(0, STEPS) as i:
                for u in range(2):
                    j = i * (2 * HALF) + u * HALF
                    act.wait_ge(records_free, i * 2 + (u + 1))
                    act.activation(record[:, u, :, 0:ATTRS], attr_sb[:, bass.ds(j * ATTRS, HALF * ATTRS)].rearrange("p (k a) -> p k a", a=ATTRS), ACT.Copy)
                    act.activation(record[:, u, :, SRC], src_f[:, bass.ds(j, HALF)], ACT.Copy)
                    act.activation(record[:, u, :, LOW], low_f[:, bass.ds(j, HALF)], ACT.Copy)
                    act.activation(record[:, u, :, DST].bitcast(I32), dst_i[:, bass.ds(j, HALF)], ACT.Copy).then_inc(records_built, 1)
                    if u == 0:
                        act.wait_ge(ln_step, (i + 1) * 3)
                        act.activation(spread[:, 1:2], spread[:, 0:1], ACT.Sqrt).then_inc(root_ready, 1)
                    act.wait_ge(low_transposed, i * 2 + (u + 3))
                    act.wait_ge(looked_up, i * 2 + (u + 1))
                    for h in range(2):
                        last = act.activation(low_rows[:, u, h * 4:h * 4 + 4, :].rearrange("p a b -> p (a b)"), T0[h][0:BN, 0:4 * EP], ACT.Copy)
                    last.then_inc(low_rows_ready, 1)
                    if u == 0:
                        act.wait_ge(node_transposed, i + 1)
                        act.activation(normed_t[:].rearrange("p a b -> p (a b)"), X0[:, 0:2 * BN], ACT.Copy).then_inc(normed_rows, 1)

        @block.vector
        def _(dve):
            dve.sem_inc(ranks_ready, 1)
            dve.sem_inc(picked_ready, 1)
            nc.vector.tensor_scalar(bq_scaled[:], bqkv_sb[:, 0:QK], SCALE, None, ALU.mult).then_inc(bias_ready, 1)
            dve.wait_ge(bias_ready, 1)
            with dve.Fori(0, STEPS) as i:
                for u in range(2):
                    col = bass.ds(i * (2 * HALF) + u * HALF, HALF)
                    n = i * 2 + u
                    dve.wait_ge(low_transposed, n + 1)
                    nc.vector.tensor_tensor(low_hot[:, u], c["iota"][0:EP, None, 0:BN].broadcast_to([EP, HALF, BN]),
                                            low_f[:, col].unsqueeze(2).broadcast_to([EP, HALF, BN]), ALU.is_equal).then_inc(low_onehot, 1)
                    dve.wait_ge(src_rows_ready, n + 1)
                    nc.vector.tensor_tensor(src_diag[:, u], c["ident"][0:EP, None, 0:EP].broadcast_to([EP, HALF, EP]),
                                            src_f[:, col].unsqueeze(2).broadcast_to([EP, HALF, EP]), ALU.mult).then_inc(diag_ready, 1)
                    if u == 0:
                        nc.vector.bn_stats(stats[:], c["x"][:, bass.ds(i, 1), :].rearrange("p a d -> p (a d)")).then_inc(ln_step, 1)
                        dve.wait_ge(ln_step, i * 3 + 1)
                    nc.vector.tensor_tensor(high_hot[:], c["iota"][0:EP, None, 0:NB].broadcast_to([EP, HALF, NB]),
                                            high_f[:, col].unsqueeze(2).broadcast_to([EP, HALF, NB]), ALU.is_equal).then_inc(high_ready, 1)
                    if u == 0:
                        nc.vector.bn_aggr(mean_var[:], stats[:]).then_inc(ln_step, 1)
                        dve.wait_ge(ln_step, i * 3 + 2)
                        nc.vector.tensor_scalar(spread[:, 0:1], mean_var[:, 1:2], EPS_LN, None, ALU.add).then_inc(ln_step, 1)
                    dve.wait_ge(src_rows_ready, n + 3)
                    for k in range(HALF):
                        last = nc.vector.scalar_tensor_tensor(
                            same_before[:, k], S0[k // 4][0:EP, (k % 4) * EP:(k % 4 + 1) * EP],
                            src_f[:, bass.ds(i * (2 * HALF) + (u * HALF + k), 1)], c["below"][0:EP, 0:EP],
                            ALU.is_equal, ALU.mult, accum_out=rank[:, k:k + 1])
                    last.then_inc(ranks_ready, 1)
                    if u == 0:
                        dve.wait_ge(root_ready, i + 1)
                        nc.vector.reciprocal(spread[:, 2:3], spread[:, 1:2]).then_inc(bias_ready, 1)
                        dve.wait_ge(bias_ready, i + 2)
                        nc.vector.tensor_scalar(normed[:], c["x"][:, bass.ds(i, 1), :].rearrange("p a d -> p (a d)"),
                                                mean_var[:, 0:1], spread[:, 2:3], ALU.subtract, ALU.mult).then_inc(normed_ready, 1)
                    dve.wait_ge(looked_up, n + 3)
                    dve.wait_ge(high_ready, n + 1)
                    nc.vector.tensor_tensor(picked[:], L0[0:EP, 0:HALF * NB].rearrange("p (k b) -> p k b", b=NB), high_hot[:], ALU.mult).then_inc(picked_ready, 1)
                    dve.wait_ge(picked_ready, n + 2)
                    nc.vector.tensor_reduce(offset[:], picked[:], AX.X, ALU.add).then_inc(offset_ready, 1)
                    dve.wait_ge(offset_ready, n + 1)
                    dve.wait_ge(ranks_ready, n + 2)
                    dve.wait_ge(records_free, n + 1)
                    nc.vector.tensor_tensor(slot[:, u], offset[:], rank[:], ALU.add).then_inc(slots_ready, 1)
                    if u == 1:
                        dve.wait_ge(qkv_ready, i + 1)
                        nc.vector.scalar_tensor_tensor(c["q"][:, bass.ds(i, 1), :].rearrange("p a d -> p (a d)"), W0[0:BN, 0:QK], SCALE,
                                                       bq_scaled[:], ALU.mult, ALU.add)
                        dve.wait_ge(kv_out_free, i + 1)
                        nc.vector.tensor_tensor(kv_out[:], W0[0:BN, QK:QKV], bqkv_sb[:, QK:QKV], ALU.add).then_inc(kv_ready, 1)

        @block.tensor
        def _(pe):
            pe.sem_inc(low_transposed, 2)
            pe.sem_inc(src_rows_ready, 2)
            pe.sem_inc(looked_up, 2)
            pe.sem_inc(records_free, 2)
            pe.sem_inc(kv_out_free, 1)
            with pe.Fori(0, STEPS) as i:
                for u in range(2):
                    n = i * 2 + u
                    pe.wait_ge(low_onehot, n + 1)
                    pe.wait_ge(low_rows_ready, n + 1)
                    for k in range(HALF):
                        last = nc.tensor.transpose(T0[k // 4][0:BN, (k % 4) * EP:(k % 4 + 1) * EP], low_hot[:, u, k], c["ident"][0:EP, 0:EP])
                    last.then_inc(low_transposed, 1)
                    pe.wait_ge(diag_ready, n + 1)
                    pe.wait_ge(ranks_ready, n + 1)
                    for h in range(2):
                        last = nc.tensor.matmul(S0[h][0:EP, 0:4 * EP], c["ones"][0:EP, 0:EP],
                                                src_diag[:, u, h * 4:h * 4 + 4, :].rearrange("p a b -> p (a b)"), start=True, stop=True)
                    last.then_inc(src_rows_ready, 1)
                    pe.wait_ge(low_rows_ready, n + 2)
                    pe.wait_ge(picked_ready, n + 1)
                    for k in range(HALF):
                        before = table[:, :, bass.ds(i * (2 * HALF) + (u * HALF + k), 1)].rearrange("p b a -> p (b a)")
                        nc.tensor.matmul(L0[0:EP, k * NB:(k + 1) * NB], low_rows[:, u, k], before, start=True, stop=False)
                        last = nc.tensor.matmul(L0[0:EP, k * NB:(k + 1) * NB], low_rows[:, u, k], base[:], start=False, stop=True)
                    last.then_inc(looked_up, 1)
                    if u == 0:
                        pe.wait_ge(normed_ready, i + 1)
                        for h in range(2):
                            last = nc.tensor.transpose(X0[:, h * BN:(h + 1) * BN], normed[:, h * 128:(h + 1) * 128], c["ident"][0:BN, 0:BN])
                        last.then_inc(node_transposed, 1)
                        pe.wait_ge(normed_rows, i + 1)
                        for h in range(2):
                            last = nc.tensor.matmul(W0[0:BN, :], normed_t[:, h, :], wqkv_sb[:, h, :], start=(h == 0), stop=(h == 1))
                        last.then_inc(qkv_ready, 1)


def attend(nc, c, records, kv_rows, Wk, bk, Wq, bq):
    with ExitStack() as ctx:
        def sb(name, shape, dt=F32):
            return ctx.enter_context(nc.sbuf_tensor(name, shape, dt))

        def ps(name):
            return ctx.enter_context(nc.psum_tensor(name, [128, 512], F32))

        def sem(name):
            return ctx.enter_context(nc.semaphore(name))

        iota, ident, ones, acc = c["iota"], c["ident"], c["ones"], c["acc"]
        gt = c["bucket_of_tile"]
        K = ATTRS + 1
        rec = sb("rec", [128, 2, SC, WIDE])
        kv = sb("kv", [128, 2, SC, KV])
        onehot = sb("onehot", [128, 2, SC, BN])
        wrpe = sb("wrpe", [K, 2, QK])
        attr_rows = sb("attr_rows", [K, BATCH * 128])
        node_rows = sb("node_rows", [BN, BATCH * 128])
        keys = sb("keys", [128, BATCH * QK])
        product = sb("product", [128, BATCH * QK])
        score = sb("score", [128, PT, PARTS, HEADS])
        src_wide = sb("src_wide", [128, PT, PARTS, HEADS])
        W = PT * 128
        cs = sb("score_src_rows", [128, 2 * W])
        changes = sb("changes", [128, W + 1])
        run = sb("run", [128, 4, W])
        edges = sb("edge_rows", [1, 2, 2, HEADS, PARTS + 1])
        gap = sb("gap", [1, HEADS, PARTS + 1])
        split = sb("split", [1, HEADS, PARTS + 1])
        pen_f = sb("pen_f", [1, HEADS, PARTS + 1])
        pen_b = sb("pen_b", [1, HEADS, PARTS + 1])
        chain_f = sb("chain_f", [1, HEADS, PARTS + 1])
        chain_b = sb("chain_b", [1, HEADS, PARTS + 1])
        carry_rows = sb("carry_rows", [1, 2, PARTS, HEADS])
        carry = sb("carry", [128, 2])
        shifted = sb("shifted", [128, W + 1])
        weight_rows = sb("weight_rows", [128, W + 1])
        factor = sb("factor", [HEADS, HEADS])
        first_node = sb("first_node", [BN, 1])
        rescale = sb("rescale", [BN, HEADS])
        weights = sb("weights", [128, SC, HEADS])
        weighted = sb("weighted", [128, 2, BATCH, HEADS, VD])

        P_attr, P_node, P_q, P_k, P_z0, P_z1, P_rows, P_misc = [ps(f"ps_c{i}") for i in range(8)]
        P_z = [P_z0, P_z1]

        weights_in = sem("weights_in")
        cleared = sem("cleared")
        records_in = [sem(f"records_in{i}") for i in range(2)]
        records_free = sem("records_free2")
        indices_seen = sem("indices_seen")
        kv_in = [sem(f"kv_in{i}") for i in range(2 * NBATCH)]
        onehot_ready = sem("onehot_ready")
        attr_transposed = sem("attr_transposed")
        attr_rows_ready = sem("attr_rows_ready")
        node_transposed = sem("node_transposed2")
        node_rows_ready = sem("node_rows_ready")
        qk_ready = sem("qk_ready")
        keys_ready = sem("keys_ready")
        product_ready = sem("product_ready")
        score_ready = sem("score_ready")
        src_wide_ready = sem("src_wide_ready")
        rows_transposed = sem("rows_transposed")
        rows_ready = sem("rows_ready")
        max_step = sem("max_step")
        ends_transposed = sem("ends_transposed")
        ends_ready = sem("ends_ready")
        carry_transposed = sem("carry_transposed")
        carry_seen = sem("carry_seen")
        shifted_ready = sem("shifted_ready")
        exp_ready = sem("exp_ready")
        weights_transposed = sem("weights_transposed")
        weights_ready = sem("weights_ready")
        factor_spread = sem("factor_spread")
        rescaled = sem("rescaled")
        den_ready = sem("den_ready")
        weighted_ready = sem("weighted_ready")
        sums_ready = sem("sums_ready")
        added = sem("added")
        acc_rescaled = sem("acc_rescaled")
        MAX_STEPS = 19

        block = ctx.enter_context(nc.Block())

        def groups(eng, score_of, maxima_of, sums_of):
            for b in range(NBATCH):
                score_of(0, 0, b)
            maxima_of(0, 0)
            with eng.Fori(0, (NSC - 2) // 2) as it:
                for u in range(2):
                    n, m = it * 2 + (u + 1), it * 2 + u
                    state = {}
                    for b in range(NBATCH):
                        score_of(n, 1 - u, b, state)
                        sums_of(m, u, b, state)
                    maxima_of(n, 1 - u)
            state = {}
            for b in range(NBATCH):
                score_of(NSC - 1, 1, b, state)
                sums_of(NSC - 2, 0, b, state)
            maxima_of(NSC - 1, 1)
            state = {}
            for b in range(NBATCH):
                sums_of(NSC - 1, 1, b, state)

        def buckets(engine, n, count):
            _, regs = nc.values_load_multi_w_load_instructions(gt[0:1, bass.ds(n * SC, count)], engines=[engine], min_val=0, max_val=NB - 1)
            return regs

        def nothing(*_):
            pass

        @block.sync
        def _(sp):
            sp.dma_start(wrpe[0:ATTRS, 0, :], Wq).then_inc(weights_in, 16)
            sp.dma_start(wrpe[ATTRS:K, 0, :], bq.rearrange("(a n) -> a n", a=1)).then_inc(weights_in, 16)
            sp.dma_start(wrpe[0:ATTRS, 1, :], Wk).then_inc(weights_in, 16)
            sp.dma_start(wrpe[ATTRS:K, 1, :], bk.rearrange("(a n) -> a n", a=1)).then_inc(weights_in, 16)
            records_v = records.rearrange("(n t p) w -> n p t w", t=SC, p=128)
            with sp.Fori(0, NSC // 2) as it:
                for u in range(2):
                    n = it * 2 + u
                    sp.wait_ge(score_ready, n * NBATCH + 1)
                    sp.sem_inc(records_free, 1)
                    sp.wait_ge(src_wide_ready, n + 1)
                    sp.sem_inc(records_free, 1)
                    sp.dma_start(rec[:, u], records_v[bass.ds(n, 1)].rearrange("a p t w -> p (a t) w")).then_inc(records_in[u], 16)

        @block.gpsimd
        def _(pool):
            nc.gpsimd.memset(acc[:], 0.0).then_inc(cleared, 1)
            nc.gpsimd.memset(changes[:], 0.0).then_inc(cleared, 1)
            nc.gpsimd.memset(edges[:], -BIG).then_inc(cleared, 1)
            nc.gpsimd.memset(gap[:], -BIG).then_inc(cleared, 1)
            nc.gpsimd.memset(pen_f[:], -BIG).then_inc(cleared, 1)
            nc.gpsimd.memset(pen_b[:], -BIG).then_inc(cleared, 1)
            nc.gpsimd.memset(shifted[:], 0.0).then_inc(cleared, 1)
            with pool.Fori(0, NSC // 2) as it:
                for u in range(2):
                    n = it * 2 + u
                    pool.wait_ge(records_in[u], it * 16 + 16)
                    pool.sem_inc(indices_seen, 1)
                    for b in range(NBATCH):
                        pool.wait_ge(weighted_ready, n * NBATCH + (b + 1))
                        pool.sem_inc(indices_seen, 1)
                        for t in range(b * BATCH, (b + 1) * BATCH):
                            nc.gpsimd.indirect_dma_start(
                                out=kv[:, u, t, :], out_offset=None, in_=kv_rows,
                                in_offset=bass.IndirectOffsetOnAxis(ap=rec[:, u, t, DST:DST + 1].bitcast(I32), axis=0)
                            ).then_inc(kv_in[u * NBATCH + b], 16)

        @block.scalar
        def _(act):
            act.sem_inc(attr_rows_ready, 1)
            act.sem_inc(node_rows_ready, 1)
            act.sem_inc(rows_ready, 1)
            act.sem_inc(src_wide_ready, 2)
            act.sem_inc(weights_ready, 1)

            def score_of(n, p, b, state=None):
                B = n * NBATCH + b
                if b == 0:
                    act.wait_ge(records_in[p], (n - p) * 8 + 16)
                    act.wait_ge(rows_transposed, n + 1)
                    nc.scalar.activation(src_wide[:].rearrange("p i k h -> p k i h"),
                                         rec[:, p, :, SRC:SRC + 1].rearrange("p (k i) a -> p k i a", i=PT).broadcast_to([128, PARTS, PT, HEADS]),
                                         ACT.Copy).then_inc(src_wide_ready, 1)
                act.wait_ge(attr_transposed, B + 1)
                act.wait_ge(qk_ready, B + 1)
                nc.scalar.activation(attr_rows[:], P_attr[0:K, :], ACT.Copy).then_inc(attr_rows_ready, 1)
                act.wait_ge(node_transposed, B + 1)
                if b == 0:
                    act.wait_ge(rescaled, n + 1)
                    nc.scalar.activation(first_node[:], P_node[0:BN, 0:1], ACT.Copy)
                nc.scalar.activation(node_rows[:], P_node[0:BN, :], ACT.Copy).then_inc(node_rows_ready, 1)

            def maxima_of(n, p):
                act.wait_ge(rows_transposed, n + 2)
                act.wait_ge(shifted_ready, n + 1)
                nc.scalar.activation(cs[:], P_rows[:], ACT.Copy).then_inc(rows_ready, 1)
                act.wait_ge(ends_transposed, n + 1)
                act.wait_ge(shifted_ready, n + 1)
                r = P_misc[0:1, :].rearrange("a (e j k h) -> a e j h k", e=2, j=2, h=HEADS)
                act.activation(edges[:, 0, :, :, 0:PARTS], r[:, 0], ACT.Copy)
                act.activation(edges[:, 1, :, :, 1:PARTS + 1], r[:, 1], ACT.Copy).then_inc(ends_ready, 1)
                act.wait_ge(shifted_ready, n + 2)
                act.wait_ge(weights_transposed, n + 1)
                nc.scalar.activation(weight_rows[:], shifted[:], ACT.Exp).then_inc(exp_ready, 1)
                act.wait_ge(weights_transposed, n + 2)
                act.wait_ge(weighted_ready, n * NBATCH + 2 * NBATCH)
                act.wait_ge(den_ready, n * NBATCH + 1)
                nc.scalar.activation(weights[:].rearrange("p (k i) h -> p k i h", i=PT),
                                     P_misc[:, 0:W].rearrange("p (i k h) -> p k i h", i=PT, k=PARTS), ACT.Copy).then_inc(weights_ready, 1)

            def sums_of(m, p, b, state=None):
                B = m * NBATCH + b
                act.wait_ge(weights_ready, m + 2)
                act.wait_ge(sums_ready, B * BATCH + (2 * SC - BATCH))
                nc.scalar.activation(weighted[:, b % 2, :, :, HEAD_V], weights[:, b * BATCH:(b + 1) * BATCH, :], ACT.Copy).then_inc(den_ready, 1)

            act.wait_ge(weights_in, 64)
            groups(act, score_of, maxima_of, sums_of)

        @block.vector
        def _(dve):
            dve.sem_inc(product_ready, 1)
            dve.sem_inc(score_ready, NBATCH + 1)
            dve.sem_inc(shifted_ready, 1)
            dve.sem_inc(weighted_ready, 2 * NBATCH)
            dve.sem_inc(rescaled, 1)
            dve.sem_inc(added, 2)
            dve.sem_inc(den_ready, 1)
            dve.wait_ge(cleared, 7)

            def score_of(n, p, b, state=None):
                B = n * NBATCH + b
                tiles = slice(b * BATCH, (b + 1) * BATCH)
                dve.wait_ge(records_in[p], (n - p) * 8 + 16)
                dve.wait_ge(sums_ready, B * BATCH + BATCH)
                nc.vector.tensor_tensor(onehot[:, p, tiles], iota[:, None, 0:BN].broadcast_to([128, BATCH, BN]),
                                        rec[:, p, tiles, LOW:LOW + 1].broadcast_to([128, BATCH, BN]), ALU.is_equal).then_inc(onehot_ready, 1)
                if state is not None:
                    weigh(n - 1, 1 - p, b)
                dve.wait_ge(kv_in[p * NBATCH + b], (n - p) * 32 + 64)
                dve.wait_ge(qk_ready, B + 2)
                nc.vector.tensor_tensor(keys[:].rearrange("p (t d) -> p t d", d=QK), kv[:, p, tiles, 0:QK],
                                        P_k[:].rearrange("p (t d) -> p t d", d=QK), ALU.add).then_inc(keys_ready, 1)
                dve.wait_ge(keys_ready, B + 1)
                nc.vector.tensor_tensor(product[:], keys[:], P_q[:], ALU.mult).then_inc(product_ready, 1)
                dve.wait_ge(product_ready, B + 2)
                dve.wait_ge(rows_transposed, n + 1)
                k0 = b * BATCH // PT
                nc.vector.tensor_reduce(score[:, :, k0:k0 + BATCH // PT, :].rearrange("p i k h -> p k i h"),
                                        product[:].rearrange("p (k i h d) -> p k i h d", i=PT, h=HEADS, d=HEAD_QK), AX.X, ALU.add).then_inc(score_ready, 1)

            def maxima_of(n, p):
                at = n * MAX_STEPS
                done = [0]

                def step(ins):
                    ins.then_inc(max_step, 1)
                    done[0] += 1
                    return done[0]

                def after(k):
                    dve.wait_ge(max_step, at + k)

                scores, sources = cs[:, 0:W], cs[:, W:2 * W]
                dve.wait_ge(rows_ready, n + 2)
                k = step(nc.vector.tensor_tensor(changes[:, 1:W], sources[:, 1:W], sources[:, 0:W - 1], ALU.not_equal))
                after(k)
                k = step(nc.vector.tensor_scalar(changes[:, 1:W], changes[:, 1:W], -BIG, None, ALU.mult))
                after(k)
                k = step(nc.vector.tensor_tensor_scan(run[:, 0], changes[:, 0:W], scores, -BIG, ALU.add, ALU.max))
                after(k)
                k = step(nc.vector.tensor_tensor_scan(run[:, 1, ::-1], changes[:, W:0:-1], run[:, 0, ::-1], -BIG, ALU.add, ALU.max))
                assert k == 4
                first_src, last_src = edges[:, 0, 1, :, 0:PARTS], edges[:, 1, 1, :, :]
                dve.wait_ge(ends_ready, n + 1)
                k = step(nc.vector.tensor_tensor(gap[:, :, 0:PARTS], first_src, last_src[:, :, 0:PARTS], ALU.not_equal))
                step(nc.vector.tensor_tensor(split[:, :, 0:PARTS], first_src, last_src[:, :, 1:PARTS + 1], ALU.not_equal))
                after(k)
                k = step(nc.vector.tensor_scalar(gap[:, :, 0:PARTS], gap[:, :, 0:PARTS], -BIG, None, ALU.mult))
                after(k)
                step(nc.vector.scalar_tensor_tensor(pen_f[:, :, 1:PARTS + 1], split[:, :, 0:PARTS], -BIG, gap[:, :, 0:PARTS], ALU.mult, ALU.min))
                k = step(nc.vector.scalar_tensor_tensor(pen_b[:, :, 0:PARTS], split[:, :, 0:PARTS], -BIG, gap[:, :, 1:PARTS + 1], ALU.mult, ALU.min))
                after(k)

                def flat(a):
                    return a.rearrange("a h k -> a (h k)")

                step(nc.vector.tensor_tensor_scan(flat(chain_f[:]), flat(pen_f[:]), flat(edges[:, 1, 0]), -BIG, ALU.add, ALU.max))
                k = step(nc.vector.tensor_tensor_scan(flat(chain_b[:])[:, ::-1], flat(pen_b[:])[:, ::-1], flat(edges[:, 0, 0])[:, ::-1], -BIG, ALU.add, ALU.max))
                after(k)
                step(nc.vector.tensor_tensor(carry_rows[:, 0].rearrange("a k h -> a h k"), chain_f[:, :, 0:PARTS], gap[:, :, 0:PARTS], ALU.add))
                k = step(nc.vector.tensor_tensor(carry_rows[:, 1].rearrange("a k h -> a h k"), chain_b[:, :, 1:PARTS + 1], gap[:, :, 1:PARTS + 1], ALU.add))
                assert k == 13
                step(nc.vector.tensor_copy(edges[:, 1, 0, :, 0], chain_f[:, :, PARTS]))
                step(nc.vector.tensor_copy(edges[:, 1, 1, :, 0], edges[:, 1, 1, :, PARTS]))
                dve.wait_ge(carry_transposed, n + 1)
                k = step(nc.vector.tensor_copy(carry[:], P_misc[:, W:W + 2]))
                after(k)
                k = step(nc.vector.tensor_tensor_scan(run[:, 2], changes[:, 0:W], scores, carry[:, 0:1], ALU.add, ALU.max))
                after(k)
                k = step(nc.vector.tensor_tensor_scan(run[:, 3, ::-1], changes[:, W:0:-1], run[:, 2, ::-1], carry[:, 1:2], ALU.add, ALU.max))
                after(k)
                dve.wait_ge(exp_ready, n + 1)
                nc.vector.tensor_tensor(shifted[:, 0:W], scores, run[:, 3], ALU.subtract)
                nc.vector.tensor_tensor(shifted[0:HEADS, W:W + 1], carry[0:HEADS, 0:1], run[0:HEADS, 3, 0:1], ALU.subtract).then_inc(shifted_ready, 1)
                dve.wait_ge(exp_ready, n + 2)
                k = step(nc.vector.scalar_tensor_tensor(factor[:], ident[0:HEADS, 0:HEADS], weight_rows[0:HEADS, W:W + 1], ident[0:HEADS, 0:HEADS], ALU.mult, ALU.subtract))
                assert k == MAX_STEPS
                dve.wait_ge(factor_spread, n + 1)
                dve.wait_ge(node_rows_ready, n * NBATCH + 2)
                nc.vector.tensor_scalar(rescale[:], P_rows[0:BN, 0:HEADS], first_node[:], 1.0, ALU.mult, ALU.add).then_inc(rescaled, 1)
                g = buckets(DVE_ENGINE, n, 1)[0]
                a = acc[:, bass.ds(g, 1), :].rearrange("p a (h d) -> p (a h) d", d=VD)
                dve.wait_ge(rescaled, n * 1 + 2)
                dve.wait_ge(added, n * SC + 2)
                nc.vector.tensor_tensor(a, a, rescale[:].unsqueeze(2).broadcast_to([BN, HEADS, VD]), ALU.mult).then_inc(acc_rescaled, 1)

            def weigh(m, p, b):
                B = m * NBATCH + b
                tiles = slice(b * BATCH, (b + 1) * BATCH)
                dve.wait_ge(weights_ready, m + 2)
                dve.wait_ge(sums_ready, B * BATCH + (2 * SC - BATCH))
                nc.vector.tensor_tensor(weighted[:, b % 2, :, :, 0:HEAD_V],
                                        kv[:, p, tiles, QK:KV].rearrange("p t (h d) -> p t h d", d=HEAD_V),
                                        weights[:, tiles, :].unsqueeze(3).broadcast_to([128, BATCH, HEADS, HEAD_V]), ALU.mult).then_inc(weighted_ready, 1)

            def sums_of(m, p, b, state=None):
                if isinstance(m, int) and m == NSC - 1:
                    weigh(m, p, b)
                if b == 0:
                    state["g"] = buckets(DVE_ENGINE, m, SC)
                    dve.wait_ge(acc_rescaled, m + 1)
                for k in range(BATCH):
                    t = b * BATCH + k
                    a = acc[:, bass.ds(state["g"][t], 1), :].rearrange("p a d -> p (a d)")
                    dve.wait_ge(added, m * SC + (t + 2))
                    dve.wait_ge(sums_ready, m * SC + (2 * SC + t + 1))
                    nc.vector.tensor_tensor(a, a, P_z[t % 2][0:BN, 0:ACCW], ALU.add).then_inc(added, 1)

            groups(dve, score_of, maxima_of, sums_of)

        @block.tensor
        def _(pe):
            pe.sem_inc(qk_ready, 1)
            pe.sem_inc(rows_transposed, 1)
            pe.sem_inc(weights_transposed, 1)
            pe.sem_inc(exp_ready, 1)
            pe.sem_inc(sums_ready, 2 * SC)
            pe.wait_ge(weights_in, 64)

            def score_of(n, p, b, state=None):
                B = n * NBATCH + b
                if b == 0:
                    first_g[0] = buckets(PE_ENGINE, n, SC)
                pe.wait_ge(records_in[p], (n - p) * 8 + 16)
                pe.wait_ge(attr_rows_ready, B + 1)
                for k in range(BATCH):
                    last = nc.tensor.transpose(P_attr[0:K, k * 128:(k + 1) * 128], rec[:, p, b * BATCH + k, 0:K], ident[:])
                last.then_inc(attr_transposed, 1)
                pe.wait_ge(onehot_ready, B + 1)
                pe.wait_ge(node_rows_ready, B + 1)
                for k in range(BATCH):
                    last = nc.tensor.transpose(P_node[0:BN, k * 128:(k + 1) * 128], onehot[:, p, b * BATCH + k], ident[:])
                last.then_inc(node_transposed, 1)
                if state is not None:
                    sum_up(n - 1, 1 - p, b, 0)
                pe.wait_ge(attr_rows_ready, B + 2)
                pe.wait_ge(node_rows_ready, B + 2)
                pe.wait_ge(product_ready, B + 1)
                for k in range(BATCH):
                    cols = slice(k * 128, (k + 1) * 128)
                    q = c["q"][:, bass.ds(first_g[0][b * BATCH + k], 1), :].rearrange("p a d -> p (a d)")
                    nc.tensor.matmul(P_k[:, cols], attr_rows[:, cols], wrpe[:, 1, :], start=True, stop=True)
                    nc.tensor.matmul(P_q[:, cols], attr_rows[:, cols], wrpe[:, 0, :], start=True, stop=False)
                    last = nc.tensor.matmul(P_q[:, cols], node_rows[:, cols], q, start=False, stop=True)
                last.then_inc(qk_ready, 1)
                if state is not None:
                    sum_up(n - 1, 1 - p, b, 1)

            def maxima_of(n, p):
                at = n * MAX_STEPS
                pe.wait_ge(score_ready, n * NBATCH + (2 * NBATCH + 1))
                pe.wait_ge(src_wide_ready, n + 3)
                pe.wait_ge(rows_ready, n + 1)
                pe.wait_ge(rescaled, n + 1)
                for i in range(PT):
                    nc.tensor.transpose(P_rows[:, i * 128:(i + 1) * 128], score[:, i].rearrange("p k h -> p (k h)"), ident[:])
                for i in range(PT):
                    last = nc.tensor.transpose(P_rows[:, W + i * 128:W + (i + 1) * 128], src_wide[:, i].rearrange("p k h -> p (k h)"), ident[:])
                last.then_inc(rows_transposed, 1)
                pe.wait_ge(max_step, at + 4)
                pe.wait_ge(weights_ready, n + 1)
                for j, col in enumerate((run[:, 1, 0:1], cs[:, W:W + 1], run[:, 1, W - 1:W], cs[:, 2 * W - 1:2 * W])):
                    last = nc.tensor.transpose(P_misc[0:1, j * 128:(j + 1) * 128], col, ident[:])
                last.then_inc(ends_transposed, 1)
                pe.wait_ge(max_step, at + 13)
                pe.sem_inc(carry_seen, 1)
                for j in range(2):
                    last = nc.tensor.transpose(P_misc[:, W + j:W + j + 1], carry_rows[:, j].rearrange("a k h -> a (k h)"), ident[0:1, 0:1])
                last.then_inc(carry_transposed, 1)
                pe.wait_ge(exp_ready, n + 2)
                for i in range(PT):
                    last = nc.tensor.transpose(P_misc[:, i * 128:(i + 1) * 128], weight_rows[:, i * 128:(i + 1) * 128], ident[:])
                last.then_inc(weights_transposed, 1)
                pe.wait_ge(max_step, at + MAX_STEPS)
                nc.tensor.matmul(P_rows[0:BN, 0:HEADS], ones[0:HEADS, 0:BN], factor[:], start=True, stop=True).then_inc(factor_spread, 1)

            first_g = [None]

            def sum_up(m, p, b, half):
                B = m * NBATCH + b
                pe.wait_ge(weighted_ready, B + (2 * NBATCH + 1))
                pe.wait_ge(den_ready, B + 2)
                for k in range(2 * half, 2 * half + 2):
                    t = b * BATCH + k
                    pe.wait_ge(added, m * SC + (t + 1))
                    nc.tensor.matmul(P_z[t % 2][0:BN, 0:ACCW], onehot[:, p, t], weighted[:, b % 2, k].rearrange("p h d -> p (h d)"),
                                     start=True, stop=True).then_inc(sums_ready, 1)

            def sums_of(m, p, b, state=None):
                if isinstance(m, int) and m == NSC - 1:
                    sum_up(m, p, b, 0)
                    sum_up(m, p, b, 1)

            groups(pe, score_of, maxima_of, sums_of)


def feed_forward(nc, c, wr, br, w1, b1, w2, b2, route_dram, out):
    GB = 5
    GN = GB * BN
    NG = NB // GB
    FC = HIDDEN // 128
    SPLIT = [(0, 320), (320, GN - 320)]
    with ExitStack() as ctx:
        def sb(name, shape, dt=F32):
            return ctx.enter_context(nc.sbuf_tensor(name, shape, dt))

        def ps(name):
            return ctx.enter_context(nc.psum_tensor(name, [128, 512], F32))

        def sem(name):
            return ctx.enter_context(nc.semaphore(name))

        x, acc, ident, ones, below = c["x"], c["acc"], c["ident"], c["ones"], c["below"]
        y = acc
        compared = c["q"][:].rearrange("p b d -> p (b d)")
        w1_sb = sb("w1_sb", [128, 2, HIDDEN])
        w2_sb = sb("w2_sb", [128, FC, DIM])
        b1_sb = sb("b1_sb", [128, FC])
        b2_sb = sb("b2_sb", [1, DIM])
        wr_sb = sb("wr_sb", [BN, DIM])
        br_sb = sb("br_sb", [BN, 1])
        inverse = sb("inverse", [BN, NB, HEADS])
        stats = sb("ff_stats", [BN, GB, 6])
        mean_var = sb("ff_mean_var", [BN, GB, 2])
        spread = sb("ff_spread", [BN, 3, GB])
        normed = sb("ff_normed", [BN, NB, DIM])
        normed_t = sb("ff_normed_t", [128, 2, NODES])
        hidden = sb("hidden", [128, FC, GN])
        stage = sb("stage", [BN, GB, DIM])
        routed = sb("routed", [BN, GB, DIM])
        route5 = sb("route5", [BN, GB])
        route = sb("route", [BN, NB])
        route_t = sb("route_t", [NB, BN])
        route_row = sb("route_row", [BN, NODES])
        counts = sb("counts", [BN, NB, 3])
        rank = sb("ff_rank", [BN, NB])
        gain = sb("gain", [BN, NB])
        P_h = [[ps(f"ps_h{i}{j}") for j in range(2)] for i in range(2)]
        P_y = [ps(f"ps_y{i}") for i in range(2)]
        P_t = [ps(f"ps_t{i}") for i in range(2)]

        loaded = sem("loaded")
        inverse_step = sem("inverse_step")
        att_step = sem("att_step")
        stats_seen = sem("stats_seen")
        root_ready = sem("ff_root_ready")
        inv_root = sem("inv_root")
        normed_ready = sem("ff_normed_ready")
        routed_ready = sem("routed_ready")
        residual_ready = sem("residual_ready")
        transposed = sem("ff_transposed")
        normed_t_ready = sem("normed_t_ready")
        up_ready = sem("up_ready")
        hidden_ready = sem("hidden_ready")
        down_ready = sem("down_ready")
        y_ready = sem("y_ready")
        route_transposed = sem("route_transposed")
        route_t_ready = sem("route_t_ready")
        route_out = sem("route_out")
        route_in = sem("route_in")
        rank_step = sem("rank_step")
        result_ready = sem("result_ready")
        stored = sem("stored")
        staged = sem("staged")
        block = ctx.enter_context(nc.Block())

        @block.sync
        def _(sp):
            sp.dma_start(wr_sb[:], wr.rearrange("d a -> a d").broadcast_to([BN, DIM])).then_inc(loaded, 16)
            sp.dma_start(br_sb[:], br.rearrange("(a n) -> a n", a=1).broadcast_to([BN, 1])).then_inc(loaded, 16)
            sp.dma_start(w1_sb[:], w1.rearrange("(k p) n -> p k n", p=128)).then_inc(loaded, 16)
            with nc.allow_non_contiguous_dma(reason="1024 biases, once"):
                sp.dma_start(b1_sb[:], b1.rearrange("(f p) -> p f", p=128)).then_inc(loaded, 16)
            sp.dma_start(w2_sb[:], w2.rearrange("(f p) n -> p f n", p=128)).then_inc(loaded, 16)
            sp.dma_start(b2_sb[:], b2.rearrange("(a n) -> a n", a=1)).then_inc(loaded, 16)
            sp.wait_ge(route_t_ready, 1)
            sp.dma_start(route_dram.rearrange("(b p) -> b p", p=BN), route_t[:]).then_inc(route_out, 16)
            sp.wait_ge(route_out, 16)
            sp.dma_start(route_row[:], route_dram.rearrange("(a n) -> a n", a=1).broadcast_to([BN, NODES])).then_inc(route_in, 16)
            out_v = out.rearrange("(b p) d -> p b d", p=BN)
            for g in range(NG):
                sp.wait_ge(result_ready, GB * (g + 1))
                sp.dma_start(out_v[:, g * GB:(g + 1) * GB, :], x[:, g * GB:(g + 1) * GB, :]).then_inc(stored, 16)
            sp.wait_ge(stored, 16 * NG)

        @block.scalar
        def _(act):
            act.sem_inc(normed_t_ready, 1)
            act.sem_inc(hidden_ready, 4)
            act.sem_inc(y_ready, 2)

            with act.Fori(0, NG) as g:
                act.wait_ge(att_step, g * 5 + 5)
                nc.scalar.activation(spread[:, 1, :], spread[:, 0, :], ACT.Sqrt).then_inc(root_ready, 1)
            act.wait_ge(route_transposed, 1)
            nc.scalar.activation(route_t[:], P_t[0][0:NB, 0:BN], ACT.Copy).then_inc(route_t_ready, 1)
            act.wait_ge(loaded, 96)
            with act.Fori(0, NG) as g:
                act.wait_ge(transposed, g * 2 + 1)
                nc.scalar.activation(stage[:], normed[:, bass.ds(g * GB, GB), :], ACT.Copy).then_inc(staged, 1)
                for k in range(2):
                    act.wait_ge(transposed, g * 2 + (k + 2))
                    nc.scalar.activation(normed_t[:, k, bass.ds(g * GN, 4 * BN)], P_t[0][:, 0:4 * BN], ACT.Copy)
                    nc.scalar.activation(normed_t[:, k, bass.ds(g * GN + 4 * BN, BN)], P_t[1][:, 0:BN], ACT.Copy).then_inc(normed_t_ready, 1)
                act.wait_ge(down_ready, g * GB + 1)
                for f in range(FC):
                    for j, (at, n) in enumerate(SPLIT):
                        act.wait_ge(up_ready, g * (2 * FC) + (2 * f + j + 1))
                        nc.scalar.activation(hidden[:, f, at:at + n], P_h[f % 2][j][:, 0:n], ACT.Gelu_apprx_tanh,
                                             bias=b1_sb[:, f:f + 1]).then_inc(hidden_ready, 1)
                for b in range(GB):
                    act.wait_ge(down_ready, g * GB + (b + 2))
                    nc.scalar.activation(y[:, bass.ds(g * GB + b, 1), 0:DIM].rearrange("p a d -> p (a d)"), P_y[b % 2][0:BN, 0:DIM], ACT.Copy).then_inc(y_ready, 1)

        @block.vector
        def _(dve):
            nc.vector.tensor_scalar(inverse[:], acc[:].rearrange("p b (h d) -> p b h d", d=VD)[:, :, :, HEAD_V], EPS_DEN, None, ALU.add).then_inc(inverse_step, 1)
            dve.wait_ge(inverse_step, 1)
            nc.vector.reciprocal(inverse[:], inverse[:]).then_inc(inverse_step, 1)
            dve.wait_ge(inverse_step, 2)
            dve.wait_ge(loaded, 96)
            with dve.Fori(0, NG) as g:
                five = bass.ds(g * GB, GB)
                sums = acc[:, five, :].rearrange("p b (h d) -> p (b h) d", d=VD)[:, :, 0:HEAD_V]
                nc.vector.tensor_tensor(sums, sums, inverse[:, five, :].rearrange("p b h -> p (b h)").unsqueeze(2).broadcast_to([BN, GB * HEADS, HEAD_V]), ALU.mult).then_inc(att_step, 1)
                dve.wait_ge(att_step, g * 5 + 1)
                nc.vector.tensor_tensor(x[:, five, :].rearrange("p b (h d) -> p (b h) d", d=HEAD_V), x[:, five, :].rearrange("p b (h d) -> p (b h) d", d=HEAD_V), sums, ALU.add).then_inc(att_step, 1)
                dve.wait_ge(att_step, g * 5 + 2)
                dve.sem_inc(stats_seen, 1)
                for b in range(GB):
                    last = nc.vector.bn_stats(stats[:, b], x[:, bass.ds(g * GB + b, 1), :].rearrange("p a d -> p (a d)"))
                last.then_inc(att_step, 1)
                dve.wait_ge(att_step, g * 5 + 3)
                dve.sem_inc(stats_seen, 1)
                for b in range(GB):
                    last = nc.vector.bn_aggr(mean_var[:, b], stats[:, b])
                last.then_inc(att_step, 1)
                dve.wait_ge(att_step, g * 5 + 4)
                nc.vector.tensor_scalar(spread[:, 0, :], mean_var[:, :, 1], EPS_LN, None, ALU.add).then_inc(att_step, 1)
                dve.wait_ge(root_ready, g + 1)
                nc.vector.reciprocal(spread[:, 2, :], spread[:, 1, :]).then_inc(inv_root, 1)
                dve.wait_ge(inv_root, g + 1)
                for b in range(GB):
                    last = nc.vector.tensor_scalar(normed[:, bass.ds(g * GB + b, 1), :].rearrange("p a d -> p (a d)"),
                                                   x[:, bass.ds(g * GB + b, 1), :].rearrange("p a d -> p (a d)"),
                                                   mean_var[:, b, 0:1], spread[:, 2, b:b + 1], ALU.subtract, ALU.mult)
                last.then_inc(normed_ready, 1)
                dve.wait_ge(normed_ready, g + 1)
                for b in range(GB):
                    last = nc.vector.scalar_tensor_tensor(routed[:, b], normed[:, bass.ds(g * GB + b, 1), :].rearrange("p a d -> p (a d)"), 1.0,
                                                          wr_sb[:], ALU.mult, ALU.mult, accum_out=route5[:, b:b + 1])
                last.then_inc(routed_ready, 1)
                nc.vector.tensor_tensor(x[:, five, :], x[:, five, :], normed[:, five, :], ALU.add).then_inc(residual_ready, 1)
                dve.wait_ge(routed_ready, g + 1)
                nc.vector.tensor_scalar(route[:, five], route5[:], br_sb[:], None, ALU.add).then_inc(inverse_step, 1)
            dve.wait_ge(route_in, 16)
            for b in range(NB):
                w = route[:, b:b + 1]
                at = b * BN
                if b:
                    dve.wait_ge(rank_step, 3 * b)
                    nc.vector.tensor_scalar(compared[:, 0:at], route_row[:, 0:at], w, 0.0, ALU.is_ge, ALU.add, accum_out=counts[:, b, 0:1]).then_inc(rank_step, 1)
                else:
                    nc.vector.memset(counts[:, 0, 0:1], 0.0).then_inc(rank_step, 1)
                nc.vector.tensor_scalar(compared[:, at:NODES], route_row[:, at:NODES], w, 0.0, ALU.is_gt, ALU.add, accum_out=counts[:, b, 1:2]).then_inc(rank_step, 1)
                nc.vector.scalar_tensor_tensor(routed[:, b % GB, 0:BN], route_row[:, at:at + BN], w, below[0:BN, 0:BN], ALU.is_equal, ALU.mult,
                                               accum_out=counts[:, b, 2:3]).then_inc(rank_step, 1)
            dve.wait_ge(rank_step, 3 * NB)
            nc.vector.tensor_reduce(rank[:], counts[:], AX.X, ALU.add).then_inc(rank_step, 1)
            dve.wait_ge(rank_step, 3 * NB + 1)
            nc.vector.scalar_tensor_tensor(gain[:], rank[:], float(KEPT), route[:], ALU.is_lt, ALU.mult).then_inc(rank_step, 1)
            dve.wait_ge(rank_step, 3 * NB + 2)
            for b in range(NB):
                dve.wait_ge(y_ready, b + 3)
                nc.vector.scalar_tensor_tensor(x[:, b, :], y[:, b, 0:DIM], gain[:, b:b + 1], x[:, b, :], ALU.mult, ALU.add).then_inc(result_ready, 1)

        @block.tensor
        def _(pe):
            pe.sem_inc(down_ready, 1)
            pe.sem_inc(transposed, 1)
            pe.wait_ge(inverse_step, 2 + NG)
            nc.tensor.transpose(P_t[0][0:NB, 0:BN], route[:], ident[0:BN, 0:BN]).then_inc(route_transposed, 1)
            pe.wait_ge(route_t_ready, 1)
            pe.wait_ge(loaded, 96)
            with pe.Fori(0, NG) as g:
                pe.wait_ge(staged, g + 1)
                for k in range(2):
                    pe.wait_ge(normed_t_ready, g * 2 + (k + 1))
                    for b in range(GB):
                        last = nc.tensor.transpose(P_t[b // 4][:, (b % 4) * BN:(b % 4 + 1) * BN],
                                                   stage[:, b, k * 128:(k + 1) * 128], ident[0:BN, 0:BN])
                    last.then_inc(transposed, 1)
                pe.wait_ge(normed_t_ready, g * 2 + 3)
                for f in range(FC):
                    for j, (at, n) in enumerate(SPLIT):
                        pe.wait_ge(hidden_ready, g * (2 * FC) + (2 * f + j + 1))
                        for k in range(2):
                            last = nc.tensor.matmul(P_h[f % 2][j][:, 0:n], w1_sb[:, k, f * 128:(f + 1) * 128],
                                                    normed_t[:, k, bass.ds(g * GN + at, n)], start=(k == 0), stop=(k == 1))
                        last.then_inc(up_ready, 1)
                pe.wait_ge(hidden_ready, g * (2 * FC) + (2 * FC + 4))
                for b in range(GB):
                    pe.wait_ge(y_ready, g * GB + (b + 1))
                    for f in range(FC):
                        nc.tensor.matmul(P_y[b % 2][0:BN, 0:DIM], hidden[:, f, b * BN:(b + 1) * BN], w2_sb[:, f, :], start=(f == 0), stop=False)
                    nc.tensor.matmul(P_y[b % 2][0:BN, 0:DIM], ones[0:1, 0:BN], b2_sb[:], start=False, stop=True).then_inc(down_ready, 1)


_INS = ["x", "src", "dst", "edge_attr_18", "L0_gnn_Wqkv", "L0_gnn_bqkv", "L0_gnn_Wk_rpe", "L0_gnn_bk_rpe", "L0_gnn_Wq_rpe", "L0_gnn_bq_rpe",
        "L0_ffn_attention_mask", "L0_ffn_wr", "L0_ffn_br", "L0_ffn_w1", "L0_ffn_b1", "L0_ffn_w2", "L0_ffn_b2"]
_OUTS = [((NODES, DIM), "float32")]


def kernel(**inputs):
    import numpy as _np
    import concourse.bacc as _bacc
    from concourse import mybir as _mybir
    from concourse.bass_utils import run_bass_kernel_spmd as _run

    nc = _bacc.Bacc("TRN2", target_bir_lowering=False, num_devices=1)
    arrays, args = {}, []
    for name in _INS:
        a = _np.ascontiguousarray(inputs[name])
        arrays[f"in_{name}_dram"] = a
        args.append(nc.dram_tensor(f"in_{name}_dram", a.shape, _mybir.dt.from_np(a.dtype), kind="ExternalInput").ap())
    for i, (shape, dtype) in enumerate(_OUTS):
        dt = _mybir.dt.from_np(_np.dtype(dtype))
        args.append(nc.dram_tensor(f"out_{i}_dram", shape, dt, kind="ExternalOutput").ap())
    gnn_ffn_kernel(nc, *args)
    r = _run(nc, [arrays], core_ids=[0])
    return r.results[0]["out_0_dram"]
```

```python
from contextlib import ExitStack

import concourse.bass as bass
from concourse import mybir

F32 = mybir.dt.float32
BF16 = mybir.dt.bfloat16
I32 = mybir.dt.int32
ALU = mybir.AluOpType
ACT = mybir.ActivationFunctionType
AX = mybir.AxisListType
PE_ENGINE = mybir.EngineType.PE
DVE_ENGINE = mybir.EngineType.DVE

NODES, DIM, EDGES, ATTRS = 3125, 256, 50000, 18
HEADS, QK = 16, 128
HEAD_QK = QK // HEADS
HEAD_V = DIM // HEADS
QKV = 2 * QK + DIM
KV = QK + DIM
HIDDEN = 1024
KEPT = NODES // 2 - 1
SCALE = HEAD_QK**-0.5
EPS_LN, EPS_DEN = 1e-5, 1e-16
BIG = 1e30

BN = 125
NB = NODES // BN
EP, EC = 125, EDGES // 125
HALF = 8
STEPS = EC // (2 * HALF)
TILE = 128
SC = 16
NSC = -(-(EDGES // TILE + NB) // SC)
NT = NSC * SC
PARTS = 8
PT = SC // PARTS
BATCH = 4
NBATCH = SC // BATCH
ONE, SRC, LOW, DST, WIDE = ATTRS, ATTRS + 1, ATTRS + 2, ATTRS + 3, ATTRS + 4
VD = HEAD_V + 1
ACCW = HEADS * VD
GCOL = NT // 4

assert NB * BN == NODES and STEPS * 2 * HALF == EC and STEPS == NB and NT == 4 * GCOL
assert PARTS * HEADS == 128


def gnn_ffn_kernel(nc, x, src, dst, attrs, Wqkv, bqkv, Wk, bk, Wq, bq, mask, wr, br, w1, b1, w2, b2, out):
    records = nc.dram_tensor("edge_records", [NT * TILE, WIDE], F32, kind="Internal").ap()
    kv_rows = nc.dram_tensor("kv_rows", [NODES, KV], F32, kind="Internal").ap()
    route_dram = nc.dram_tensor("route_dram", [NODES], F32, kind="Internal").ap()

    with ExitStack() as keep:
        def lasting(name, shape, dt=F32):
            return keep.enter_context(nc.sbuf_tensor(name, shape, dt))

        c = {
            "x": lasting("x_sb", [BN, NB, DIM]),
            "q": lasting("q_sb", [BN, NB, QK]),
            "bucket_of_tile": lasting("bucket_of_tile", [1, NT], I32),
            "ident": lasting("ident", [128, 128]),
            "iota": lasting("iota_row", [128, 128]),
            "below": lasting("below", [128, 128]),
            "above": lasting("above", [128, 128]),
            "ones": lasting("ones", [128, 128]),
        }
        order_edges(nc, c, x, src, dst, attrs, Wqkv, bqkv, records, kv_rows)
        c["acc"] = lasting("acc", [BN, NB, ACCW])
        attend(nc, c, records, kv_rows, Wk, bk, Wq, bq)
        feed_forward(nc, c, wr, br, w1, b1, w2, b2, route_dram, out)


def order_edges(nc, c, x, src, dst, attrs, Wqkv, bqkv, records, kv_rows):
    with ExitStack() as ctx:
        def sb(name, shape, dt=F32):
            return ctx.enter_context(nc.sbuf_tensor(name, shape, dt))

        def sem(name):
            return ctx.enter_context(nc.semaphore(name))

        src_i = sb("src_i", [EP, EC], I32)
        dst_i = sb("dst_i", [EP, EC], I32)
        src_f = sb("src_f", [EP, EC])
        low_f = sb("low_f", [EP, EC])
        high_f = sb("high_f", [EP, EC])
        fix = sb("fix", [EP, EC])
        high_i = sb("high_i", [EP, EC], I32)
        attr_sb = sb("attr_sb", [EP, EC * ATTRS])
        table = sb("table", [BN, NB, EC + 1])
        total_i = sb("total_i", [BN, NB], I32)
        tiles_i = sb("tiles_i", [BN, NB], I32)
        tiles_f = sb("tiles_f", [BN, NB])
        tile_end = sb("tile_end", [BN, NB])
        tile_start = sb("tile_start", [BN, NB])
        base = sb("base", [BN, NB])
        tile_no_i = sb("tile_no_i", [GCOL, 4], I32)
        tile_no = sb("tile_no", [GCOL, 4])
        passed = sb("passed", [GCOL, 4, NB])
        bucket_col = sb("bucket_col", [GCOL, 4])
        iota_i = sb("iota_i", [128, 128], I32)
        iota_b = sb("iota_b", [128, 128], BF16)
        empty = sb("empty", [128, NT // 16, WIDE])
        bqkv_sb = sb("bqkv_sb", [BN, QKV])
        wqkv_sb = sb("wqkv_sb", [128, 2, QKV])

        ps = [ctx.enter_context(nc.psum_tensor(f"ps_a{i}", [128, 512], F32)) for i in range(8)]

        with ExitStack() as first:
            def sb1(name, shape, dt=F32):
                return first.enter_context(nc.sbuf_tensor(name, shape, dt))

            def sem1(name):
                return first.enter_context(nc.semaphore(name))

            low_hot = sb1("low_hot", [EP, 2, HALF, BN], BF16)
            high_hot = sb1("high_hot", [EP, 2, HALF, NB], BF16)
            edges_in = sem1("edges_in")
            nodes_in = sem1("nodes_in")
            prefilled = sem1("prefilled")
            made = sem1("made")
            digits = sem1("digits")
            hot_ready = sem1("hot_ready")
            counts_ready = sem1("counts_ready")
            table_filled = sem1("table_filled")
            summed = sem1("summed")
            totals_ready = sem1("totals_ready")
            layout_step = sem1("layout_step")
            buckets_ready = sem1("buckets_ready")
            block = first.enter_context(nc.Block())

            @block.sync
            def _(sp):
                sp.dma_start(src_i[:], src.rearrange("(p c) -> p c", c=EC)).then_inc(edges_in, 16)
                sp.dma_start(c["x"][:], x.rearrange("(b p) d -> p b d", p=BN)).then_inc(nodes_in, 16)
                sp.dma_start(dst_i[:], dst.rearrange("(p c) -> p c", c=EC)).then_inc(nodes_in, 16)
                sp.dma_start(attr_sb[:], attrs.rearrange("(p c) a -> p (c a)", c=EC)).then_inc(nodes_in, 16)
                sp.dma_start(wqkv_sb[:], Wqkv.rearrange("(k p) n -> p k n", p=128)).then_inc(nodes_in, 16)
                sp.dma_start(bqkv_sb[:], bqkv.rearrange("(a n) -> a n", a=1).broadcast_to([BN, QKV])).then_inc(nodes_in, 16)
                sp.wait_ge(made, 10)
                records_v = records.rearrange("(p a r) w -> a p (r w)", p=128, a=16)
                for a in range(16):
                    sp.dma_start(records_v[a], empty[:].rearrange("p r w -> p (r w)")).then_inc(prefilled, 16)
                sp.wait_ge(nodes_in, 16 * 5)
                sp.wait_ge(prefilled, 16 * 16)

            @block.gpsimd
            def _(pool):
                nc.gpsimd.iota(iota_i[:], pattern=[[1, 128]], base=0, channel_multiplier=0).then_inc(made, 1)
                nc.gpsimd.iota(tile_no_i[:], pattern=[[GCOL, 4]], base=0, channel_multiplier=1).then_inc(made, 1)
                nc.gpsimd.memset(c["ident"][:], 0.0).then_inc(made, 1)
                nc.gpsimd.memset(c["ones"][:], 1.0).then_inc(made, 1)
                pool.wait_ge(made, 4)
                nc.gpsimd.affine_select(out=c["ident"][:], in_=c["ident"][:], compare_op=ALU.not_equal, fill=1.0,
                                        base=0, pattern=[[-1, 128]], channel_multiplier=1).then_inc(made, 1)
                nc.gpsimd.affine_select(out=c["below"][:], in_=c["ones"][:], compare_op=ALU.is_gt, fill=0.0,
                                        base=0, pattern=[[-1, 128]], channel_multiplier=1).then_inc(made, 1)
                nc.gpsimd.affine_select(out=c["above"][:], in_=c["ones"][:], compare_op=ALU.is_gt, fill=0.0,
                                        base=0, pattern=[[1, 128]], channel_multiplier=-1).then_inc(made, 1)
                nc.gpsimd.memset(empty[:], 0.0).then_inc(made, 1)
                pool.wait_ge(made, 8)
                nc.gpsimd.memset(empty[:, :, SRC], -1.0).then_inc(made, 1)
                nc.gpsimd.memset(empty[:, :, LOW], -1.0).then_inc(made, 1)

            @block.vector
            def _(dve):
                dve.wait_ge(made, 2)
                nc.vector.tensor_copy(c["iota"][:], iota_i[:]).then_inc(digits, 1)
                nc.vector.tensor_copy(iota_b[:], iota_i[:]).then_inc(digits, 1)
                nc.vector.tensor_copy(tile_no[:], tile_no_i[:]).then_inc(digits, 1)
                nc.vector.memset(table[:, :, 0:1], 0.0).then_inc(digits, 1)
                dve.wait_ge(edges_in, 16)
                nc.vector.tensor_copy(src_f[:], src_i[:]).then_inc(digits, 1)
                dve.wait_ge(digits, 5)
                nc.vector.tensor_scalar(high_i[:], src_f[:], 1.0 / BN, None, ALU.mult).then_inc(digits, 1)
                dve.wait_ge(digits, 6)
                nc.vector.tensor_copy(high_f[:], high_i[:]).then_inc(digits, 1)
                dve.wait_ge(digits, 7)
                nc.vector.scalar_tensor_tensor(low_f[:], high_f[:], -float(BN), src_f[:], ALU.mult, ALU.add).then_inc(digits, 1)
                dve.wait_ge(digits, 8)
                nc.vector.tensor_scalar(fix[:], low_f[:], 0.0, None, ALU.is_lt).then_inc(digits, 1)
                dve.wait_ge(digits, 9)
                nc.vector.tensor_tensor(high_f[:], high_f[:], fix[:], ALU.subtract).then_inc(digits, 1)
                nc.vector.scalar_tensor_tensor(low_f[:], fix[:], float(BN), low_f[:], ALU.mult, ALU.add).then_inc(digits, 1)
                dve.wait_ge(digits, 11)
                nc.vector.tensor_scalar(fix[:], low_f[:], float(BN), None, ALU.is_ge).then_inc(digits, 1)
                dve.wait_ge(digits, 12)
                nc.vector.tensor_tensor(high_f[:], high_f[:], fix[:], ALU.add).then_inc(digits, 1)
                nc.vector.scalar_tensor_tensor(low_f[:], fix[:], -float(BN), low_f[:], ALU.mult, ALU.add).then_inc(digits, 1)
                dve.wait_ge(digits, 14)

                with dve.Fori(0, STEPS) as i:
                    for u in range(2):
                        col = bass.ds(i * (2 * HALF) + u * HALF, HALF)
                        dve.wait_ge(counts_ready, i * 2 + (u + 1))
                        nc.vector.tensor_tensor(low_hot[:, u], iota_b[0:EP, None, 0:BN].broadcast_to([EP, HALF, BN]),
                                                low_f[:, col].unsqueeze(2).broadcast_to([EP, HALF, BN]), ALU.is_equal)
                        nc.vector.tensor_tensor(high_hot[:, u], iota_b[0:EP, None, 0:NB].broadcast_to([EP, HALF, NB]),
                                                high_f[:, col].unsqueeze(2).broadcast_to([EP, HALF, NB]), ALU.is_equal).then_inc(hot_ready, 1)

                dve.wait_ge(table_filled, 2 + 2 * STEPS)
                for b in range(NB):
                    nc.vector.tensor_tensor_scan(table[:, b, 1:], table[:, b, 1:], table[:, b, 1:], 0.0, ALU.add, ALU.max).then_inc(summed, 1)

                dve.wait_ge(totals_ready, 2)
                nc.vector.tensor_scalar(total_i[:], ps[0][0:BN, 0:NB], float(TILE - 1), None, ALU.add).then_inc(layout_step, 1)
                dve.wait_ge(layout_step, 1)
                nc.vector.tensor_scalar(tiles_i[:], total_i[:], 7, None, ALU.logical_shift_right).then_inc(layout_step, 1)
                dve.wait_ge(layout_step, 2)
                nc.vector.tensor_copy(tiles_f[:], tiles_i[:]).then_inc(layout_step, 1)
                dve.wait_ge(layout_step, 3)
                nc.vector.tensor_tensor_scan(tile_end[:], tiles_f[:], tiles_f[:], 0.0, ALU.add, ALU.max).then_inc(layout_step, 1)
                dve.wait_ge(layout_step, 4)
                nc.vector.tensor_tensor(tile_start[:], tile_end[:], tiles_f[:], ALU.subtract).then_inc(layout_step, 1)
                nc.vector.tensor_tensor(passed[:], tile_end[0:GCOL, None, :].broadcast_to([GCOL, 4, NB]),
                                        tile_no[:].unsqueeze(2).broadcast_to([GCOL, 4, NB]), ALU.is_le).then_inc(layout_step, 1)
                dve.wait_ge(layout_step, 6)
                nc.vector.scalar_tensor_tensor(base[:], tile_start[:], float(TILE), ps[1][0:BN, 0:NB], ALU.mult, ALU.add).then_inc(layout_step, 1)
                nc.vector.tensor_reduce(bucket_col[:], passed[:], AX.X, ALU.add).then_inc(layout_step, 1)
                dve.wait_ge(layout_step, 8)
                nc.vector.tensor_scalar(bucket_col[:], bucket_col[:], float(NB - 1), None, ALU.min).then_inc(layout_step, 1)
                dve.wait_ge(buckets_ready, 1)
                nc.vector.tensor_copy(c["bucket_of_tile"][:], ps[2][0:1, 0:NT])

            @block.tensor
            def _(pe):
                pe.sem_inc(counts_ready, 2)
                with pe.Fori(0, STEPS) as i:
                    for u in range(2):
                        pe.wait_ge(hot_ready, i * 2 + (u + 1))
                        pe.wait_ge(table_filled, i * 2 + (u + 1))
                        for k in range(HALF):
                            last = nc.tensor.matmul(ps[u][0:BN, k * NB:(k + 1) * NB], low_hot[:, u, k], high_hot[:, u, k], start=True, stop=True)
                        last.then_inc(counts_ready, 1)
                pe.wait_ge(summed, NB)
                pe.wait_ge(made, 7)
                pe.wait_ge(table_filled, 2 + 2 * STEPS)
                nc.tensor.matmul(ps[0][0:BN, 0:NB], c["ones"][0:BN, 0:BN], table[:, :, EC], start=True, stop=True).then_inc(totals_ready, 1)
                nc.tensor.matmul(ps[1][0:BN, 0:NB], c["above"][0:BN, 0:BN], table[:, :, EC], start=True, stop=True).then_inc(totals_ready, 1)
                pe.wait_ge(layout_step, 9)
                for k in range(4):
                    last = nc.tensor.matmul(ps[2][0:1, k * GCOL:(k + 1) * GCOL], bucket_col[:, k:k + 1], c["ident"][0:GCOL, 0:GCOL], start=True, stop=True)
                last.then_inc(buckets_ready, 1)

            @block.scalar
            def _(act):
                act.sem_inc(table_filled, 2)
                with act.Fori(0, STEPS) as i:
                    for u in range(2):
                        act.wait_ge(counts_ready, i * 2 + (u + 3))
                        nc.scalar.activation(table[:, :, bass.ds(i * (2 * HALF) + (u * HALF + 1), HALF)],
                                             ps[u][0:BN, 0:HALF * NB].rearrange("p (k b) -> p b k", b=NB), ACT.Copy).then_inc(table_filled, 1)

        place_edges(nc, c, ps, src_f, low_f, high_f, dst_i, attr_sb, table, base, wqkv_sb, bqkv_sb, records, kv_rows)


def place_edges(nc, c, ps, src_f, low_f, high_f, dst_i, attr_sb, table, base, wqkv_sb, bqkv_sb, records, kv_rows):
    with ExitStack() as ctx:
        def sb(name, shape, dt=F32):
            return ctx.enter_context(nc.sbuf_tensor(name, shape, dt))

        def sem(name):
            return ctx.enter_context(nc.semaphore(name))

        low_hot = sb("low_hot_f", [EP, 2, HALF, BN])
        low_rows = sb("low_rows", [BN, 2, HALF, EP])
        src_diag = sb("src_diag", [EP, 2, HALF, EP])
        high_hot = sb("high_hot_f", [EP, HALF, NB])
        same_before = sb("same_before", [EP, HALF, EP])
        rank = sb("rank", [EP, HALF])
        picked = sb("picked", [EP, HALF, NB])
        offset = sb("offset", [EP, HALF])
        slot = sb("slot", [EP, 2, HALF], I32)
        record = sb("record", [EP, 2, HALF, WIDE])
        stats = sb("stats", [BN, 6])
        mean_var = sb("mean_var", [BN, 2])
        spread = sb("spread", [BN, 3])
        normed = sb("normed", [BN, DIM])
        normed_t = sb("normed_t", [128, 2, BN])
        kv_out = sb("kv_out", [BN, KV])
        bq_scaled = sb("bq_scaled", [BN, QK])

        low_onehot = sem("low_onehot")
        diag_ready = sem("diag_ready")
        low_transposed = sem("low_transposed")
        low_rows_ready = sem("low_rows_ready")
        src_rows_ready = sem("src_rows_ready")
        ranks_ready = sem("ranks_ready")
        high_ready = sem("high_ready")
        looked_up = sem("looked_up")
        picked_ready = sem("picked_ready")
        offset_ready = sem("offset_ready")
        slots_ready = sem("slots_ready")
        records_built = sem("records_built")
        scattered = [sem(f"scattered{u}") for u in range(2)]
        ln_step = sem("ln_step")
        root_ready = sem("root_ready")
        normed_ready = sem("normed_ready")
        node_transposed = sem("node_transposed")
        normed_rows = sem("normed_rows")
        qkv_ready = sem("qkv_ready")
        q_ready = sem("q_ready")
        kv_ready = sem("kv_ready")
        kv_stored = sem("kv_stored")
        bias_ready = sem("bias_ready")
        ones_set = sem("ones_set")
        records_free = sem("records_free")
        kv_out_free = sem("kv_out_free")
        scatters_begun = sem("scatters_begun")
        block = ctx.enter_context(nc.Block())
        T0, S0, L0, X0, W0 = ps[0:2], ps[2:4], ps[4], ps[5], ps[6]

        @block.sync
        def _(sp):
            with sp.Fori(0, STEPS) as i:
                sp.wait_ge(scattered[0], (i + 1) * (16 * HALF))
                sp.sem_inc(records_free, 1)
                sp.wait_ge(kv_ready, i + 1)
                sp.dma_start(kv_rows[bass.ds(i * BN, BN), :], kv_out[:]).then_inc(kv_stored, 16)
                sp.wait_ge(scattered[1], (i + 1) * (16 * HALF))
                sp.sem_inc(records_free, 1)
                sp.wait_ge(kv_stored, (i + 1) * 16)
                sp.sem_inc(kv_out_free, 1)

        @block.gpsimd
        def _(pool):
            nc.gpsimd.memset(record[:, :, :, ONE], 1.0).then_inc(ones_set, 1)
            with pool.Fori(0, STEPS) as i:
                for u in range(2):
                    pool.wait_ge(records_built, i * 2 + (u + 1))
                    pool.wait_ge(slots_ready, i * 2 + (u + 1))
                    pool.sem_inc(scatters_begun, 1)
                    for k in range(HALF):
                        nc.gpsimd.indirect_dma_start(
                            out=records, out_offset=bass.IndirectOffsetOnAxis(ap=slot[:, u, k:k + 1], axis=0),
                            in_=record[:, u, k, :], in_offset=None).then_inc(scattered[u], 16)
            for u in range(2):
                pool.wait_ge(scattered[u], 16 * HALF * STEPS)

        @block.scalar
        def _(act):
            act.sem_inc(low_rows_ready, 1)
            act.wait_ge(ones_set, 1)
            with act.Fori(0, STEPS) as i:
                for u in range(2):
                    j = i * (2 * HALF) + u * HALF
                    act.wait_ge(records_free, i * 2 + (u + 1))
                    act.activation(record[:, u, :, 0:ATTRS], attr_sb[:, bass.ds(j * ATTRS, HALF * ATTRS)].rearrange("p (k a) -> p k a", a=ATTRS), ACT.Copy)
                    act.activation(record[:, u, :, SRC], src_f[:, bass.ds(j, HALF)], ACT.Copy)
                    act.activation(record[:, u, :, LOW], low_f[:, bass.ds(j, HALF)], ACT.Copy)
                    act.activation(record[:, u, :, DST].bitcast(I32), dst_i[:, bass.ds(j, HALF)], ACT.Copy).then_inc(records_built, 1)
                    if u == 0:
                        act.wait_ge(ln_step, (i + 1) * 3)
                        act.activation(spread[:, 1:2], spread[:, 0:1], ACT.Sqrt).then_inc(root_ready, 1)
                    act.wait_ge(low_transposed, i * 2 + (u + 3))
                    act.wait_ge(looked_up, i * 2 + (u + 1))
                    for h in range(2):
                        last = act.activation(low_rows[:, u, h * 4:h * 4 + 4, :].rearrange("p a b -> p (a b)"), T0[h][0:BN, 0:4 * EP], ACT.Copy)
                    last.then_inc(low_rows_ready, 1)
                    if u == 0:
                        act.wait_ge(node_transposed, i + 1)
                        act.activation(normed_t[:].rearrange("p a b -> p (a b)"), X0[:, 0:2 * BN], ACT.Copy).then_inc(normed_rows, 1)

        @block.vector
        def _(dve):
            dve.sem_inc(ranks_ready, 1)
            dve.sem_inc(picked_ready, 1)
            nc.vector.tensor_scalar(bq_scaled[:], bqkv_sb[:, 0:QK], SCALE, None, ALU.mult).then_inc(bias_ready, 1)
            dve.wait_ge(bias_ready, 1)
            with dve.Fori(0, STEPS) as i:
                for u in range(2):
                    col = bass.ds(i * (2 * HALF) + u * HALF, HALF)
                    n = i * 2 + u
                    dve.wait_ge(low_transposed, n + 1)
                    nc.vector.tensor_tensor(low_hot[:, u], c["iota"][0:EP, None, 0:BN].broadcast_to([EP, HALF, BN]),
                                            low_f[:, col].unsqueeze(2).broadcast_to([EP, HALF, BN]), ALU.is_equal).then_inc(low_onehot, 1)
                    dve.wait_ge(src_rows_ready, n + 1)
                    nc.vector.tensor_tensor(src_diag[:, u], c["ident"][0:EP, None, 0:EP].broadcast_to([EP, HALF, EP]),
                                            src_f[:, col].unsqueeze(2).broadcast_to([EP, HALF, EP]), ALU.mult).then_inc(diag_ready, 1)
                    if u == 0:
                        nc.vector.bn_stats(stats[:], c["x"][:, bass.ds(i, 1), :].rearrange("p a d -> p (a d)")).then_inc(ln_step, 1)
                        dve.wait_ge(ln_step, i * 3 + 1)
                    nc.vector.tensor_tensor(high_hot[:], c["iota"][0:EP, None, 0:NB].broadcast_to([EP, HALF, NB]),
                                            high_f[:, col].unsqueeze(2).broadcast_to([EP, HALF, NB]), ALU.is_equal).then_inc(high_ready, 1)
                    if u == 0:
                        nc.vector.bn_aggr(mean_var[:], stats[:]).then_inc(ln_step, 1)
                        dve.wait_ge(ln_step, i * 3 + 2)
                        nc.vector.tensor_scalar(spread[:, 0:1], mean_var[:, 1:2], EPS_LN, None, ALU.add).then_inc(ln_step, 1)
                    dve.wait_ge(src_rows_ready, n + 3)
                    for k in range(HALF):
                        last = nc.vector.scalar_tensor_tensor(
                            same_before[:, k], S0[k // 4][0:EP, (k % 4) * EP:(k % 4 + 1) * EP],
                            src_f[:, bass.ds(i * (2 * HALF) + (u * HALF + k), 1)], c["below"][0:EP, 0:EP],
                            ALU.is_equal, ALU.mult, accum_out=rank[:, k:k + 1])
                    last.then_inc(ranks_ready, 1)
                    if u == 0:
                        dve.wait_ge(root_ready, i + 1)
                        nc.vector.reciprocal(spread[:, 2:3], spread[:, 1:2]).then_inc(bias_ready, 1)
                        dve.wait_ge(bias_ready, i + 2)
                        nc.vector.tensor_scalar(normed[:], c["x"][:, bass.ds(i, 1), :].rearrange("p a d -> p (a d)"),
                                                mean_var[:, 0:1], spread[:, 2:3], ALU.subtract, ALU.mult).then_inc(normed_ready, 1)
                    dve.wait_ge(looked_up, n + 3)
                    dve.wait_ge(high_ready, n + 1)
                    nc.vector.tensor_tensor(picked[:], L0[0:EP, 0:HALF * NB].rearrange("p (k b) -> p k b", b=NB), high_hot[:], ALU.mult).then_inc(picked_ready, 1)
                    dve.wait_ge(picked_ready, n + 2)
                    nc.vector.tensor_reduce(offset[:], picked[:], AX.X, ALU.add).then_inc(offset_ready, 1)
                    dve.wait_ge(offset_ready, n + 1)
                    dve.wait_ge(ranks_ready, n + 2)
                    dve.wait_ge(records_free, n + 1)
                    nc.vector.tensor_tensor(slot[:, u], offset[:], rank[:], ALU.add).then_inc(slots_ready, 1)
                    if u == 1:
                        dve.wait_ge(qkv_ready, i + 1)
                        nc.vector.scalar_tensor_tensor(c["q"][:, bass.ds(i, 1), :].rearrange("p a d -> p (a d)"), W0[0:BN, 0:QK], SCALE,
                                                       bq_scaled[:], ALU.mult, ALU.add)
                        dve.wait_ge(kv_out_free, i + 1)
                        nc.vector.tensor_tensor(kv_out[:], W0[0:BN, QK:QKV], bqkv_sb[:, QK:QKV], ALU.add).then_inc(kv_ready, 1)

        @block.tensor
        def _(pe):
            pe.sem_inc(low_transposed, 2)
            pe.sem_inc(src_rows_ready, 2)
            pe.sem_inc(looked_up, 2)
            pe.sem_inc(records_free, 2)
            pe.sem_inc(kv_out_free, 1)
            with pe.Fori(0, STEPS) as i:
                for u in range(2):
                    n = i * 2 + u
                    pe.wait_ge(low_onehot, n + 1)
                    pe.wait_ge(low_rows_ready, n + 1)
                    for k in range(HALF):
                        last = nc.tensor.transpose(T0[k // 4][0:BN, (k % 4) * EP:(k % 4 + 1) * EP], low_hot[:, u, k], c["ident"][0:EP, 0:EP])
                    last.then_inc(low_transposed, 1)
                    pe.wait_ge(diag_ready, n + 1)
                    pe.wait_ge(ranks_ready, n + 1)
                    for h in range(2):
                        last = nc.tensor.matmul(S0[h][0:EP, 0:4 * EP], c["ones"][0:EP, 0:EP],
                                                src_diag[:, u, h * 4:h * 4 + 4, :].rearrange("p a b -> p (a b)"), start=True, stop=True)
                    last.then_inc(src_rows_ready, 1)
                    pe.wait_ge(low_rows_ready, n + 2)
                    pe.wait_ge(picked_ready, n + 1)
                    for k in range(HALF):
                        before = table[:, :, bass.ds(i * (2 * HALF) + (u * HALF + k), 1)].rearrange("p b a -> p (b a)")
                        nc.tensor.matmul(L0[0:EP, k * NB:(k + 1) * NB], low_rows[:, u, k], before, start=True, stop=False)
                        last = nc.tensor.matmul(L0[0:EP, k * NB:(k + 1) * NB], low_rows[:, u, k], base[:], start=False, stop=True)
                    last.then_inc(looked_up, 1)
                    if u == 0:
                        pe.wait_ge(normed_ready, i + 1)
                        for h in range(2):
                            last = nc.tensor.transpose(X0[:, h * BN:(h + 1) * BN], normed[:, h * 128:(h + 1) * 128], c["ident"][0:BN, 0:BN])
                        last.then_inc(node_transposed, 1)
                        pe.wait_ge(normed_rows, i + 1)
                        for h in range(2):
                            last = nc.tensor.matmul(W0[0:BN, :], normed_t[:, h, :], wqkv_sb[:, h, :], start=(h == 0), stop=(h == 1))
                        last.then_inc(qkv_ready, 1)


def attend(nc, c, records, kv_rows, Wk, bk, Wq, bq):
    with ExitStack() as ctx:
        def sb(name, shape, dt=F32):
            return ctx.enter_context(nc.sbuf_tensor(name, shape, dt))

        def ps(name):
            return ctx.enter_context(nc.psum_tensor(name, [128, 512], F32))

        def sem(name):
            return ctx.enter_context(nc.semaphore(name))

        iota, ident, ones, acc = c["iota"], c["ident"], c["ones"], c["acc"]
        gt = c["bucket_of_tile"]
        K = ATTRS + 1
        rec = sb("rec", [128, 2, SC, WIDE])
        kv = sb("kv", [128, 2, SC, KV])
        onehot = sb("onehot", [128, 2, SC, BN])
        wrpe = sb("wrpe", [K, 2, QK])
        attr_rows = sb("attr_rows", [K, 2, BATCH * 128])
        node_rows = sb("node_rows", [BN, 2, BATCH * 128])
        keys = sb("keys", [128, BATCH * QK])
        product = sb("product", [128, BATCH * QK])
        score = sb("score", [128, 2, PT, PARTS, HEADS])
        src_wide = sb("src_wide", [128, PT, PARTS, HEADS])
        W = PT * 128
        cs = sb("score_src_rows", [128, 2 * W])
        changes = sb("changes", [128, W + 1])
        run = sb("run", [128, 4, W])
        edges = sb("edge_rows", [1, 2, 2, HEADS, PARTS + 1])
        gap = sb("gap", [1, HEADS, PARTS + 1])
        split = sb("split", [1, HEADS, PARTS + 1])
        pen_f = sb("pen_f", [1, HEADS, PARTS + 1])
        pen_b = sb("pen_b", [1, HEADS, PARTS + 1])
        chain_f = sb("chain_f", [1, HEADS, PARTS + 1])
        chain_b = sb("chain_b", [1, HEADS, PARTS + 1])
        carry_rows = sb("carry_rows", [1, 2, PARTS, HEADS])
        carry = sb("carry", [128, 2])
        shifted = sb("shifted", [128, W + 1])
        weight_rows = sb("weight_rows", [128, W + 1])
        factor = sb("factor", [HEADS, HEADS])
        first_node = sb("first_node", [BN, 2])
        rescale = sb("rescale", [BN, HEADS])
        weights = sb("weights", [128, SC, HEADS])
        weighted = sb("weighted", [128, 2, BATCH, HEADS, VD])

        P_attr, P_node, P_q, P_k, P_z0, P_z1, P_max = [ps(f"ps_c{i}") for i in range(7)]
        P_z = [P_z0, P_z1]

        weights_in = sem("weights_in")
        cleared = sem("cleared")
        records_in = [sem(f"records_in{i}") for i in range(2)]
        records_free = sem("records_free2")
        indices_seen = sem("indices_seen")
        kv_in = [sem(f"kv_in{i}") for i in range(2 * NBATCH)]
        onehot_ready = sem("onehot_ready")
        attr_transposed = sem("attr_transposed")
        attr_rows_ready = sem("attr_rows_ready")
        node_transposed = sem("node_transposed2")
        node_rows_ready = sem("node_rows_ready")
        k_ready = sem("k_ready")
        q_ready = sem("q_ready2")
        keys_ready = sem("keys_ready")
        product_ready = sem("product_ready")
        score_ready = sem("score_ready")
        src_wide_ready = sem("src_wide_ready")
        rows_transposed = sem("rows_transposed")
        rows_ready = sem("rows_ready")
        max_step = sem("max_step")
        ends_transposed = sem("ends_transposed")
        ends_ready = sem("ends_ready")
        carry_transposed = sem("carry_transposed")
        carry_seen = sem("carry_seen")
        shifted_ready = sem("shifted_ready")
        exp_ready = sem("exp_ready")
        weights_transposed = sem("weights_transposed")
        weights_ready = sem("weights_ready")
        factor_spread = sem("factor_spread")
        rescaled = sem("rescaled")
        acc_rescaled = sem("acc_rescaled")
        den_ready = sem("den_ready")
        weighted_ready = sem("weighted_ready")
        sums_ready = sem("sums_ready")
        added = sem("added")
        MAX_STEPS = 19

        block = ctx.enter_context(nc.Block())

        SUM_LAG, WEIGH_LAG = 6, 5
        TOTAL = NSC * NBATCH

        def batch(n, p, b, d):
            return n * NBATCH + (b + d), n + (b + d) // NBATCH, (p + (b + d) // NBATCH) % 2, (b + d) % NBATCH

        def exists(number, total=TOTAL):
            return not isinstance(number, int) or 0 <= number < total

        def all_steps(eng, step):
            for b in range(2, NBATCH):
                step(-1, 1, b)
            for n in range(2):
                for b in range(NBATCH):
                    step(n, n % 2, b)
            with eng.Fori(0, (NSC - 4) // 2) as it:
                for u in range(2):
                    for b in range(NBATCH):
                        step(it * 2 + (u + 2), u, b)
            for s in range((NSC - 2) * NBATCH, TOTAL + SUM_LAG):
                step(s // NBATCH, s // NBATCH % 2, s % NBATCH)

        def buckets(engine, first_tile, count):
            _, regs = nc.values_load_multi_w_load_instructions(
                gt[0:1, bass.ds(first_tile, count)], engines=[engine], min_val=0, max_val=NB - 1,
                skip_runtime_bounds_check_because="counted from 0 and clamped to NB - 1 where it is made")
            return regs

        @block.sync
        def _(sp):
            sp.dma_start(wrpe[0:ATTRS, 0, :], Wq).then_inc(weights_in, 16)
            sp.dma_start(wrpe[ATTRS:K, 0, :], bq.rearrange("(a n) -> a n", a=1)).then_inc(weights_in, 16)
            sp.dma_start(wrpe[0:ATTRS, 1, :], Wk).then_inc(weights_in, 16)
            sp.dma_start(wrpe[ATTRS:K, 1, :], bk.rearrange("(a n) -> a n", a=1)).then_inc(weights_in, 16)
            records_v = records.rearrange("(n t p) w -> n p t w", t=SC, p=128)
            with sp.Fori(0, NSC // 2) as it:
                for u in range(2):
                    n = it * 2 + u
                    sp.wait_ge(score_ready, n * NBATCH + 1)
                    sp.sem_inc(records_free, 1)
                    sp.wait_ge(src_wide_ready, n + 1)
                    sp.sem_inc(records_free, 1)
                    sp.dma_start(rec[:, u], records_v[bass.ds(n, 1)].rearrange("a p t w -> p (a t) w")).then_inc(records_in[u], 16)

        @block.gpsimd
        def _(pool):
            nc.gpsimd.memset(acc[:], 0.0).then_inc(cleared, 1)
            nc.gpsimd.memset(changes[:], 0.0).then_inc(cleared, 1)
            nc.gpsimd.memset(edges[:], -BIG).then_inc(cleared, 1)
            nc.gpsimd.memset(gap[:], -BIG).then_inc(cleared, 1)
            nc.gpsimd.memset(pen_f[:], -BIG).then_inc(cleared, 1)
            nc.gpsimd.memset(pen_b[:], -BIG).then_inc(cleared, 1)
            nc.gpsimd.memset(shifted[:], 0.0).then_inc(cleared, 1)
            with pool.Fori(0, NSC // 2) as it:
                for u in range(2):
                    n = it * 2 + u
                    pool.wait_ge(records_in[u], it * 16 + 16)
                    pool.sem_inc(indices_seen, 1)
                    for b in range(NBATCH):
                        pool.wait_ge(weighted_ready, n * NBATCH + (b + 1))
                        pool.sem_inc(indices_seen, 1)
                        for t in range(b * BATCH, (b + 1) * BATCH):
                            nc.gpsimd.indirect_dma_start(
                                out=kv[:, u, t, :], out_offset=None, in_=kv_rows,
                                in_offset=bass.IndirectOffsetOnAxis(ap=rec[:, u, t, DST:DST + 1].bitcast(I32), axis=0)
                            ).then_inc(kv_in[u * NBATCH + b], 16)

        @block.scalar
        def _(act):
            act.sem_inc(attr_rows_ready, 1)
            act.sem_inc(node_rows_ready, 1)
            act.sem_inc(src_wide_ready, 2)
            act.sem_inc(exp_ready, 1)
            act.sem_inc(den_ready, 1)

            def step(n, p, b):
                m = n - 1
                if b == 0 and exists(m, NSC):
                    act.wait_ge(rows_transposed, m + 3)
                    act.wait_ge(shifted_ready, m + 1)
                    nc.scalar.activation(cs[:], P_max[:], ACT.Copy).then_inc(rows_ready, 1)
                B, g, pg, bb = batch(n, p, b, 1)
                if exists(B):
                    act.wait_ge(node_transposed, B + 1)
                    act.wait_ge(q_ready, B + 1)
                    if bb == 0:
                        act.wait_ge(rescaled, g + 1)
                        nc.scalar.activation(first_node[:, pg:pg + 1], P_node[0:BN, 0:1], ACT.Copy)
                    nc.scalar.activation(node_rows[:, bb % 2], P_node[0:BN, :], ACT.Copy).then_inc(node_rows_ready, 1)
                if b == 0 and exists(m, NSC):
                    act.wait_ge(ends_transposed, m + 1)
                    r = P_max[0:1, :].rearrange("a (e j k h) -> a e j h k", e=2, j=2, h=HEADS)
                    act.activation(edges[:, 0, :, :, 0:PARTS], r[:, 0], ACT.Copy)
                    act.activation(edges[:, 1, :, :, 1:PARTS + 1], r[:, 1], ACT.Copy).then_inc(ends_ready, 1)
                if b == 1 and exists(m, NSC):
                    act.wait_ge(shifted_ready, m + 2)
                    act.wait_ge(weights_transposed, m + 1)
                    act.wait_ge(rescaled, m + 2)
                    nc.scalar.activation(weight_rows[:], shifted[:], ACT.Exp).then_inc(exp_ready, 1)
                    act.wait_ge(weights_transposed, m + 2)
                    act.wait_ge(weighted_ready, m * NBATCH + 2 * NBATCH)
                    act.wait_ge(den_ready, m * NBATCH + 1)
                    nc.scalar.activation(weights[:].rearrange("p (k i) h -> p k i h", i=PT),
                                         P_max[:, 0:W].rearrange("p (i k h) -> p k i h", i=PT, k=PARTS), ACT.Copy).then_inc(weights_ready, 1)
                if b == 3 and exists(n, NSC):
                    act.wait_ge(records_in[p], (n - p) * 8 + 16)
                    act.wait_ge(rows_transposed, n + 2)
                    nc.scalar.activation(src_wide[:].rearrange("p i k h -> p k i h"),
                                         rec[:, p, :, SRC:SRC + 1].rearrange("p (k i) a -> p k i a", i=PT).broadcast_to([128, PARTS, PT, HEADS]),
                                         ACT.Copy).then_inc(src_wide_ready, 1)
                B, g, pg, bb = batch(n, p, b, 2)
                if exists(B):
                    act.wait_ge(attr_transposed, B + 1)
                    act.wait_ge(q_ready, B + 1)
                    nc.scalar.activation(attr_rows[:, bb % 2], P_attr[0:K, :], ACT.Copy).then_inc(attr_rows_ready, 1)
                B, g, pg, bb = batch(n, p, b, -WEIGH_LAG)
                if exists(B):
                    act.wait_ge(weights_ready, g + 1)
                    act.wait_ge(sums_ready, B * BATCH + (2 * SC - BATCH))
                    nc.scalar.activation(weighted[:, bb % 2, :, :, HEAD_V], weights[:, bb * BATCH:(bb + 1) * BATCH, :], ACT.Copy).then_inc(den_ready, 1)

            all_steps(act, step)

        @block.vector
        def _(dve):
            dve.sem_inc(keys_ready, 1)
            dve.sem_inc(product_ready, 1)
            dve.sem_inc(score_ready, NBATCH + 1)
            dve.sem_inc(shifted_ready, 1)
            dve.sem_inc(weighted_ready, 2 * NBATCH)
            dve.sem_inc(rescaled, 2)
            dve.sem_inc(added, 2)
            dve.wait_ge(cleared, 7)
            scores, sources = cs[:, 0:W], cs[:, W:2 * W]
            first_src, last_src = edges[:, 0, 1, :, 0:PARTS], edges[:, 1, 1, :, :]

            def counted(ins):
                ins.then_inc(max_step, 1)

            def local_maxima(m):
                def after(k):
                    dve.wait_ge(max_step, m * MAX_STEPS + k)

                dve.wait_ge(rows_ready, m + 1)
                counted(nc.vector.tensor_tensor(changes[:, 1:W], sources[:, 1:W], sources[:, 0:W - 1], ALU.not_equal))
                after(1)
                counted(nc.vector.tensor_scalar(changes[:, 1:W], changes[:, 1:W], -BIG, None, ALU.mult))
                after(2)
                counted(nc.vector.tensor_tensor_scan(run[:, 0], changes[:, 0:W], scores, -BIG, ALU.add, ALU.max))
                after(3)
                counted(nc.vector.tensor_tensor_scan(run[:, 1, ::-1], changes[:, W:0:-1], run[:, 0, ::-1], -BIG, ALU.add, ALU.max))

            def flat(a):
                return a.rearrange("a h k -> a (h k)")

            def carries(m):
                def after(k):
                    dve.wait_ge(max_step, m * MAX_STEPS + k)

                dve.wait_ge(ends_ready, m + 1)
                counted(nc.vector.tensor_tensor(gap[:, :, 0:PARTS], first_src, last_src[:, :, 0:PARTS], ALU.not_equal))
                counted(nc.vector.tensor_tensor(split[:, :, 0:PARTS], first_src, last_src[:, :, 1:PARTS + 1], ALU.not_equal))
                after(5)
                counted(nc.vector.tensor_scalar(gap[:, :, 0:PARTS], gap[:, :, 0:PARTS], -BIG, None, ALU.mult))
                after(7)
                counted(nc.vector.scalar_tensor_tensor(pen_f[:, :, 1:PARTS + 1], split[:, :, 0:PARTS], -BIG, gap[:, :, 0:PARTS], ALU.mult, ALU.min))
                counted(nc.vector.scalar_tensor_tensor(pen_b[:, :, 0:PARTS], split[:, :, 0:PARTS], -BIG, gap[:, :, 1:PARTS + 1], ALU.mult, ALU.min))
                after(9)
                counted(nc.vector.tensor_tensor_scan(flat(chain_f[:]), flat(pen_f[:]), flat(edges[:, 1, 0]), -BIG, ALU.add, ALU.max))
                counted(nc.vector.tensor_tensor_scan(flat(chain_b[:])[:, ::-1], flat(pen_b[:])[:, ::-1], flat(edges[:, 0, 0])[:, ::-1], -BIG, ALU.add, ALU.max))
                after(11)
                counted(nc.vector.tensor_tensor(carry_rows[:, 0].rearrange("a k h -> a h k"), chain_f[:, :, 0:PARTS], gap[:, :, 0:PARTS], ALU.add))
                counted(nc.vector.tensor_tensor(carry_rows[:, 1].rearrange("a k h -> a h k"), chain_b[:, :, 1:PARTS + 1], gap[:, :, 1:PARTS + 1], ALU.add))
                counted(nc.vector.tensor_copy(edges[:, 1, 0, :, 0], chain_f[:, :, PARTS]))
                counted(nc.vector.tensor_copy(edges[:, 1, 1, :, 0], edges[:, 1, 1, :, PARTS]))

            def full_maxima(m):
                def after(k):
                    dve.wait_ge(max_step, m * MAX_STEPS + k)

                dve.wait_ge(carry_transposed, m + 1)
                counted(nc.vector.tensor_copy(carry[:], P_max[:, W:W + 2]))
                after(16)
                counted(nc.vector.tensor_tensor_scan(run[:, 2], changes[:, 0:W], scores, carry[:, 0:1], ALU.add, ALU.max))
                after(17)
                counted(nc.vector.tensor_tensor_scan(run[:, 3, ::-1], changes[:, W:0:-1], run[:, 2, ::-1], carry[:, 1:2], ALU.add, ALU.max))
                after(18)
                dve.wait_ge(exp_ready, m + 1)
                nc.vector.tensor_tensor(shifted[:, 0:W], scores, run[:, 3], ALU.subtract)
                nc.vector.tensor_tensor(shifted[0:HEADS, W:W + 1], carry[0:HEADS, 0:1], run[0:HEADS, 3, 0:1], ALU.subtract).then_inc(shifted_ready, 1)

            def factors(m):
                dve.wait_ge(exp_ready, m + 2)
                counted(nc.vector.scalar_tensor_tensor(factor[:], ident[0:HEADS, 0:HEADS], weight_rows[0:HEADS, W:W + 1], ident[0:HEADS, 0:HEADS], ALU.mult, ALU.subtract))

            def rescale_carried(m, p):
                dve.wait_ge(factor_spread, m + 1)
                nc.vector.tensor_scalar(rescale[:], P_max[0:BN, 0:HEADS], first_node[:, p:p + 1], 1.0, ALU.mult, ALU.add).then_inc(rescaled, 1)
                g = buckets(DVE_ENGINE, m * SC, 1)[0]
                a = acc[:, bass.ds(g, 1), :].rearrange("p a (h d) -> p (a h) d", d=VD)
                dve.wait_ge(rescaled, m + 3)
                dve.wait_ge(added, m * SC + 2)
                nc.vector.tensor_tensor(a, a, rescale[:].unsqueeze(2).broadcast_to([BN, HEADS, VD]), ALU.mult).then_inc(acc_rescaled, 1)

            def step(n, p, b):
                m = n - 1
                B, g, pg, bb = batch(n, p, b, 0)
                tiles = slice(bb * BATCH, (bb + 1) * BATCH)
                if exists(B):
                    dve.wait_ge(kv_in[pg * NBATCH + bb], (g - pg) * 32 + 64)
                    dve.wait_ge(k_ready, B + 1)
                    nc.vector.tensor_tensor(keys[:].rearrange("p (t d) -> p t d", d=QK), kv[:, pg, tiles, 0:QK],
                                            P_k[:].rearrange("p (t d) -> p t d", d=QK), ALU.add).then_inc(keys_ready, 1)
                if b == 1 and exists(m, NSC):
                    full_maxima(m)
                if exists(B):
                    dve.wait_ge(q_ready, B + 3)
                    dve.wait_ge(keys_ready, B + 2)
                    nc.vector.tensor_tensor(product[:], keys[:], P_q[:], ALU.mult).then_inc(product_ready, 1)
                    dve.wait_ge(product_ready, B + 2)
                    dve.wait_ge(rows_transposed, n + 1)
                    k0 = bb * BATCH // PT
                    nc.vector.tensor_reduce(score[:, pg, :, k0:k0 + BATCH // PT, :].rearrange("p i k h -> p k i h"),
                                            product[:].rearrange("p (k i h d) -> p k i h d", i=PT, h=HEADS, d=HEAD_QK), AX.X, ALU.add).then_inc(score_ready, 1)
                if b == 2 and exists(m, NSC):
                    rescale_carried(m, 1 - p)
                B, g, pg, bb = batch(n, p, b, -SUM_LAG)
                if exists(B):
                    regs = buckets(DVE_ENGINE, B * BATCH, BATCH)
                    dve.wait_ge(acc_rescaled, g + 1)
                for k in range(BATCH):
                    if k == 2 and b == 0 and exists(m, NSC):
                        local_maxima(m)
                    if exists(B):
                        a = acc[:, bass.ds(regs[k], 1), :].rearrange("p a d -> p (a d)")
                        dve.wait_ge(added, B * BATCH + (k + 2))
                        dve.wait_ge(sums_ready, B * BATCH + (2 * SC + k + 1))
                        nc.vector.tensor_tensor(a, a, P_z[k % 2][0:BN, 0:ACCW], ALU.add).then_inc(added, 1)
                B, g, pg, bb = batch(n, p, b, -WEIGH_LAG)
                tiles = slice(bb * BATCH, (bb + 1) * BATCH)
                if exists(B):
                    dve.wait_ge(weights_ready, g + 1)
                    dve.wait_ge(sums_ready, B * BATCH + (2 * SC - BATCH))
                    nc.vector.tensor_tensor(weighted[:, bb % 2, :, :, 0:HEAD_V],
                                            kv[:, pg, tiles, QK:KV].rearrange("p t (h d) -> p t h d", d=HEAD_V),
                                            weights[:, tiles, :].unsqueeze(3).broadcast_to([128, BATCH, HEADS, HEAD_V]), ALU.mult).then_inc(weighted_ready, 1)
                if b == 0 and exists(m, NSC):
                    carries(m)
                if b == 1 and exists(m, NSC):
                    factors(m)
                B, g, pg, bb = batch(n, p, b, 2)
                tiles = slice(bb * BATCH, (bb + 1) * BATCH)
                if exists(B):
                    dve.wait_ge(records_in[pg], (g - pg) * 8 + 16)
                    dve.wait_ge(sums_ready, B * BATCH + BATCH)
                    nc.vector.tensor_tensor(onehot[:, pg, tiles], iota[:, None, 0:BN].broadcast_to([128, BATCH, BN]),
                                            rec[:, pg, tiles, LOW:LOW + 1].broadcast_to([128, BATCH, BN]), ALU.is_equal).then_inc(onehot_ready, 1)

            all_steps(dve, step)

        @block.tensor
        def _(pe):
            pe.sem_inc(q_ready, 2)
            pe.sem_inc(rows_transposed, 2)
            pe.sem_inc(weights_transposed, 1)
            pe.sem_inc(sums_ready, 2 * SC)
            pe.wait_ge(weights_in, 64)

            def step(n, p, b):
                m = n - 1
                if b == 0 and exists(m, NSC):
                    pe.wait_ge(score_ready, m * NBATCH + (2 * NBATCH + 1))
                    pe.wait_ge(src_wide_ready, m + 3)
                    pe.wait_ge(rescaled, m + 2)
                    for i in range(PT):
                        nc.tensor.transpose(P_max[:, i * 128:(i + 1) * 128], score[:, 1 - p, i].rearrange("p k h -> p (k h)"), ident[:])
                    for i in range(PT):
                        last = nc.tensor.transpose(P_max[:, W + i * 128:W + (i + 1) * 128], src_wide[:, i].rearrange("p k h -> p (k h)"), ident[:])
                    last.then_inc(rows_transposed, 1)
                if b == 2 and exists(m, NSC):
                    pe.wait_ge(max_step, m * MAX_STEPS + MAX_STEPS)
                    pe.wait_ge(weights_ready, m + 1)
                    nc.tensor.matmul(P_max[0:BN, 0:HEADS], ones[0:HEADS, 0:BN], factor[:], start=True, stop=True).then_inc(factor_spread, 1)
                B, g, pg, bb = batch(n, p, b, 1)
                if exists(B):
                    pe.wait_ge(onehot_ready, B + 1)
                    pe.wait_ge(node_rows_ready, B + 1)
                    for k in range(BATCH):
                        last = nc.tensor.transpose(P_node[0:BN, k * 128:(k + 1) * 128], onehot[:, pg, bb * BATCH + k], ident[:])
                    last.then_inc(node_transposed, 1)
                if b == 1 and exists(m, NSC):
                    pe.wait_ge(max_step, m * MAX_STEPS + 13)
                    pe.sem_inc(carry_seen, 1)
                    for j in range(2):
                        last = nc.tensor.transpose(P_max[:, W + j:W + j + 1], carry_rows[:, j].rearrange("a k h -> a (k h)"), ident[0:1, 0:1])
                    last.then_inc(carry_transposed, 1)
                if exists(B):
                    pe.wait_ge(attr_rows_ready, B + 2)
                    pe.wait_ge(keys_ready, B + 1)
                    for k in range(BATCH):
                        cols = slice(k * 128, (k + 1) * 128)
                        last = nc.tensor.matmul(P_k[:, cols], attr_rows[:, bb % 2, cols], wrpe[:, 1, :], start=True, stop=True)
                    last.then_inc(k_ready, 1)
                Z, gz, pz, bz = batch(n, p, b, -SUM_LAG)
                if exists(Z):
                    pe.wait_ge(weighted_ready, Z + (2 * NBATCH + 1))
                    pe.wait_ge(den_ready, Z + 2)
                    for k in range(BATCH):
                        pe.wait_ge(added, Z * BATCH + (k + 1))
                        nc.tensor.matmul(P_z[k % 2][0:BN, 0:ACCW], onehot[:, pz, bz * BATCH + k], weighted[:, bz % 2, k].rearrange("p h d -> p (h d)"),
                                         start=True, stop=True).then_inc(sums_ready, 1)
                if b == 0 and exists(m, NSC):
                    pe.wait_ge(max_step, m * MAX_STEPS + 4)
                    for j, col in enumerate((run[:, 1, 0:1], cs[:, W:W + 1], run[:, 1, W - 1:W], cs[:, 2 * W - 1:2 * W])):
                        last = nc.tensor.transpose(P_max[0:1, j * 128:(j + 1) * 128], col, ident[:])
                    last.then_inc(ends_transposed, 1)
                if b == 1 and exists(m, NSC):
                    pe.wait_ge(exp_ready, m + 2)
                    for i in range(PT):
                        last = nc.tensor.transpose(P_max[:, i * 128:(i + 1) * 128], weight_rows[:, i * 128:(i + 1) * 128], ident[:])
                    last.then_inc(weights_transposed, 1)
                if exists(B):
                    regs = buckets(PE_ENGINE, B * BATCH, BATCH)
                    pe.wait_ge(node_rows_ready, B + 2)
                    pe.wait_ge(product_ready, B + 1)
                    for k in range(BATCH):
                        cols = slice(k * 128, (k + 1) * 128)
                        q = c["q"][:, bass.ds(regs[k], 1), :].rearrange("p a d -> p (a d)")
                        nc.tensor.matmul(P_q[:, cols], attr_rows[:, bb % 2, cols], wrpe[:, 0, :], start=True, stop=False)
                        last = nc.tensor.matmul(P_q[:, cols], node_rows[:, bb % 2, cols], q, start=False, stop=True)
                    last.then_inc(q_ready, 1)
                B, g, pg, bb = batch(n, p, b, 2)
                if exists(B):
                    pe.wait_ge(records_in[pg], (g - pg) * 8 + 16)
                    pe.wait_ge(attr_rows_ready, B + 1)
                    for k in range(BATCH):
                        last = nc.tensor.transpose(P_attr[0:K, k * 128:(k + 1) * 128], rec[:, pg, bb * BATCH + k, 0:K], ident[:])
                    last.then_inc(attr_transposed, 1)

            all_steps(pe, step)


def feed_forward(nc, c, wr, br, w1, b1, w2, b2, route_dram, out):
    GB = 5
    GN = GB * BN
    NG = NB // GB
    FC = HIDDEN // 128
    SPLIT = [(0, 320), (320, GN - 320)]
    with ExitStack() as ctx:
        def sb(name, shape, dt=F32):
            return ctx.enter_context(nc.sbuf_tensor(name, shape, dt))

        def ps(name):
            return ctx.enter_context(nc.psum_tensor(name, [128, 512], F32))

        def sem(name):
            return ctx.enter_context(nc.semaphore(name))

        x, acc, ident, ones, below = c["x"], c["acc"], c["ident"], c["ones"], c["below"]
        y = acc
        compared = c["q"][:].rearrange("p b d -> p (b d)")
        w1_sb = sb("w1_sb", [128, 2, HIDDEN])
        w2_sb = sb("w2_sb", [128, FC, DIM])
        b1_sb = sb("b1_sb", [128, FC])
        b2_sb = sb("b2_sb", [1, DIM])
        wr_sb = sb("wr_sb", [BN, DIM])
        br_sb = sb("br_sb", [BN, 1])
        inverse = sb("inverse", [BN, NB, HEADS])
        stats = sb("ff_stats", [BN, GB, 6])
        mean_var = sb("ff_mean_var", [BN, GB, 2])
        spread = sb("ff_spread", [BN, 3, GB])
        normed = sb("ff_normed", [BN, NB, DIM])
        normed_t = sb("ff_normed_t", [128, 2, NODES])
        hidden = sb("hidden", [128, FC, GN])
        stage = sb("stage", [BN, GB, DIM])
        routed = sb("routed", [BN, GB, DIM])
        route5 = sb("route5", [BN, GB])
        route = sb("route", [BN, NB])
        route_t = sb("route_t", [NB, BN])
        route_row = sb("route_row", [BN, NODES])
        counts = sb("counts", [BN, NB, 3])
        rank = sb("ff_rank", [BN, NB])
        gain = sb("gain", [BN, NB])
        P_h = [[ps(f"ps_h{i}{j}") for j in range(2)] for i in range(2)]
        P_y = [ps(f"ps_y{i}") for i in range(2)]
        P_t = [ps(f"ps_t{i}") for i in range(2)]

        loaded = sem("loaded")
        inverse_step = sem("inverse_step")
        att_step = sem("att_step")
        stats_seen = sem("stats_seen")
        root_ready = sem("ff_root_ready")
        inv_root = sem("inv_root")
        normed_ready = sem("ff_normed_ready")
        routed_ready = sem("routed_ready")
        residual_ready = sem("residual_ready")
        transposed = sem("ff_transposed")
        normed_t_ready = sem("normed_t_ready")
        up_ready = sem("up_ready")
        hidden_ready = sem("hidden_ready")
        down_ready = sem("down_ready")
        y_ready = sem("y_ready")
        route_transposed = sem("route_transposed")
        route_t_ready = sem("route_t_ready")
        route_out = sem("route_out")
        route_in = sem("route_in")
        rank_step = sem("rank_step")
        result_ready = sem("result_ready")
        stored = sem("stored")
        staged = sem("staged")
        block = ctx.enter_context(nc.Block())

        @block.sync
        def _(sp):
            sp.dma_start(wr_sb[:], wr.rearrange("d a -> a d").broadcast_to([BN, DIM])).then_inc(loaded, 16)
            sp.dma_start(br_sb[:], br.rearrange("(a n) -> a n", a=1).broadcast_to([BN, 1])).then_inc(loaded, 16)
            sp.dma_start(w1_sb[:], w1.rearrange("(k p) n -> p k n", p=128)).then_inc(loaded, 16)
            with nc.allow_non_contiguous_dma(reason="1024 biases, once"):
                sp.dma_start(b1_sb[:], b1.rearrange("(f p) -> p f", p=128)).then_inc(loaded, 16)
            sp.dma_start(w2_sb[:], w2.rearrange("(f p) n -> p f n", p=128)).then_inc(loaded, 16)
            sp.dma_start(b2_sb[:], b2.rearrange("(a n) -> a n", a=1)).then_inc(loaded, 16)
            sp.wait_ge(route_t_ready, 1)
            sp.dma_start(route_dram.rearrange("(b p) -> b p", p=BN), route_t[:]).then_inc(route_out, 16)
            sp.wait_ge(route_out, 16)
            sp.dma_start(route_row[:], route_dram.rearrange("(a n) -> a n", a=1).broadcast_to([BN, NODES])).then_inc(route_in, 16)
            out_v = out.rearrange("(b p) d -> p b d", p=BN)
            for g in range(NG):
                sp.wait_ge(result_ready, GB * (g + 1))
                sp.dma_start(out_v[:, g * GB:(g + 1) * GB, :], x[:, g * GB:(g + 1) * GB, :]).then_inc(stored, 16)
            sp.wait_ge(stored, 16 * NG)

        @block.scalar
        def _(act):
            act.sem_inc(normed_t_ready, 1)
            act.sem_inc(hidden_ready, 4)
            act.sem_inc(y_ready, 2)

            with act.Fori(0, NG) as g:
                act.wait_ge(att_step, g * 5 + 5)
                nc.scalar.activation(spread[:, 1, :], spread[:, 0, :], ACT.Sqrt).then_inc(root_ready, 1)
            act.wait_ge(route_transposed, 1)
            nc.scalar.activation(route_t[:], P_t[0][0:NB, 0:BN], ACT.Copy).then_inc(route_t_ready, 1)
            act.wait_ge(loaded, 96)
            with act.Fori(0, NG) as g:
                act.wait_ge(transposed, g * 2 + 1)
                nc.scalar.activation(stage[:], normed[:, bass.ds(g * GB, GB), :], ACT.Copy).then_inc(staged, 1)
                for k in range(2):
                    act.wait_ge(transposed, g * 2 + (k + 2))
                    nc.scalar.activation(normed_t[:, k, bass.ds(g * GN, 4 * BN)], P_t[0][:, 0:4 * BN], ACT.Copy)
                    nc.scalar.activation(normed_t[:, k, bass.ds(g * GN + 4 * BN, BN)], P_t[1][:, 0:BN], ACT.Copy).then_inc(normed_t_ready, 1)
                act.wait_ge(down_ready, g * GB + 1)
                for f in range(FC):
                    for j, (at, n) in enumerate(SPLIT):
                        act.wait_ge(up_ready, g * (2 * FC) + (2 * f + j + 1))
                        nc.scalar.activation(hidden[:, f, at:at + n], P_h[f % 2][j][:, 0:n], ACT.Gelu_apprx_tanh,
                                             bias=b1_sb[:, f:f + 1]).then_inc(hidden_ready, 1)
                for b in range(GB):
                    act.wait_ge(down_ready, g * GB + (b + 2))
                    nc.scalar.activation(y[:, bass.ds(g * GB + b, 1), 0:DIM].rearrange("p a d -> p (a d)"), P_y[b % 2][0:BN, 0:DIM], ACT.Copy).then_inc(y_ready, 1)

        @block.vector
        def _(dve):
            nc.vector.tensor_scalar(inverse[:], acc[:].rearrange("p b (h d) -> p b h d", d=VD)[:, :, :, HEAD_V], EPS_DEN, None, ALU.add).then_inc(inverse_step, 1)
            dve.wait_ge(inverse_step, 1)
            nc.vector.reciprocal(inverse[:], inverse[:]).then_inc(inverse_step, 1)
            dve.wait_ge(inverse_step, 2)
            dve.wait_ge(loaded, 96)
            with dve.Fori(0, NG) as g:
                five = bass.ds(g * GB, GB)
                sums = acc[:, five, :].rearrange("p b (h d) -> p (b h) d", d=VD)[:, :, 0:HEAD_V]
                nc.vector.tensor_tensor(sums, sums, inverse[:, five, :].rearrange("p b h -> p (b h)").unsqueeze(2).broadcast_to([BN, GB * HEADS, HEAD_V]), ALU.mult).then_inc(att_step, 1)
                dve.wait_ge(att_step, g * 5 + 1)
                nc.vector.tensor_tensor(x[:, five, :].rearrange("p b (h d) -> p (b h) d", d=HEAD_V), x[:, five, :].rearrange("p b (h d) -> p (b h) d", d=HEAD_V), sums, ALU.add).then_inc(att_step, 1)
                dve.wait_ge(att_step, g * 5 + 2)
                dve.sem_inc(stats_seen, 1)
                for b in range(GB):
                    last = nc.vector.bn_stats(stats[:, b], x[:, bass.ds(g * GB + b, 1), :].rearrange("p a d -> p (a d)"))
                last.then_inc(att_step, 1)
                dve.wait_ge(att_step, g * 5 + 3)
                dve.sem_inc(stats_seen, 1)
                for b in range(GB):
                    last = nc.vector.bn_aggr(mean_var[:, b], stats[:, b])
                last.then_inc(att_step, 1)
                dve.wait_ge(att_step, g * 5 + 4)
                nc.vector.tensor_scalar(spread[:, 0, :], mean_var[:, :, 1], EPS_LN, None, ALU.add).then_inc(att_step, 1)
                dve.wait_ge(root_ready, g + 1)
                nc.vector.reciprocal(spread[:, 2, :], spread[:, 1, :]).then_inc(inv_root, 1)
                dve.wait_ge(inv_root, g + 1)
                for b in range(GB):
                    last = nc.vector.tensor_scalar(normed[:, bass.ds(g * GB + b, 1), :].rearrange("p a d -> p (a d)"),
                                                   x[:, bass.ds(g * GB + b, 1), :].rearrange("p a d -> p (a d)"),
                                                   mean_var[:, b, 0:1], spread[:, 2, b:b + 1], ALU.subtract, ALU.mult)
                last.then_inc(normed_ready, 1)
                dve.wait_ge(normed_ready, g + 1)
                for b in range(GB):
                    last = nc.vector.scalar_tensor_tensor(routed[:, b], normed[:, bass.ds(g * GB + b, 1), :].rearrange("p a d -> p (a d)"), 1.0,
                                                          wr_sb[:], ALU.mult, ALU.mult, accum_out=route5[:, b:b + 1])
                last.then_inc(routed_ready, 1)
                nc.vector.tensor_tensor(x[:, five, :], x[:, five, :], normed[:, five, :], ALU.add).then_inc(residual_ready, 1)
                dve.wait_ge(routed_ready, g + 1)
                nc.vector.tensor_scalar(route[:, five], route5[:], br_sb[:], None, ALU.add).then_inc(inverse_step, 1)
            dve.wait_ge(route_in, 16)
            for b in range(NB):
                w = route[:, b:b + 1]
                at = b * BN
                if b:
                    dve.wait_ge(rank_step, 3 * b)
                    nc.vector.tensor_scalar(compared[:, 0:at], route_row[:, 0:at], w, 0.0, ALU.is_ge, ALU.add, accum_out=counts[:, b, 0:1]).then_inc(rank_step, 1)
                else:
                    nc.vector.memset(counts[:, 0, 0:1], 0.0).then_inc(rank_step, 1)
                nc.vector.tensor_scalar(compared[:, at:NODES], route_row[:, at:NODES], w, 0.0, ALU.is_gt, ALU.add, accum_out=counts[:, b, 1:2]).then_inc(rank_step, 1)
                nc.vector.scalar_tensor_tensor(routed[:, b % GB, 0:BN], route_row[:, at:at + BN], w, below[0:BN, 0:BN], ALU.is_equal, ALU.mult,
                                               accum_out=counts[:, b, 2:3]).then_inc(rank_step, 1)
            dve.wait_ge(rank_step, 3 * NB)
            nc.vector.tensor_reduce(rank[:], counts[:], AX.X, ALU.add).then_inc(rank_step, 1)
            dve.wait_ge(rank_step, 3 * NB + 1)
            nc.vector.scalar_tensor_tensor(gain[:], rank[:], float(KEPT), route[:], ALU.is_lt, ALU.mult).then_inc(rank_step, 1)
            dve.wait_ge(rank_step, 3 * NB + 2)
            for b in range(NB):
                dve.wait_ge(y_ready, b + 3)
                nc.vector.scalar_tensor_tensor(x[:, b, :], y[:, b, 0:DIM], gain[:, b:b + 1], x[:, b, :], ALU.mult, ALU.add).then_inc(result_ready, 1)

        @block.tensor
        def _(pe):
            pe.sem_inc(down_ready, 1)
            pe.sem_inc(transposed, 1)
            pe.wait_ge(inverse_step, 2 + NG)
            nc.tensor.transpose(P_t[0][0:NB, 0:BN], route[:], ident[0:BN, 0:BN]).then_inc(route_transposed, 1)
            pe.wait_ge(route_t_ready, 1)
            pe.wait_ge(loaded, 96)
            with pe.Fori(0, NG) as g:
                pe.wait_ge(staged, g + 1)
                for k in range(2):
                    pe.wait_ge(normed_t_ready, g * 2 + (k + 1))
                    for b in range(GB):
                        last = nc.tensor.transpose(P_t[b // 4][:, (b % 4) * BN:(b % 4 + 1) * BN],
                                                   stage[:, b, k * 128:(k + 1) * 128], ident[0:BN, 0:BN])
                    last.then_inc(transposed, 1)
                pe.wait_ge(normed_t_ready, g * 2 + 3)
                for f in range(FC):
                    for j, (at, n) in enumerate(SPLIT):
                        pe.wait_ge(hidden_ready, g * (2 * FC) + (2 * f + j + 1))
                        for k in range(2):
                            last = nc.tensor.matmul(P_h[f % 2][j][:, 0:n], w1_sb[:, k, f * 128:(f + 1) * 128],
                                                    normed_t[:, k, bass.ds(g * GN + at, n)], start=(k == 0), stop=(k == 1))
                        last.then_inc(up_ready, 1)
                pe.wait_ge(hidden_ready, g * (2 * FC) + (2 * FC + 4))
                for b in range(GB):
                    pe.wait_ge(y_ready, g * GB + (b + 1))
                    for f in range(FC):
                        nc.tensor.matmul(P_y[b % 2][0:BN, 0:DIM], hidden[:, f, b * BN:(b + 1) * BN], w2_sb[:, f, :], start=(f == 0), stop=False)
                    nc.tensor.matmul(P_y[b % 2][0:BN, 0:DIM], ones[0:1, 0:BN], b2_sb[:], start=False, stop=True).then_inc(down_ready, 1)


_INS = ["x", "src", "dst", "edge_attr_18", "L0_gnn_Wqkv", "L0_gnn_bqkv", "L0_gnn_Wk_rpe", "L0_gnn_bk_rpe", "L0_gnn_Wq_rpe", "L0_gnn_bq_rpe",
        "L0_ffn_attention_mask", "L0_ffn_wr", "L0_ffn_br", "L0_ffn_w1", "L0_ffn_b1", "L0_ffn_w2", "L0_ffn_b2"]
_OUTS = [((NODES, DIM), "float32")]


def kernel(**inputs):
    import numpy as _np
    import concourse.bacc as _bacc
    from concourse import mybir as _mybir
    from concourse.bass_utils import run_bass_kernel_spmd as _run

    nc = _bacc.Bacc("TRN2", target_bir_lowering=False, num_devices=1)
    arrays, args = {}, []
    for name in _INS:
        a = _np.ascontiguousarray(inputs[name])
        arrays[f"in_{name}_dram"] = a
        args.append(nc.dram_tensor(f"in_{name}_dram", a.shape, _mybir.dt.from_np(a.dtype), kind="ExternalInput").ap())
    for i, (shape, dtype) in enumerate(_OUTS):
        dt = _mybir.dt.from_np(_np.dtype(dtype))
        args.append(nc.dram_tensor(f"out_{i}_dram", shape, dt, kind="ExternalOutput").ap())
    gnn_ffn_kernel(nc, *args)
    r = _run(nc, [arrays], core_ids=[0])
    return r.results[0]["out_0_dram"]
```

```python
from contextlib import ExitStack

import concourse.bass as bass
from concourse import mybir

F32 = mybir.dt.float32
BF16 = mybir.dt.bfloat16
I32 = mybir.dt.int32
ALU = mybir.AluOpType
ACT = mybir.ActivationFunctionType
AX = mybir.AxisListType
PE_ENGINE = mybir.EngineType.PE
DVE_ENGINE = mybir.EngineType.DVE

NODES, DIM, EDGES, ATTRS = 3125, 256, 50000, 18
HEADS, QK = 16, 128
HEAD_QK = QK // HEADS
HEAD_V = DIM // HEADS
QKV = 2 * QK + DIM
KV = QK + DIM
HIDDEN = 1024
KEPT = NODES // 2 - 1
SCALE = HEAD_QK**-0.5
EPS_LN, EPS_DEN = 1e-5, 1e-16
BIG = 1e30

BN = 125
NB = NODES // BN
EP, EC = 125, EDGES // 125
HALF = 8
STEPS = EC // (2 * HALF)
TILE = 128
SC = 16
NSC = -(-(EDGES // TILE + NB) // SC)
NT = NSC * SC
PARTS = 8
PT = SC // PARTS
BATCH = 4
NBATCH = SC // BATCH
ONE, SRC, LOW, DST, WIDE = ATTRS, ATTRS + 1, ATTRS + 2, ATTRS + 3, ATTRS + 4
VD = HEAD_V + 1
ACCW = HEADS * VD
GCOL = NT // 4

assert NB * BN == NODES and STEPS * 2 * HALF == EC and STEPS == NB and NT == 4 * GCOL
assert PARTS * HEADS == 128


def gnn_ffn_kernel(nc, x, src, dst, attrs, Wqkv, bqkv, Wk, bk, Wq, bq, mask, wr, br, w1, b1, w2, b2, out):
    records = nc.dram_tensor("edge_records", [NT * TILE, WIDE], F32, kind="Internal").ap()
    kv_rows = nc.dram_tensor("kv_rows", [NODES, KV], F32, kind="Internal").ap()
    route_dram = nc.dram_tensor("route_dram", [NODES], F32, kind="Internal").ap()

    with ExitStack() as keep:
        def lasting(name, shape, dt=F32):
            return keep.enter_context(nc.sbuf_tensor(name, shape, dt))

        c = {
            "x": lasting("x_sb", [BN, NB, DIM]),
            "q": lasting("q_sb", [BN, NB, QK]),
            "bucket_of_tile": lasting("bucket_of_tile", [1, NT], I32),
            "ident": lasting("ident", [128, 128]),
            "iota": lasting("iota_row", [128, 128]),
            "below": lasting("below", [128, 128]),
            "above": lasting("above", [128, 128]),
            "ones": lasting("ones", [128, 128]),
        }
        order_edges(nc, c, x, src, dst, attrs, Wqkv, bqkv, records, kv_rows)
        c["acc"] = lasting("acc", [BN, NB, ACCW])
        attend(nc, c, records, kv_rows, Wk, bk, Wq, bq)
        feed_forward(nc, c, wr, br, w1, b1, w2, b2, route_dram, out)


def order_edges(nc, c, x, src, dst, attrs, Wqkv, bqkv, records, kv_rows):
    with ExitStack() as ctx:
        def sb(name, shape, dt=F32):
            return ctx.enter_context(nc.sbuf_tensor(name, shape, dt))

        def sem(name):
            return ctx.enter_context(nc.semaphore(name))

        src_i = sb("src_i", [EP, EC], I32)
        dst_i = sb("dst_i", [EP, EC], I32)
        src_f = sb("src_f", [EP, EC])
        low_f = sb("low_f", [EP, EC])
        high_f = sb("high_f", [EP, EC])
        fix = sb("fix", [EP, EC])
        high_i = sb("high_i", [EP, EC], I32)
        attr_sb = sb("attr_sb", [EP, EC * ATTRS])
        table = sb("table", [BN, NB, EC + 1])
        total_i = sb("total_i", [BN, NB], I32)
        tiles_i = sb("tiles_i", [BN, NB], I32)
        tiles_f = sb("tiles_f", [BN, NB])
        tile_end = sb("tile_end", [BN, NB])
        tile_start = sb("tile_start", [BN, NB])
        base = sb("base", [BN, NB])
        tile_no_i = sb("tile_no_i", [GCOL, 4], I32)
        tile_no = sb("tile_no", [GCOL, 4])
        passed = sb("passed", [GCOL, 4, NB])
        bucket_col = sb("bucket_col", [GCOL, 4])
        iota_i = sb("iota_i", [128, 128], I32)
        iota_b = sb("iota_b", [128, 128], BF16)
        empty = sb("empty", [128, NT // 16, WIDE])
        bqkv_sb = sb("bqkv_sb", [BN, QKV])
        wqkv_sb = sb("wqkv_sb", [128, 2, QKV])

        ps = [ctx.enter_context(nc.psum_tensor(f"ps_a{i}", [128, 512], F32)) for i in range(8)]

        with ExitStack() as first:
            def sb1(name, shape, dt=F32):
                return first.enter_context(nc.sbuf_tensor(name, shape, dt))

            def sem1(name):
                return first.enter_context(nc.semaphore(name))

            low_hot = sb1("low_hot", [EP, 2, HALF, BN], BF16)
            high_hot = sb1("high_hot", [EP, 2, HALF, NB], BF16)
            edges_in = sem1("edges_in")
            nodes_in = sem1("nodes_in")
            prefilled = sem1("prefilled")
            made = sem1("made")
            digits = sem1("digits")
            hot_ready = sem1("hot_ready")
            counts_ready = sem1("counts_ready")
            table_filled = sem1("table_filled")
            summed = sem1("summed")
            totals_ready = sem1("totals_ready")
            layout_step = sem1("layout_step")
            buckets_ready = sem1("buckets_ready")
            block = first.enter_context(nc.Block())

            @block.sync
            def _(sp):
                sp.dma_start(src_i[:], src.rearrange("(p c) -> p c", c=EC)).then_inc(edges_in, 16)
                sp.dma_start(c["x"][:], x.rearrange("(b p) d -> p b d", p=BN)).then_inc(nodes_in, 16)
                sp.dma_start(dst_i[:], dst.rearrange("(p c) -> p c", c=EC)).then_inc(nodes_in, 16)
                sp.dma_start(attr_sb[:], attrs.rearrange("(p c) a -> p (c a)", c=EC)).then_inc(nodes_in, 16)
                sp.dma_start(wqkv_sb[:], Wqkv.rearrange("(k p) n -> p k n", p=128)).then_inc(nodes_in, 16)
                sp.dma_start(bqkv_sb[:], bqkv.rearrange("(a n) -> a n", a=1).broadcast_to([BN, QKV])).then_inc(nodes_in, 16)
                sp.wait_ge(made, 10)
                records_v = records.rearrange("(p a r) w -> a p (r w)", p=128, a=16)
                for a in range(16):
                    sp.dma_start(records_v[a], empty[:].rearrange("p r w -> p (r w)")).then_inc(prefilled, 16)
                sp.wait_ge(nodes_in, 16 * 5)
                sp.wait_ge(prefilled, 16 * 16)

            @block.gpsimd
            def _(pool):
                nc.gpsimd.iota(iota_i[:], pattern=[[1, 128]], base=0, channel_multiplier=0).then_inc(made, 1)
                nc.gpsimd.iota(tile_no_i[:], pattern=[[GCOL, 4]], base=0, channel_multiplier=1).then_inc(made, 1)
                nc.gpsimd.memset(c["ident"][:], 0.0).then_inc(made, 1)
                nc.gpsimd.memset(c["ones"][:], 1.0).then_inc(made, 1)
                pool.wait_ge(made, 4)
                nc.gpsimd.affine_select(out=c["ident"][:], in_=c["ident"][:], compare_op=ALU.not_equal, fill=1.0,
                                        base=0, pattern=[[-1, 128]], channel_multiplier=1).then_inc(made, 1)
                nc.gpsimd.affine_select(out=c["below"][:], in_=c["ones"][:], compare_op=ALU.is_gt, fill=0.0,
                                        base=0, pattern=[[-1, 128]], channel_multiplier=1).then_inc(made, 1)
                nc.gpsimd.affine_select(out=c["above"][:], in_=c["ones"][:], compare_op=ALU.is_gt, fill=0.0,
                                        base=0, pattern=[[1, 128]], channel_multiplier=-1).then_inc(made, 1)
                nc.gpsimd.memset(empty[:], 0.0).then_inc(made, 1)
                pool.wait_ge(made, 8)
                nc.gpsimd.memset(empty[:, :, SRC], -1.0).then_inc(made, 1)
                nc.gpsimd.memset(empty[:, :, LOW], -1.0).then_inc(made, 1)

            @block.vector
            def _(dve):
                dve.wait_ge(made, 2)
                nc.vector.tensor_copy(c["iota"][:], iota_i[:]).then_inc(digits, 1)
                nc.vector.tensor_copy(iota_b[:], iota_i[:]).then_inc(digits, 1)
                nc.vector.tensor_copy(tile_no[:], tile_no_i[:]).then_inc(digits, 1)
                nc.vector.memset(table[:, :, 0:1], 0.0).then_inc(digits, 1)
                dve.wait_ge(edges_in, 16)
                nc.vector.tensor_copy(src_f[:], src_i[:]).then_inc(digits, 1)
                dve.wait_ge(digits, 5)
                nc.vector.tensor_scalar(high_i[:], src_f[:], 1.0 / BN, None, ALU.mult).then_inc(digits, 1)
                dve.wait_ge(digits, 6)
                nc.vector.tensor_copy(high_f[:], high_i[:]).then_inc(digits, 1)
                dve.wait_ge(digits, 7)
                nc.vector.scalar_tensor_tensor(low_f[:], high_f[:], -float(BN), src_f[:], ALU.mult, ALU.add).then_inc(digits, 1)
                dve.wait_ge(digits, 8)
                nc.vector.tensor_scalar(fix[:], low_f[:], 0.0, None, ALU.is_lt).then_inc(digits, 1)
                dve.wait_ge(digits, 9)
                nc.vector.tensor_tensor(high_f[:], high_f[:], fix[:], ALU.subtract).then_inc(digits, 1)
                nc.vector.scalar_tensor_tensor(low_f[:], fix[:], float(BN), low_f[:], ALU.mult, ALU.add).then_inc(digits, 1)
                dve.wait_ge(digits, 11)
                nc.vector.tensor_scalar(fix[:], low_f[:], float(BN), None, ALU.is_ge).then_inc(digits, 1)
                dve.wait_ge(digits, 12)
                nc.vector.tensor_tensor(high_f[:], high_f[:], fix[:], ALU.add).then_inc(digits, 1)
                nc.vector.scalar_tensor_tensor(low_f[:], fix[:], -float(BN), low_f[:], ALU.mult, ALU.add).then_inc(digits, 1)
                dve.wait_ge(digits, 14)

                with dve.Fori(0, STEPS) as i:
                    for u in range(2):
                        col = bass.ds(i * (2 * HALF) + u * HALF, HALF)
                        dve.wait_ge(counts_ready, i * 2 + (u + 1))
                        nc.vector.tensor_tensor(low_hot[:, u], iota_b[0:EP, None, 0:BN].broadcast_to([EP, HALF, BN]),
                                                low_f[:, col].unsqueeze(2).broadcast_to([EP, HALF, BN]), ALU.is_equal)
                        nc.vector.tensor_tensor(high_hot[:, u], iota_b[0:EP, None, 0:NB].broadcast_to([EP, HALF, NB]),
                                                high_f[:, col].unsqueeze(2).broadcast_to([EP, HALF, NB]), ALU.is_equal).then_inc(hot_ready, 1)

                dve.wait_ge(table_filled, 2 + 2 * STEPS)
                for b in range(NB):
                    nc.vector.tensor_tensor_scan(table[:, b, 1:], table[:, b, 1:], table[:, b, 1:], 0.0, ALU.add, ALU.max).then_inc(summed, 1)

                dve.wait_ge(totals_ready, 2)
                nc.vector.tensor_scalar(total_i[:], ps[0][0:BN, 0:NB], float(TILE - 1), None, ALU.add).then_inc(layout_step, 1)
                dve.wait_ge(layout_step, 1)
                nc.vector.tensor_scalar(tiles_i[:], total_i[:], 7, None, ALU.logical_shift_right).then_inc(layout_step, 1)
                dve.wait_ge(layout_step, 2)
                nc.vector.tensor_copy(tiles_f[:], tiles_i[:]).then_inc(layout_step, 1)
                dve.wait_ge(layout_step, 3)
                nc.vector.tensor_tensor_scan(tile_end[:], tiles_f[:], tiles_f[:], 0.0, ALU.add, ALU.max).then_inc(layout_step, 1)
                dve.wait_ge(layout_step, 4)
                nc.vector.tensor_tensor(tile_start[:], tile_end[:], tiles_f[:], ALU.subtract).then_inc(layout_step, 1)
                nc.vector.tensor_tensor(passed[:], tile_end[0:GCOL, None, :].broadcast_to([GCOL, 4, NB]),
                                        tile_no[:].unsqueeze(2).broadcast_to([GCOL, 4, NB]), ALU.is_le).then_inc(layout_step, 1)
                dve.wait_ge(layout_step, 6)
                nc.vector.scalar_tensor_tensor(base[:], tile_start[:], float(TILE), ps[1][0:BN, 0:NB], ALU.mult, ALU.add).then_inc(layout_step, 1)
                nc.vector.tensor_reduce(bucket_col[:], passed[:], AX.X, ALU.add).then_inc(layout_step, 1)
                dve.wait_ge(layout_step, 8)
                nc.vector.tensor_scalar(bucket_col[:], bucket_col[:], float(NB - 1), None, ALU.min).then_inc(layout_step, 1)
                dve.wait_ge(buckets_ready, 1)
                nc.vector.tensor_copy(c["bucket_of_tile"][:], ps[2][0:1, 0:NT])

            @block.tensor
            def _(pe):
                pe.sem_inc(counts_ready, 2)
                with pe.Fori(0, STEPS) as i:
                    for u in range(2):
                        pe.wait_ge(hot_ready, i * 2 + (u + 1))
                        pe.wait_ge(table_filled, i * 2 + (u + 1))
                        for k in range(HALF):
                            last = nc.tensor.matmul(ps[u][0:BN, k * NB:(k + 1) * NB], low_hot[:, u, k], high_hot[:, u, k], start=True, stop=True)
                        last.then_inc(counts_ready, 1)
                pe.wait_ge(summed, NB)
                pe.wait_ge(made, 7)
                pe.wait_ge(table_filled, 2 + 2 * STEPS)
                nc.tensor.matmul(ps[0][0:BN, 0:NB], c["ones"][0:BN, 0:BN], table[:, :, EC], start=True, stop=True).then_inc(totals_ready, 1)
                nc.tensor.matmul(ps[1][0:BN, 0:NB], c["above"][0:BN, 0:BN], table[:, :, EC], start=True, stop=True).then_inc(totals_ready, 1)
                pe.wait_ge(layout_step, 9)
                for k in range(4):
                    last = nc.tensor.matmul(ps[2][0:1, k * GCOL:(k + 1) * GCOL], bucket_col[:, k:k + 1], c["ident"][0:GCOL, 0:GCOL], start=True, stop=True)
                last.then_inc(buckets_ready, 1)

            @block.scalar
            def _(act):
                act.sem_inc(table_filled, 2)
                with act.Fori(0, STEPS) as i:
                    for u in range(2):
                        act.wait_ge(counts_ready, i * 2 + (u + 3))
                        nc.scalar.activation(table[:, :, bass.ds(i * (2 * HALF) + (u * HALF + 1), HALF)],
                                             ps[u][0:BN, 0:HALF * NB].rearrange("p (k b) -> p b k", b=NB), ACT.Copy).then_inc(table_filled, 1)

        place_edges(nc, c, ps, src_f, low_f, high_f, dst_i, attr_sb, table, base, wqkv_sb, bqkv_sb, records, kv_rows)


def place_edges(nc, c, ps, src_f, low_f, high_f, dst_i, attr_sb, table, base, wqkv_sb, bqkv_sb, records, kv_rows):
    with ExitStack() as ctx:
        def sb(name, shape, dt=F32):
            return ctx.enter_context(nc.sbuf_tensor(name, shape, dt))

        def sem(name):
            return ctx.enter_context(nc.semaphore(name))

        low_hot = sb("low_hot_f", [EP, 2, HALF, BN])
        low_rows = sb("low_rows", [BN, 2, HALF, EP])
        src_diag = sb("src_diag", [EP, 2, HALF, EP])
        high_hot = sb("high_hot_f", [EP, HALF, NB])
        same_before = sb("same_before", [EP, HALF, EP])
        rank = sb("rank", [EP, HALF])
        picked = sb("picked", [EP, HALF, NB])
        offset = sb("offset", [EP, HALF])
        slot = sb("slot", [EP, 2, HALF], I32)
        record = sb("record", [EP, 2, HALF, WIDE])
        stats = sb("stats", [BN, 6])
        mean_var = sb("mean_var", [BN, 2])
        spread = sb("spread", [BN, 3])
        normed = sb("normed", [BN, DIM])
        normed_t = sb("normed_t", [128, 2, BN])
        kv_out = sb("kv_out", [BN, KV])
        bq_scaled = sb("bq_scaled", [BN, QK])

        low_onehot = sem("low_onehot")
        diag_ready = sem("diag_ready")
        low_transposed = sem("low_transposed")
        low_rows_ready = sem("low_rows_ready")
        src_rows_ready = sem("src_rows_ready")
        ranks_ready = sem("ranks_ready")
        high_ready = sem("high_ready")
        looked_up = sem("looked_up")
        picked_ready = sem("picked_ready")
        offset_ready = sem("offset_ready")
        slots_ready = sem("slots_ready")
        records_built = sem("records_built")
        scattered = [sem(f"scattered{u}") for u in range(2)]
        ln_step = sem("ln_step")
        root_ready = sem("root_ready")
        normed_ready = sem("normed_ready")
        node_transposed = sem("node_transposed")
        normed_rows = sem("normed_rows")
        qkv_ready = sem("qkv_ready")
        q_ready = sem("q_ready")
        kv_ready = sem("kv_ready")
        kv_stored = sem("kv_stored")
        bias_ready = sem("bias_ready")
        ones_set = sem("ones_set")
        records_free = sem("records_free")
        kv_out_free = sem("kv_out_free")
        scatters_begun = sem("scatters_begun")
        block = ctx.enter_context(nc.Block())
        T0, S0, L0, X0, W0 = ps[0:2], ps[2:4], ps[4], ps[5], ps[6]

        @block.sync
        def _(sp):
            with sp.Fori(0, STEPS) as i:
                sp.wait_ge(scattered[0], (i + 1) * (16 * HALF))
                sp.sem_inc(records_free, 1)
                sp.wait_ge(kv_ready, i + 1)
                sp.dma_start(kv_rows[bass.ds(i * BN, BN), :], kv_out[:]).then_inc(kv_stored, 16)
                sp.wait_ge(scattered[1], (i + 1) * (16 * HALF))
                sp.sem_inc(records_free, 1)
                sp.wait_ge(kv_stored, (i + 1) * 16)
                sp.sem_inc(kv_out_free, 1)

        @block.gpsimd
        def _(pool):
            nc.gpsimd.memset(record[:, :, :, ONE], 1.0).then_inc(ones_set, 1)
            with pool.Fori(0, STEPS) as i:
                for u in range(2):
                    pool.wait_ge(records_built, i * 2 + (u + 1))
                    pool.wait_ge(slots_ready, i * 2 + (u + 1))
                    pool.sem_inc(scatters_begun, 1)
                    for k in range(HALF):
                        nc.gpsimd.indirect_dma_start(
                            out=records, out_offset=bass.IndirectOffsetOnAxis(ap=slot[:, u, k:k + 1], axis=0),
                            in_=record[:, u, k, :], in_offset=None).then_inc(scattered[u], 16)
            for u in range(2):
                pool.wait_ge(scattered[u], 16 * HALF * STEPS)

        def halves(eng, half):
            half(0, 0, True)
            half(0, 1, True)
            with eng.Fori(0, STEPS - 2) as t:
                for u in range(2):
                    half(t + 1, u, True)
            half(STEPS - 1, 0, True)
            half(STEPS - 1, 1, False)

        def columns(n):
            return bass.ds(n * HALF, HALF)

        @block.scalar
        def _(act):
            act.sem_inc(low_rows_ready, 1)
            act.wait_ge(ones_set, 1)

            def copy_low_rows(n, u):
                act.wait_ge(low_transposed, n + 3)
                act.wait_ge(looked_up, n + 1)
                for h in range(2):
                    last = act.activation(low_rows[:, u, h * 4:h * 4 + 4, :].rearrange("p a b -> p (a b)"), T0[h][0:BN, 0:4 * EP], ACT.Copy)
                last.then_inc(low_rows_ready, 1)

            def half(i, u, more):
                n = i * 2 + u
                act.wait_ge(records_free, n + 1)
                act.activation(record[:, u, :, 0:ATTRS], attr_sb[:, bass.ds(n * (HALF * ATTRS), HALF * ATTRS)].rearrange("p (k a) -> p k a", a=ATTRS), ACT.Copy)
                act.activation(record[:, u, :, SRC], src_f[:, columns(n)], ACT.Copy)
                act.activation(record[:, u, :, LOW], low_f[:, columns(n)], ACT.Copy)
                act.activation(record[:, u, :, DST].bitcast(I32), dst_i[:, columns(n)], ACT.Copy).then_inc(records_built, 1)
                if u == 1:
                    act.wait_ge(node_transposed, i + 1)
                    act.activation(normed_t[:].rearrange("p a b -> p (a b)"), X0[:, 0:2 * BN], ACT.Copy).then_inc(normed_rows, 1)
                if more:
                    copy_low_rows(n + 1, 1 - u)
                if u == 0:
                    act.wait_ge(ln_step, (i + 1) * 3)
                    act.activation(spread[:, 1:2], spread[:, 0:1], ACT.Sqrt).then_inc(root_ready, 1)

            copy_low_rows(0, 0)
            halves(act, half)

        @block.vector
        def _(dve):
            dve.sem_inc(ranks_ready, 1)
            dve.sem_inc(picked_ready, 1)
            nc.vector.tensor_scalar(bq_scaled[:], bqkv_sb[:, 0:QK], SCALE, None, ALU.mult).then_inc(bias_ready, 1)
            dve.wait_ge(bias_ready, 1)

            def add_bias(i):
                dve.wait_ge(qkv_ready, i + 1)
                nc.vector.scalar_tensor_tensor(c["q"][:, bass.ds(i, 1), :].rearrange("p a d -> p (a d)"), W0[0:BN, 0:QK], SCALE,
                                               bq_scaled[:], ALU.mult, ALU.add)
                dve.wait_ge(kv_out_free, i + 1)
                nc.vector.tensor_tensor(kv_out[:], W0[0:BN, QK:QKV], bqkv_sb[:, QK:QKV], ALU.add).then_inc(kv_ready, 1)

            def one_hot_rows(n, u):
                dve.wait_ge(low_transposed, n + 1)
                nc.vector.tensor_tensor(low_hot[:, u], c["iota"][0:EP, None, 0:BN].broadcast_to([EP, HALF, BN]),
                                        low_f[:, columns(n)].unsqueeze(2).broadcast_to([EP, HALF, BN]), ALU.is_equal).then_inc(low_onehot, 1)
                dve.wait_ge(src_rows_ready, n + 1)
                nc.vector.tensor_tensor(src_diag[:, u], c["ident"][0:EP, None, 0:EP].broadcast_to([EP, HALF, EP]),
                                        src_f[:, columns(n)].unsqueeze(2).broadcast_to([EP, HALF, EP]), ALU.mult).then_inc(diag_ready, 1)

            def half(i, u, more):
                n = i * 2 + u
                if u == 1:
                    dve.wait_ge(root_ready, i + 1)
                    nc.vector.reciprocal(spread[:, 2:3], spread[:, 1:2]).then_inc(bias_ready, 1)
                    dve.wait_ge(bias_ready, i + 2)
                    nc.vector.tensor_scalar(normed[:], c["x"][:, bass.ds(i, 1), :].rearrange("p a d -> p (a d)"),
                                            mean_var[:, 0:1], spread[:, 2:3], ALU.subtract, ALU.mult).then_inc(normed_ready, 1)
                if more:
                    one_hot_rows(n + 1, 1 - u)
                if u == 0:
                    nc.vector.bn_stats(stats[:], c["x"][:, bass.ds(i, 1), :].rearrange("p a d -> p (a d)")).then_inc(ln_step, 1)
                    dve.wait_ge(ln_step, i * 3 + 1)
                nc.vector.tensor_tensor(high_hot[:], c["iota"][0:EP, None, 0:NB].broadcast_to([EP, HALF, NB]),
                                        high_f[:, columns(n)].unsqueeze(2).broadcast_to([EP, HALF, NB]), ALU.is_equal).then_inc(high_ready, 1)
                if u == 0:
                    nc.vector.bn_aggr(mean_var[:], stats[:]).then_inc(ln_step, 1)
                    dve.wait_ge(ln_step, i * 3 + 2)
                    nc.vector.tensor_scalar(spread[:, 0:1], mean_var[:, 1:2], EPS_LN, None, ALU.add).then_inc(ln_step, 1)
                dve.wait_ge(src_rows_ready, n + 3)
                for k in range(HALF):
                    last = nc.vector.scalar_tensor_tensor(
                        same_before[:, k], S0[k // 4][0:EP, (k % 4) * EP:(k % 4 + 1) * EP],
                        src_f[:, bass.ds(n * HALF + k, 1)], c["below"][0:EP, 0:EP],
                        ALU.is_equal, ALU.mult, accum_out=rank[:, k:k + 1])
                last.then_inc(ranks_ready, 1)
                dve.wait_ge(looked_up, n + 3)
                dve.wait_ge(high_ready, n + 1)
                nc.vector.tensor_tensor(picked[:], L0[0:EP, 0:HALF * NB].rearrange("p (k b) -> p k b", b=NB), high_hot[:], ALU.mult).then_inc(picked_ready, 1)
                dve.wait_ge(picked_ready, n + 2)
                nc.vector.tensor_reduce(offset[:], picked[:], AX.X, ALU.add).then_inc(offset_ready, 1)
                dve.wait_ge(offset_ready, n + 1)
                dve.wait_ge(ranks_ready, n + 2)
                dve.wait_ge(records_free, n + 1)
                nc.vector.tensor_tensor(slot[:, u], offset[:], rank[:], ALU.add).then_inc(slots_ready, 1)
                if u == 0 and (not isinstance(i, int) or i > 0):
                    add_bias(i - 1)

            one_hot_rows(0, 0)
            halves(dve, half)
            add_bias(STEPS - 1)

        @block.tensor
        def _(pe):
            pe.sem_inc(low_transposed, 2)
            pe.sem_inc(src_rows_ready, 2)
            pe.sem_inc(looked_up, 2)
            pe.sem_inc(records_free, 2)
            pe.sem_inc(kv_out_free, 1)

            def transpose_low(n, u):
                pe.wait_ge(low_onehot, n + 1)
                pe.wait_ge(low_rows_ready, n + 1)
                for k in range(HALF):
                    last = nc.tensor.transpose(T0[k // 4][0:BN, (k % 4) * EP:(k % 4 + 1) * EP], low_hot[:, u, k], c["ident"][0:EP, 0:EP])
                last.then_inc(low_transposed, 1)

            def spread_sources(n, u):
                pe.wait_ge(diag_ready, n + 1)
                pe.wait_ge(ranks_ready, n + 1)
                for h in range(2):
                    last = nc.tensor.matmul(S0[h][0:EP, 0:4 * EP], c["ones"][0:EP, 0:EP],
                                            src_diag[:, u, h * 4:h * 4 + 4, :].rearrange("p a b -> p (a b)"), start=True, stop=True)
                last.then_inc(src_rows_ready, 1)

            def half(i, u, more):
                n = i * 2 + u
                pe.wait_ge(low_rows_ready, n + 2)
                pe.wait_ge(picked_ready, n + 1)
                for k in range(HALF):
                    before = table[:, :, bass.ds(n * HALF + k, 1)].rearrange("p b a -> p (b a)")
                    nc.tensor.matmul(L0[0:EP, k * NB:(k + 1) * NB], low_rows[:, u, k], before, start=True, stop=False)
                    last = nc.tensor.matmul(L0[0:EP, k * NB:(k + 1) * NB], low_rows[:, u, k], base[:], start=False, stop=True)
                last.then_inc(looked_up, 1)
                if u == 1:
                    pe.wait_ge(normed_ready, i + 1)
                    for h in range(2):
                        last = nc.tensor.transpose(X0[:, h * BN:(h + 1) * BN], normed[:, h * 128:(h + 1) * 128], c["ident"][0:BN, 0:BN])
                    last.then_inc(node_transposed, 1)
                if more:
                    transpose_low(n + 1, 1 - u)
                if more:
                    spread_sources(n + 1, 1 - u)
                if u == 1:
                    pe.wait_ge(normed_rows, i + 1)
                    for h in range(2):
                        last = nc.tensor.matmul(W0[0:BN, :], normed_t[:, h, :], wqkv_sb[:, h, :], start=(h == 0), stop=(h == 1))
                    last.then_inc(qkv_ready, 1)

            transpose_low(0, 0)
            spread_sources(0, 0)
            halves(pe, half)


def attend(nc, c, records, kv_rows, Wk, bk, Wq, bq):
    with ExitStack() as ctx:
        def sb(name, shape, dt=F32):
            return ctx.enter_context(nc.sbuf_tensor(name, shape, dt))

        def ps(name):
            return ctx.enter_context(nc.psum_tensor(name, [128, 512], F32))

        def sem(name):
            return ctx.enter_context(nc.semaphore(name))

        iota, ident, ones, acc = c["iota"], c["ident"], c["ones"], c["acc"]
        gt = c["bucket_of_tile"]
        K = ATTRS + 1
        rec = sb("rec", [128, 2, SC, WIDE])
        kv = sb("kv", [128, 2, SC, KV])
        onehot = sb("onehot", [128, 2, SC, BN])
        distance = sb("distance", [128, BATCH, BN])
        ATTR_PARTS, WEIGHT_PARTS = (0, 0, 0, 1, 1, 2), (0, 1, 2, 0, 1, 0)
        PAIRS = len(ATTR_PARTS)
        KS = PAIRS * K
        wrpe = sb("wrpe", [K, 2, QK])
        wrest = sb("wrest", [K, 2, 2, QK])
        wparts = sb("wparts", [K, 3, 2, QK], BF16)
        wstack = sb("wstack", [KS, 2, QK], BF16)
        ident_b = sb("ident_b", [128, 128], BF16)
        parts = sb("attr_parts", [128, 2, SC, PAIRS, K], BF16)
        arest = sb("attr_rest", [128, 2, SC, K])
        attr_rows = sb("attr_rows", [KS, 2, BATCH * 128], BF16)
        node_rows = sb("node_rows", [BN, 2, BATCH * 128])
        keys = sb("keys", [128, 2, BATCH * QK])
        product = sb("product", [128, BATCH * QK])
        score = sb("score", [128, 2, PT, PARTS, HEADS])
        src_wide = sb("src_wide", [128, PT, PARTS, HEADS])
        W = PT * 128
        cs = sb("score_src_rows", [128, 2 * W])
        changes = sb("changes", [128, W + 1])
        run = sb("run", [128, 4, W])
        edges = sb("edge_rows", [1, 2, 2, HEADS, PARTS + 1])
        gap = sb("gap", [1, HEADS, PARTS + 1])
        split = sb("split", [1, HEADS, PARTS + 1])
        pen_f = sb("pen_f", [1, HEADS, PARTS + 1])
        pen_b = sb("pen_b", [1, HEADS, PARTS + 1])
        chain_f = sb("chain_f", [1, HEADS, PARTS + 1])
        chain_b = sb("chain_b", [1, HEADS, PARTS + 1])
        carry_rows = sb("carry_rows", [1, 2, PARTS, HEADS])
        carry = sb("carry", [128, 2])
        shifted = sb("shifted", [128, W + 1])
        weight_rows = sb("weight_rows", [128, W + 1])
        factor = sb("factor", [HEADS, HEADS])
        first_node = sb("first_node", [BN, 2])
        rescale = sb("rescale", [BN, HEADS])
        weights = sb("weights", [128, SC, HEADS])
        weighted = sb("weighted", [128, 2, BATCH, HEADS, VD])

        P_rows, P_q, P_k, P_max = ps("ps_rows"), ps("ps_q"), ps("ps_k"), ps("ps_max")
        P_parts = P_rows[0:KS, 0:BATCH * 64].bitcast(BF16)
        P_z = [ps(f"ps_z{k}") for k in range(BATCH)]

        weights_in = sem("weights_in")
        wpart_step = sem("wpart_step")
        weights_spread = sem("weights_spread")
        ident_ready = sem("ident_ready")
        part_ready = sem("part_ready")
        rest_ready = sem("rest_ready")
        cleared = sem("cleared")
        records_in = [sem(f"records_in{i}") for i in range(2)]
        records_free = sem("records_free2")
        indices_seen = sem("indices_seen")
        kv_in = [sem(f"kv_in{i}") for i in range(2 * NBATCH)]
        distance_ready = sem("distance_ready")
        onehot_ready = sem("onehot_ready")
        attr_transposed = sem("attr_transposed")
        attr_rows_ready = sem("attr_rows_ready")
        node_transposed = sem("node_transposed2")
        node_rows_ready = sem("node_rows_ready")
        k_ready = sem("k_ready")
        q_ready = sem("q_ready2")
        keys_ready = sem("keys_ready")
        product_ready = sem("product_ready")
        score_ready = sem("score_ready")
        src_wide_ready = sem("src_wide_ready")
        rows_transposed = sem("rows_transposed")
        rows_ready = sem("rows_ready")
        max_step = sem("max_step")
        end_sources_transposed = sem("end_sources_transposed")
        end_sources_ready = sem("end_sources_ready")
        ends_transposed = sem("ends_transposed")
        ends_ready = sem("ends_ready")
        carry_transposed = sem("carry_transposed")
        carry_seen = sem("carry_seen")
        shifted_ready = sem("shifted_ready")
        exp_ready = sem("exp_ready")
        weights_transposed = sem("weights_transposed")
        weights_ready = sem("weights_ready")
        factor_spread = sem("factor_spread")
        rescaled = sem("rescaled")
        acc_rescaled = sem("acc_rescaled")
        den_ready = sem("den_ready")
        weighted_ready = sem("weighted_ready")
        sums_ready = sem("sums_ready")
        added = sem("added")
        MAX_STEPS = 19

        block = ctx.enter_context(nc.Block())

        ADD_LAG, SUM_LAG, WEIGH_LAG = 7, 6, 5
        TOTAL = NSC * NBATCH

        def batch(n, p, b, d):
            return n * NBATCH + (b + d), n + (b + d) // NBATCH, (p + (b + d) // NBATCH) % 2, (b + d) % NBATCH

        def exists(number, total=TOTAL):
            return not isinstance(number, int) or 0 <= number < total

        def all_steps(eng, step):
            for b in range(2, NBATCH):
                step(-1, 1, b)
            for n in range(2):
                for b in range(NBATCH):
                    step(n, n % 2, b)
            with eng.Fori(0, (NSC - 4) // 2) as it:
                for u in range(2):
                    for b in range(NBATCH):
                        step(it * 2 + (u + 2), u, b)
            for s in range((NSC - 2) * NBATCH, TOTAL + ADD_LAG):
                step(s // NBATCH, s // NBATCH % 2, s % NBATCH)

        def buckets(engine, first_tile, count):
            _, regs = nc.values_load_multi_w_load_instructions(
                gt[0:1, bass.ds(first_tile, count)], engines=[engine], min_val=0, max_val=NB - 1,
                skip_runtime_bounds_check_because="counted from 0 and clamped to NB - 1 where it is made")
            return regs

        @block.sync
        def _(sp):
            records_v = records.rearrange("(n t p) w -> n p t w", t=SC, p=128)
            with sp.Fori(0, NSC // 2) as it:
                for u in range(2):
                    n = it * 2 + u
                    sp.wait_ge(score_ready, n * NBATCH + 1)
                    sp.sem_inc(records_free, 1)
                    sp.wait_ge(src_wide_ready, n + 1)
                    sp.sem_inc(records_free, 1)
                    sp.dma_start(rec[:, u], records_v[bass.ds(n, 1)].rearrange("a p t w -> p (a t) w")).then_inc(records_in[u], 16)

        @block.gpsimd
        def _(pool):
            nc.gpsimd.memset(changes[:], 0.0).then_inc(cleared, 1)
            nc.gpsimd.memset(edges[:], -BIG).then_inc(cleared, 1)
            nc.gpsimd.memset(gap[:], -BIG).then_inc(cleared, 1)
            nc.gpsimd.memset(pen_f[:], -BIG).then_inc(cleared, 1)
            nc.gpsimd.memset(pen_b[:], -BIG).then_inc(cleared, 1)
            nc.gpsimd.memset(shifted[:], 0.0).then_inc(cleared, 1)
            with pool.Fori(0, NSC // 2) as it:
                for u in range(2):
                    n = it * 2 + u
                    pool.wait_ge(records_in[u], it * 16 + 16)
                    pool.sem_inc(indices_seen, 1)
                    pool.wait_ge(part_ready, n * 3 + 1)
                    nc.gpsimd.tensor_tensor(arest[:, 0], rec[:, u, :, 0:K], parts[:, u, :, 0, :], ALU.subtract).then_inc(rest_ready, 1)
                    pool.wait_ge(part_ready, n * 3 + 2)
                    pool.wait_ge(rest_ready, n * 2 + 1)
                    nc.gpsimd.tensor_tensor(arest[:, 1], arest[:, 0], parts[:, u, :, 3, :], ALU.subtract).then_inc(rest_ready, 1)
                    for b in range(NBATCH):
                        pool.wait_ge(weighted_ready, n * NBATCH + (b + 1))
                        pool.sem_inc(indices_seen, 1)
                        for t in range(b * BATCH, (b + 1) * BATCH):
                            nc.gpsimd.indirect_dma_start(
                                out=kv[:, u, t, :], out_offset=None, in_=kv_rows,
                                in_offset=bass.IndirectOffsetOnAxis(ap=rec[:, u, t, DST:DST + 1].bitcast(I32), axis=0)
                            ).then_inc(kv_in[u * NBATCH + b], 16)

        @block.scalar
        def _(act):
            act.dma_start(wrpe[0:ATTRS, 0, :], Wq).then_inc(weights_in, 16)
            act.dma_start(wrpe[ATTRS:K, 0, :], bq.rearrange("(a n) -> a n", a=1)).then_inc(weights_in, 16)
            act.dma_start(wrpe[0:ATTRS, 1, :], Wk).then_inc(weights_in, 16)
            act.dma_start(wrpe[ATTRS:K, 1, :], bk.rearrange("(a n) -> a n", a=1)).then_inc(weights_in, 16)
            act.sem_inc(attr_rows_ready, 1)
            act.sem_inc(node_rows_ready, 2)
            act.sem_inc(keys_ready, 1)
            act.sem_inc(src_wide_ready, 2)
            act.sem_inc(exp_ready, 1)
            act.sem_inc(den_ready, 1)

            nc.scalar.activation(ident_b[:], ident[:], ACT.Copy).then_inc(ident_ready, 1)

            def attr_part(g, pg, part):
                first, count = ATTR_PARTS.index(part), ATTR_PARTS.count(part)
                if part == 0:
                    act.wait_ge(records_in[pg], (g - pg) * 8 + 16)
                    source = rec[:, pg, :, 0:K]
                else:
                    act.wait_ge(rest_ready, g * 2 + part)
                    source = arest[:, part - 1]
                nc.scalar.activation(parts[:, pg, :, first:first + count, :], source.unsqueeze(2).broadcast_to([128, SC, count, K]), ACT.Copy).then_inc(part_ready, 1)

            for part in range(3):
                attr_part(0, 0, part)
            act.wait_ge(wpart_step, 5)
            for j, part in enumerate(WEIGHT_PARTS):
                act.dma_start(wstack[j * K:(j + 1) * K], wparts[:, part]).then_inc(weights_spread, 16)

            def step(n, p, b):
                m = n - 1
                B, g, pg, bb = batch(n, p, b, 1)
                if exists(B):
                    act.wait_ge(records_in[pg], (g - pg) * 8 + 16)
                    act.wait_ge(sums_ready, B * BATCH + BATCH)
                    for t in range(BATCH):
                        last = nc.scalar.activation(distance[:, t], iota[:, 0:BN], ACT.Abs, scale=-1.0, bias=rec[:, pg, bb * BATCH + t, LOW:LOW + 1])
                    last.then_inc(distance_ready, 1)
                    act.wait_ge(distance_ready, B + 1)
                    nc.scalar.activation(onehot[:, pg, bb * BATCH:(bb + 1) * BATCH], distance[:], ACT.Relu, scale=-1.0, bias=ones[:, 0:1]).then_inc(onehot_ready, 1)
                if b == 1 and exists(n + 1, NSC):
                    attr_part(n + 1, 1 - p, 0)
                if b == 0 and exists(m, NSC):
                    act.wait_ge(rows_transposed, m + 3)
                    act.wait_ge(shifted_ready, m + 1)
                    nc.scalar.activation(cs[:], P_max[:], ACT.Copy).then_inc(rows_ready, 1)
                B, g, pg, bb = batch(n, p, b, 2)
                if exists(B):
                    act.wait_ge(attr_transposed, B + 1)
                    act.wait_ge(q_ready, B + 1)
                    nc.scalar.activation(attr_rows[:, bb % 2], P_parts[:], ACT.Copy).then_inc(attr_rows_ready, 1)
                B, g, pg, bb = batch(n, p, b, 1)
                if exists(B):
                    act.wait_ge(k_ready, B + 1)
                    if not isinstance(B, int) or B > 0:
                        act.wait_ge(product_ready, B)
                    nc.scalar.activation(keys[:, bb % 2], P_k[:], ACT.Copy).then_inc(keys_ready, 1)
                    act.wait_ge(node_transposed, B + 1)
                    act.wait_ge(q_ready, B + 1)
                    if bb == 0:
                        act.wait_ge(rescaled, g + 1)
                        nc.scalar.activation(first_node[:, pg:pg + 1], P_rows[0:BN, 0:1], ACT.Copy)
                    nc.scalar.activation(node_rows[:, bb % 2], P_rows[0:BN, :], ACT.Copy).then_inc(node_rows_ready, 1)
                if b == 0 and exists(m, NSC):
                    r = P_max[0:1, :].rearrange("a (e j k h) -> a e j h k", e=2, j=2, h=HEADS)
                    act.wait_ge(end_sources_transposed, m + 1)
                    act.activation(edges[:, 0, 1, :, 0:PARTS], r[:, 0, 1], ACT.Copy)
                    act.activation(edges[:, 1, 1, :, 1:PARTS + 1], r[:, 1, 1], ACT.Copy).then_inc(end_sources_ready, 1)
                    act.wait_ge(ends_transposed, m + 1)
                    act.activation(edges[:, 0, 0, :, 0:PARTS], r[:, 0, 0], ACT.Copy)
                    act.activation(edges[:, 1, 0, :, 1:PARTS + 1], r[:, 1, 0], ACT.Copy).then_inc(ends_ready, 1)
                if b == 1 and exists(n + 1, NSC):
                    attr_part(n + 1, 1 - p, 1)
                if b == 1 and exists(m, NSC):
                    act.wait_ge(shifted_ready, m + 2)
                    act.wait_ge(weights_transposed, m + 1)
                    act.wait_ge(rescaled, m + 2)
                    nc.scalar.activation(weight_rows[:], shifted[:], ACT.Exp).then_inc(exp_ready, 1)
                    act.wait_ge(weights_transposed, m + 2)
                    act.wait_ge(weighted_ready, m * NBATCH + 2 * NBATCH)
                    act.wait_ge(den_ready, m * NBATCH + 1)
                    nc.scalar.activation(weights[:].rearrange("p (k i) h -> p k i h", i=PT),
                                         P_max[:, 0:W].rearrange("p (i k h) -> p k i h", i=PT, k=PARTS), ACT.Copy).then_inc(weights_ready, 1)
                if b == 2 and exists(n, NSC):
                    act.wait_ge(records_in[p], (n - p) * 8 + 16)
                    act.wait_ge(rows_transposed, n + 2)
                    nc.scalar.activation(src_wide[:].rearrange("p i k h -> p k i h"),
                                         rec[:, p, :, SRC:SRC + 1].rearrange("p (k i) a -> p k i a", i=PT).broadcast_to([128, PARTS, PT, HEADS]),
                                         ACT.Copy).then_inc(src_wide_ready, 1)
                if b == 1 and exists(n + 1, NSC):
                    attr_part(n + 1, 1 - p, 2)
                B, g, pg, bb = batch(n, p, b, -WEIGH_LAG)
                if exists(B):
                    act.wait_ge(weights_ready, g + 1)
                    act.wait_ge(sums_ready, B * BATCH + (2 * SC - BATCH))
                    nc.scalar.activation(weighted[:, bb % 2, :, :, HEAD_V], weights[:, bb * BATCH:(bb + 1) * BATCH, :], ACT.Copy).then_inc(den_ready, 1)

            all_steps(act, step)

        @block.vector
        def _(dve):
            dve.sem_inc(product_ready, 1)
            dve.sem_inc(score_ready, NBATCH + 1)
            dve.sem_inc(shifted_ready, 1)
            dve.sem_inc(weighted_ready, 2 * NBATCH)
            dve.sem_inc(rescaled, 2)
            nc.vector.memset(acc[:], 0.0).then_inc(added, BATCH)
            dve.wait_ge(cleared, 6)
            dve.wait_ge(weights_in, 64)
            left = wrpe[:]
            for part in range(3):
                if part:
                    dve.wait_ge(wpart_step, 2 * part - 1)
                    nc.vector.tensor_tensor(wrest[:, part - 1], left, wparts[:, part - 1], ALU.subtract).then_inc(wpart_step, 1)
                    left = wrest[:, part - 1]
                    dve.wait_ge(wpart_step, 2 * part)
                nc.vector.tensor_copy(wparts[:, part], left).then_inc(wpart_step, 1)
            scores, sources = cs[:, 0:W], cs[:, W:2 * W]
            first_src, last_src = edges[:, 0, 1, :, 0:PARTS], edges[:, 1, 1, :, :]

            def counted(ins):
                ins.then_inc(max_step, 1)

            def after(m, k):
                dve.wait_ge(max_step, m * MAX_STEPS + k)

            def mark_changes(m):
                dve.wait_ge(rows_ready, m + 1)
                counted(nc.vector.tensor_tensor(changes[:, 1:W], sources[:, 1:W], sources[:, 0:W - 1], ALU.not_equal))

            def scale_changes(m):
                after(m, 1)
                counted(nc.vector.tensor_scalar(changes[:, 1:W], changes[:, 1:W], -BIG, None, ALU.mult))

            def scan_forward(m):
                after(m, 2)
                counted(nc.vector.tensor_tensor_scan(run[:, 0], changes[:, 0:W], scores, -BIG, ALU.add, ALU.max))

            def scan_backward(m):
                after(m, 3)
                counted(nc.vector.tensor_tensor_scan(run[:, 1, ::-1], changes[:, W:0:-1], run[:, 0, ::-1], -BIG, ALU.add, ALU.max))

            def flat(a):
                return a.rearrange("a h k -> a (h k)")

            def gaps(m):
                dve.wait_ge(end_sources_ready, m + 1)
                counted(nc.vector.tensor_tensor(gap[:, :, 0:PARTS], first_src, last_src[:, :, 0:PARTS], ALU.not_equal))
                counted(nc.vector.tensor_tensor(split[:, :, 0:PARTS], first_src, last_src[:, :, 1:PARTS + 1], ALU.not_equal))
                after(m, 5)
                counted(nc.vector.tensor_scalar(gap[:, :, 0:PARTS], gap[:, :, 0:PARTS], -BIG, None, ALU.mult))

            def penalties(m):
                after(m, 7)
                counted(nc.vector.scalar_tensor_tensor(pen_f[:, :, 1:PARTS + 1], split[:, :, 0:PARTS], -BIG, gap[:, :, 0:PARTS], ALU.mult, ALU.min))
                counted(nc.vector.scalar_tensor_tensor(pen_b[:, :, 0:PARTS], split[:, :, 0:PARTS], -BIG, gap[:, :, 1:PARTS + 1], ALU.mult, ALU.min))

            def carries(m):
                dve.wait_ge(ends_ready, m + 1)
                after(m, 9)
                counted(nc.vector.tensor_tensor_scan(flat(chain_f[:]), flat(pen_f[:]), flat(edges[:, 1, 0]), -BIG, ALU.add, ALU.max))
                counted(nc.vector.tensor_tensor_scan(flat(chain_b[:])[:, ::-1], flat(pen_b[:])[:, ::-1], flat(edges[:, 0, 0])[:, ::-1], -BIG, ALU.add, ALU.max))
                after(m, 11)
                counted(nc.vector.tensor_tensor(carry_rows[:, 0].rearrange("a k h -> a h k"), chain_f[:, :, 0:PARTS], gap[:, :, 0:PARTS], ALU.add))
                counted(nc.vector.tensor_tensor(carry_rows[:, 1].rearrange("a k h -> a h k"), chain_b[:, :, 1:PARTS + 1], gap[:, :, 1:PARTS + 1], ALU.add))
                counted(nc.vector.tensor_copy(edges[:, 1, 0, :, 0], chain_f[:, :, PARTS]))
                counted(nc.vector.tensor_copy(edges[:, 1, 1, :, 0], edges[:, 1, 1, :, PARTS]))

            def full_maxima(m):
                dve.wait_ge(carry_transposed, m + 1)
                counted(nc.vector.tensor_copy(carry[:], P_max[:, W:W + 2]))
                after(m, 16)
                counted(nc.vector.tensor_tensor_scan(run[:, 2], changes[:, 0:W], scores, carry[:, 0:1], ALU.add, ALU.max))
                after(m, 17)
                counted(nc.vector.tensor_tensor_scan(run[:, 3, ::-1], changes[:, W:0:-1], run[:, 2, ::-1], carry[:, 1:2], ALU.add, ALU.max))
                after(m, 18)
                dve.wait_ge(exp_ready, m + 1)
                nc.vector.tensor_tensor(shifted[:, 0:W], scores, run[:, 3], ALU.subtract)
                nc.vector.tensor_tensor(shifted[0:HEADS, W:W + 1], carry[0:HEADS, 0:1], run[0:HEADS, 3, 0:1], ALU.subtract).then_inc(shifted_ready, 1)

            def factors(m):
                dve.wait_ge(exp_ready, m + 2)
                counted(nc.vector.scalar_tensor_tensor(factor[:], ident[0:HEADS, 0:HEADS], weight_rows[0:HEADS, W:W + 1], ident[0:HEADS, 0:HEADS], ALU.mult, ALU.subtract))

            def rescale_carried(m, p):
                dve.wait_ge(factor_spread, m + 1)
                nc.vector.tensor_scalar(rescale[:], P_max[0:BN, 0:HEADS], first_node[:, p:p + 1], 1.0, ALU.mult, ALU.add).then_inc(rescaled, 1)
                g = buckets(DVE_ENGINE, m * SC, 1)[0]
                a = acc[:, bass.ds(g, 1), :].rearrange("p a (h d) -> p (a h) d", d=VD)
                dve.wait_ge(rescaled, m + 3)
                dve.wait_ge(added, m * SC + BATCH)
                nc.vector.tensor_tensor(a, a, rescale[:].unsqueeze(2).broadcast_to([BN, HEADS, VD]), ALU.mult).then_inc(acc_rescaled, 1)

            def step(n, p, b):
                m = n - 1
                B, g, pg, bb = batch(n, p, b, 0)
                Z, gz, pz, bz = batch(n, p, b, -ADD_LAG)
                V, gv, pv, bv = batch(n, p, b, -WEIGH_LAG)
                maxima = exists(m, NSC)

                def add_sums(k):
                    if exists(Z):
                        a = acc[:, bass.ds(regs[k], 1), :].rearrange("p a d -> p (a d)")
                        dve.wait_ge(added, Z * BATCH + (k + BATCH))
                        dve.wait_ge(sums_ready, Z * BATCH + (2 * SC + k + 1))
                        nc.vector.tensor_tensor(a, a, P_z[k][0:BN, 0:ACCW], ALU.add).then_inc(added, 1)

                if exists(Z):
                    regs = buckets(DVE_ENGINE, Z * BATCH, BATCH)
                    dve.wait_ge(acc_rescaled, gz + 1)
                add_sums(0)
                if b == 1 and maxima:
                    full_maxima(m)
                add_sums(1)
                if exists(B):
                    dve.wait_ge(keys_ready, B + 2)
                    dve.wait_ge(q_ready, B + 3)
                    dve.wait_ge(score_ready, B + (NBATCH + 1))
                    nc.vector.tensor_tensor(product[:], keys[:, bb % 2], P_q[:], ALU.mult).then_inc(product_ready, 1)
                add_sums(2)
                if b == 0 and maxima:
                    mark_changes(m)
                add_sums(3)
                if b == 0 and maxima:
                    scale_changes(m)
                    scan_forward(m)
                if exists(B):
                    dve.wait_ge(product_ready, B + 2)
                    dve.wait_ge(rows_transposed, n + 1)
                    k0 = bb * BATCH // PT
                    nc.vector.tensor_reduce(score[:, pg, :, k0:k0 + BATCH // PT, :].rearrange("p i k h -> p k i h"),
                                            product[:].rearrange("p (k i h d) -> p k i h d", i=PT, h=HEADS, d=HEAD_QK), AX.X, ALU.add).then_inc(score_ready, 1)
                if b == 0 and maxima:
                    scan_backward(m)
                if b == 1 and maxima:
                    factors(m)
                if exists(V):
                    tiles = slice(bv * BATCH, (bv + 1) * BATCH)
                    dve.wait_ge(weights_ready, gv + 1)
                    dve.wait_ge(sums_ready, V * BATCH + (2 * SC - BATCH))
                    nc.vector.tensor_tensor(weighted[:, bv % 2, :, :, 0:HEAD_V],
                                            kv[:, pv, tiles, QK:KV].rearrange("p t (h d) -> p t h d", d=HEAD_V),
                                            weights[:, tiles, :].unsqueeze(3).broadcast_to([128, BATCH, HEADS, HEAD_V]), ALU.mult).then_inc(weighted_ready, 1)
                if b == 0 and maxima:
                    gaps(m)
                    penalties(m)
                    carries(m)
                if b == 2 and maxima:
                    rescale_carried(m, 1 - p)

            all_steps(dve, step)

        @block.tensor
        def _(pe):
            pe.sem_inc(q_ready, 2)
            pe.sem_inc(rows_transposed, 2)
            pe.sem_inc(weights_transposed, 1)
            pe.sem_inc(sums_ready, 2 * SC)
            pe.wait_ge(ident_ready, 1)

            def step(n, p, b):
                m = n - 1
                Z, gz, pz, bz = batch(n, p, b, -SUM_LAG)

                def sums(tiles):
                    if exists(Z):
                        pe.wait_ge(weighted_ready, Z + (2 * NBATCH + 1))
                        pe.wait_ge(den_ready, Z + 2)
                        for k in tiles:
                            pe.wait_ge(added, Z * BATCH + (k + 1))
                            nc.tensor.matmul(P_z[k][0:BN, 0:ACCW], onehot[:, pz, bz * BATCH + k], weighted[:, bz % 2, k].rearrange("p h d -> p (h d)"),
                                             start=True, stop=True).then_inc(sums_ready, 1)

                if b == 0 and exists(m, NSC):
                    pe.wait_ge(score_ready, m * NBATCH + (2 * NBATCH + 1))
                    pe.wait_ge(src_wide_ready, m + 3)
                    pe.wait_ge(rescaled, m + 2)
                    for i in range(PT):
                        nc.tensor.transpose(P_max[:, i * 128:(i + 1) * 128], score[:, 1 - p, i].rearrange("p k h -> p (k h)"), ident[:])
                    for i in range(PT):
                        last = nc.tensor.transpose(P_max[:, W + i * 128:W + (i + 1) * 128], src_wide[:, i].rearrange("p k h -> p (k h)"), ident[:])
                    last.then_inc(rows_transposed, 1)
                if b == 2 and exists(m, NSC):
                    pe.wait_ge(max_step, m * MAX_STEPS + MAX_STEPS)
                    pe.wait_ge(weights_ready, m + 1)
                    nc.tensor.matmul(P_max[0:BN, 0:HEADS], ones[0:HEADS, 0:BN], factor[:], start=True, stop=True).then_inc(factor_spread, 1)
                B, g, pg, bb = batch(n, p, b, 1)
                A, ga, pa, ba = batch(n, p, b, 2)
                if exists(A):
                    pe.wait_ge(part_ready, ga * 3 + 3)
                    pe.wait_ge(node_rows_ready, A + 1)
                    pe.wait_ge(attr_rows_ready, A + 1)
                    for k in range(BATCH):
                        last = nc.tensor.transpose(P_parts[:, k * 128:(k + 1) * 128], parts[:, pa, ba * BATCH + k].rearrange("p j a -> p (j a)"), ident_b[:])
                    last.then_inc(attr_transposed, 1)
                if b == 1 and exists(m, NSC):
                    pe.wait_ge(max_step, m * MAX_STEPS + 13)
                    pe.sem_inc(carry_seen, 1)
                    for j in range(2):
                        last = nc.tensor.transpose(P_max[:, W + j:W + j + 1], carry_rows[:, j].rearrange("a k h -> a (k h)"), ident[0:1, 0:1])
                    last.then_inc(carry_transposed, 1)
                if exists(B):
                    pe.wait_ge(attr_rows_ready, B + 2)
                    if isinstance(B, int) and B == 0:
                        pe.wait_ge(weights_spread, 16 * PAIRS)
                    pe.wait_ge(keys_ready, B + 1)
                    pe.wait_ge(kv_in[pg * NBATCH + bb], (g - pg) * 32 + 64)
                    for k in range(BATCH):
                        cols = slice(k * 128, (k + 1) * 128)
                        nc.tensor.matmul(P_k[:, cols], attr_rows[:, bb % 2, cols], wstack[:, 1, :], start=True, stop=False)
                        last = nc.tensor.matmul(P_k[:, cols], ident[:], kv[:, pg, bb * BATCH + k, 0:QK], start=False, stop=True)
                    last.then_inc(k_ready, 1)
                if b == 0 and exists(m, NSC):
                    pe.wait_ge(rows_ready, m + 1)
                    for j, col in ((1, cs[:, W:W + 1]), (3, cs[:, 2 * W - 1:2 * W])):
                        last = nc.tensor.transpose(P_max[0:1, j * 128:(j + 1) * 128], col, ident[:])
                    last.then_inc(end_sources_transposed, 1)
                if exists(B):
                    pe.wait_ge(onehot_ready, B + 1)
                    pe.wait_ge(attr_rows_ready, A + 2 if exists(A) else A + 1)
                    for k in range(BATCH):
                        last = nc.tensor.transpose(P_rows[0:BN, k * 128:(k + 1) * 128], onehot[:, pg, bb * BATCH + k], ident[:])
                    last.then_inc(node_transposed, 1)
                early = 1 if b == 1 and exists(m, NSC) else 0
                sums(range(early))
                if b == 1 and exists(m, NSC):
                    pe.wait_ge(exp_ready, m + 2)
                    for i in range(PT):
                        last = nc.tensor.transpose(P_max[:, i * 128:(i + 1) * 128], weight_rows[:, i * 128:(i + 1) * 128], ident[:])
                    last.then_inc(weights_transposed, 1)
                sums(range(early, BATCH))
                if b == 0 and exists(m, NSC):
                    pe.wait_ge(max_step, m * MAX_STEPS + 4)
                    pe.wait_ge(end_sources_ready, m + 1)
                    for j, col in ((0, run[:, 1, 0:1]), (2, run[:, 1, W - 1:W])):
                        last = nc.tensor.transpose(P_max[0:1, j * 128:(j + 1) * 128], col, ident[:])
                    last.then_inc(ends_transposed, 1)
                if exists(B):
                    regs = buckets(PE_ENGINE, B * BATCH, BATCH)
                    pe.wait_ge(node_rows_ready, B + 3)
                    pe.wait_ge(product_ready, B + 1)
                    for k in range(BATCH):
                        cols = slice(k * 128, (k + 1) * 128)
                        q = c["q"][:, bass.ds(regs[k], 1), :].rearrange("p a d -> p (a d)")
                        nc.tensor.matmul(P_q[:, cols], attr_rows[:, bb % 2, cols], wstack[:, 0, :], start=True, stop=False)
                        last = nc.tensor.matmul(P_q[:, cols], node_rows[:, bb % 2, cols], q, start=False, stop=True)
                    last.then_inc(q_ready, 1)

            all_steps(pe, step)


def feed_forward(nc, c, wr, br, w1, b1, w2, b2, route_dram, out):
    GB = 5
    GN = GB * BN
    NG = NB // GB
    FC = HIDDEN // 128
    SPLIT = [(0, 320), (320, GN - 320)]
    with ExitStack() as ctx:
        def sb(name, shape, dt=F32):
            return ctx.enter_context(nc.sbuf_tensor(name, shape, dt))

        def ps(name):
            return ctx.enter_context(nc.psum_tensor(name, [128, 512], F32))

        def sem(name):
            return ctx.enter_context(nc.semaphore(name))

        x, acc, ident, below = c["x"], c["acc"], c["ident"], c["below"]
        y = acc
        compared = c["q"][:].rearrange("p b d -> p (b d)")
        w1_sb = sb("w1_sb", [128, 2, HIDDEN])
        w2_sb = sb("w2_sb", [128, FC, DIM])
        b1_sb = sb("b1_sb", [128, FC])
        b2_sb = sb("b2_sb", [BN, DIM])
        wr_sb = sb("wr_sb", [BN, DIM])
        br_sb = sb("br_sb", [BN, 1])
        inverse = sb("inverse", [BN, NB, HEADS])
        stats = sb("ff_stats", [BN, GB, 6])
        mean_var = sb("ff_mean_var", [BN, NB, 2])
        mean_var5 = sb("ff_mean_var_of_group", [BN, GB, 2])
        spread = sb("ff_spread", [BN, 3, NB])
        normed = sb("ff_normed", [BN, NB, DIM])
        normed_t = sb("ff_normed_t", [128, 2, NODES])
        hidden = sb("hidden", [128, FC, GN])
        stage = sb("stage", [BN, GB, DIM])
        routed = sb("routed", [BN, GB, DIM])
        route5 = sb("route5", [BN, GB])
        route = sb("route", [BN, NB])
        route_t = sb("route_t", [NB, BN])
        route_row = sb("route_row", [BN, NODES])
        counts = sb("counts", [BN, NB, 3])
        rank = sb("ff_rank", [BN, NB])
        gain = sb("gain", [BN, NB])
        P_h = [[ps(f"ps_h{i}{j}") for j in range(2)] for i in range(2)]
        P_y = [ps(f"ps_y{i}") for i in range(2)]
        P_t = [ps(f"ps_t{i}") for i in range(2)]
        P_r = P_t[1]

        loaded = sem("loaded")
        inverse_step = sem("inverse_step")
        att_step = sem("att_step")
        stats_seen = sem("stats_seen")
        root_ready = sem("ff_root_ready")
        inv_root = sem("inv_root")
        normed_ready = sem("ff_normed_ready")
        routed_ready = sem("routed_ready")
        residual_ready = sem("residual_ready")
        transposed = sem("ff_transposed")
        normed_t_ready = sem("normed_t_ready")
        up_ready = sem("up_ready")
        hidden_ready = sem("hidden_ready")
        down_ready = sem("down_ready")
        y_ready = sem("y_ready")
        route_transposed = sem("route_transposed")
        route_t_ready = sem("route_t_ready")
        route_out = sem("route_out")
        route_in = sem("route_in")
        rank_step = sem("rank_step")
        bias_added = sem("bias_added")
        result_ready = sem("result_ready")
        stored = sem("stored")
        staged = sem("staged")
        spread_ready = sem("spread_ready")
        route_ready = sem("route_ready")
        block = ctx.enter_context(nc.Block())

        @block.sync
        def _(sp):
            sp.dma_start(wr_sb[:], wr.rearrange("d a -> a d").broadcast_to([BN, DIM])).then_inc(loaded, 16)
            sp.dma_start(br_sb[:], br.rearrange("(a n) -> a n", a=1).broadcast_to([BN, 1])).then_inc(loaded, 16)
            sp.dma_start(w1_sb[:], w1.rearrange("(k p) n -> p k n", p=128)).then_inc(loaded, 16)
            with nc.allow_non_contiguous_dma(reason="1024 biases, once"):
                sp.dma_start(b1_sb[:], b1.rearrange("(f p) -> p f", p=128)).then_inc(loaded, 16)
            sp.dma_start(w2_sb[:], w2.rearrange("(f p) n -> p f n", p=128)).then_inc(loaded, 16)
            sp.dma_start(b2_sb[:], b2.rearrange("(a n) -> a n", a=1).broadcast_to([BN, DIM])).then_inc(loaded, 16)
            sp.wait_ge(route_t_ready, 1)
            sp.dma_start(route_dram.rearrange("(b p) -> b p", p=BN), route_t[:]).then_inc(route_out, 16)
            sp.wait_ge(route_out, 16)
            sp.dma_start(route_row[:], route_dram.rearrange("(a n) -> a n", a=1).broadcast_to([BN, NODES])).then_inc(route_in, 16)
            out_v = out.rearrange("(b p) d -> p b d", p=BN)
            for g in range(NG):
                sp.wait_ge(result_ready, GB * (g + 1))
                sp.dma_start(out_v[:, g * GB:(g + 1) * GB, :], x[:, g * GB:(g + 1) * GB, :]).then_inc(stored, 16)
            sp.wait_ge(stored, 16 * NG)

        rest = slice(GB, NB)

        @block.scalar
        def _(act):
            act.sem_inc(normed_t_ready, 1)
            act.sem_inc(hidden_ready, 4)
            act.sem_inc(y_ready, 2)

            def copy_stage(g):
                act.wait_ge(transposed, g * 2 + 1)
                nc.scalar.activation(stage[:], normed[:, bass.ds(g * GB, GB), :], ACT.Copy).then_inc(staged, 1)

            def copy_transposed(g, k):
                act.wait_ge(transposed, g * 2 + (k + 2))
                nc.scalar.activation(normed_t[:, k, bass.ds(g * GN, 4 * BN)], P_t[0][:, 0:4 * BN], ACT.Copy)
                nc.scalar.activation(normed_t[:, k, bass.ds(g * GN + 4 * BN, BN)], P_t[1][:, 0:BN], ACT.Copy).then_inc(normed_t_ready, 1)

            def rest_roots():
                act.wait_ge(spread_ready, 2)
                nc.scalar.activation(spread[:, 1, rest], spread[:, 0, rest], ACT.Sqrt).then_inc(root_ready, 1)

            def up(g):
                act.wait_ge(down_ready, g * GB + 1)
                for f in range(FC):
                    if isinstance(g, int) and g == 0 and f == 6:
                        rest_roots()
                    for j, (at, n) in enumerate(SPLIT):
                        act.wait_ge(up_ready, g * (2 * FC) + (2 * f + j + 1))
                        nc.scalar.activation(hidden[:, f, at:at + n], P_h[f % 2][j][:, 0:n], ACT.Gelu_apprx_tanh,
                                             bias=b1_sb[:, f:f + 1]).then_inc(hidden_ready, 1)

            def down(g, more):
                for b in range(GB):
                    act.wait_ge(down_ready, g * GB + (b + 2))
                    nc.scalar.activation(y[:, bass.ds(g * GB + b, 1), 0:DIM].rearrange("p a d -> p (a d)"), P_y[b % 2][0:BN, 0:DIM], ACT.Copy).then_inc(y_ready, 1)
                    if more and b in (1, 3):
                        copy_transposed(g + 1, b // 2)

            act.wait_ge(spread_ready, 1)
            nc.scalar.activation(spread[:, 1, 0:GB], spread[:, 0, 0:GB], ACT.Sqrt).then_inc(root_ready, 1)
            act.wait_ge(normed_ready, 1)
            copy_stage(0)
            copy_transposed(0, 0)
            copy_transposed(0, 1)
            act.wait_ge(loaded, 96)
            up(0)
            act.wait_ge(normed_ready, 2)
            copy_stage(1)
            down(0, True)
            act.wait_ge(normed_ready, NG)
            act.wait_ge(route_transposed, 1)
            nc.scalar.activation(route_t[:], P_r[0:NB, 0:BN], ACT.Copy).then_inc(route_t_ready, 1)
            with act.Fori(0, NG - 2) as t:
                copy_stage(t + 2)
                up(t + 1)
                down(t + 1, True)
            up(NG - 1)
            down(NG - 1, False)

        @block.vector
        def _(dve):
            def inverse_sums(groups, part):
                nc.vector.tensor_scalar(inverse[:, groups], acc[:, groups].rearrange("p b (h d) -> p b h d", d=VD)[:, :, :, HEAD_V], EPS_DEN, None, ALU.add).then_inc(inverse_step, 1)
                dve.wait_ge(inverse_step, 2 * part - 1)
                nc.vector.reciprocal(inverse[:, groups], inverse[:, groups]).then_inc(inverse_step, 1)
                dve.wait_ge(inverse_step, 2 * part)


            def residual_and_stats(g):
                five = bass.ds(g * GB, GB)
                sums = acc[:, five, :].rearrange("p b (h d) -> p (b h) d", d=VD)[:, :, 0:HEAD_V]
                nc.vector.tensor_tensor(sums, sums, inverse[:, five, :].rearrange("p b h -> p (b h)").unsqueeze(2).broadcast_to([BN, GB * HEADS, HEAD_V]), ALU.mult).then_inc(att_step, 1)
                dve.wait_ge(att_step, g * 5 + 1)
                nc.vector.tensor_tensor(x[:, five, :].rearrange("p b (h d) -> p (b h) d", d=HEAD_V), x[:, five, :].rearrange("p b (h d) -> p (b h) d", d=HEAD_V), sums, ALU.add).then_inc(att_step, 1)
                dve.wait_ge(att_step, g * 5 + 2)
                dve.sem_inc(stats_seen, 1)
                for b in range(GB):
                    last = nc.vector.bn_stats(stats[:, b], x[:, bass.ds(g * GB + b, 1), :].rearrange("p a d -> p (a d)"))
                last.then_inc(att_step, 1)
                dve.wait_ge(att_step, g * 5 + 3)
                dve.sem_inc(stats_seen, 1)
                for b in range(GB):
                    last = nc.vector.bn_aggr(mean_var5[:, b], stats[:, b])
                last.then_inc(att_step, 1)
                dve.wait_ge(att_step, g * 5 + 4)
                nc.vector.tensor_copy(mean_var[:, five], mean_var5[:]).then_inc(att_step, 1)

            def inverse_root(groups, part):
                nc.vector.tensor_scalar(spread[:, 0, groups], mean_var[:, groups, 1], EPS_LN, None, ALU.add).then_inc(spread_ready, 1)
                dve.wait_ge(root_ready, part)
                nc.vector.reciprocal(spread[:, 2, groups], spread[:, 1, groups]).then_inc(inv_root, 1)
                dve.wait_ge(inv_root, part)

            def normalise(g):
                for b in range(GB):
                    last = nc.vector.tensor_scalar(normed[:, bass.ds(g * GB + b, 1), :].rearrange("p a d -> p (a d)"),
                                                   x[:, bass.ds(g * GB + b, 1), :].rearrange("p a d -> p (a d)"),
                                                   mean_var[:, bass.ds(g * GB + b, 1), 0:1].rearrange("p a d -> p (a d)"),
                                                   spread[:, 2, bass.ds(g * GB + b, 1)], ALU.subtract, ALU.mult)
                last.then_inc(normed_ready, 1)

            def router(g, done):
                five = bass.ds(g * GB, GB)
                dve.wait_ge(normed_ready, g + 1)
                for b in range(GB):
                    last = nc.vector.scalar_tensor_tensor(routed[:, b], normed[:, bass.ds(g * GB + b, 1), :].rearrange("p a d -> p (a d)"), 1.0,
                                                          wr_sb[:], ALU.mult, ALU.mult, accum_out=route5[:, b:b + 1])
                last.then_inc(routed_ready, 1)
                nc.vector.tensor_tensor(x[:, five, :], x[:, five, :], normed[:, five, :], ALU.add).then_inc(residual_ready, 1)
                dve.wait_ge(routed_ready, done)
                nc.vector.tensor_scalar(route[:, five], route5[:], br_sb[:], None, ALU.add).then_inc(route_ready, 1)

            inverse_sums(slice(0, GB), 1)
            residual_and_stats(0)
            dve.wait_ge(att_step, 5)
            inverse_root(slice(0, GB), 1)
            normalise(0)
            inverse_sums(rest, 2)
            with dve.Fori(0, NG - 1) as t:
                residual_and_stats(t + 1)
            dve.wait_ge(att_step, 5 * NG)
            inverse_root(rest, 2)
            dve.wait_ge(loaded, 96)
            with dve.Fori(0, NG - 1) as t:
                normalise(t + 1)
                router(t + 1, t + 1)
            dve.wait_ge(route_ready, NG - 1)
            router(0, NG)
            dve.wait_ge(route_in, 16)
            for b in range(NB):
                w = route[:, b:b + 1]
                at = b * BN
                if b:
                    dve.wait_ge(rank_step, 3 * b)
                    nc.vector.tensor_scalar(compared[:, 0:at], route_row[:, 0:at], w, 0.0, ALU.is_ge, ALU.add, accum_out=counts[:, b, 0:1]).then_inc(rank_step, 1)
                else:
                    nc.vector.memset(counts[:, 0, 0:1], 0.0).then_inc(rank_step, 1)
                nc.vector.tensor_scalar(compared[:, at:NODES], route_row[:, at:NODES], w, 0.0, ALU.is_gt, ALU.add, accum_out=counts[:, b, 1:2]).then_inc(rank_step, 1)
                nc.vector.scalar_tensor_tensor(routed[:, b % GB, 0:BN], route_row[:, at:at + BN], w, below[0:BN, 0:BN], ALU.is_equal, ALU.mult,
                                               accum_out=counts[:, b, 2:3]).then_inc(rank_step, 1)
            dve.wait_ge(rank_step, 3 * NB)
            nc.vector.tensor_reduce(rank[:], counts[:], AX.X, ALU.add).then_inc(rank_step, 1)
            dve.wait_ge(rank_step, 3 * NB + 1)
            nc.vector.scalar_tensor_tensor(gain[:], rank[:], float(KEPT), route[:], ALU.is_lt, ALU.mult).then_inc(rank_step, 1)
            dve.wait_ge(rank_step, 3 * NB + 2)
            for b in range(NB):
                nc.vector.scalar_tensor_tensor(x[:, b, :], b2_sb[:], gain[:, b:b + 1], x[:, b, :], ALU.mult, ALU.add).then_inc(bias_added, 1)
            for b in range(NB):
                dve.wait_ge(bias_added, b + 1)
                dve.wait_ge(y_ready, b + 3)
                nc.vector.scalar_tensor_tensor(x[:, b, :], y[:, b, 0:DIM], gain[:, b:b + 1], x[:, b, :], ALU.mult, ALU.add).then_inc(result_ready, 1)

        @block.tensor
        def _(pe):
            pe.sem_inc(down_ready, 1)
            pe.sem_inc(transposed, 1)

            def transpose(g, k):
                pe.wait_ge(staged, g + 1)
                pe.wait_ge(normed_t_ready, g * 2 + (k + 1))
                for b in range(GB):
                    last = nc.tensor.transpose(P_t[b // 4][:, (b % 4) * BN:(b % 4 + 1) * BN],
                                               stage[:, b, k * 128:(k + 1) * 128], ident[0:BN, 0:BN])
                last.then_inc(transposed, 1)

            def up(g):
                pe.wait_ge(normed_t_ready, g * 2 + 3)
                for f in range(FC):
                    for j, (at, n) in enumerate(SPLIT):
                        pe.wait_ge(hidden_ready, g * (2 * FC) + (2 * f + j + 1))
                        for k in range(2):
                            last = nc.tensor.matmul(P_h[f % 2][j][:, 0:n], w1_sb[:, k, f * 128:(f + 1) * 128],
                                                    normed_t[:, k, bass.ds(g * GN + at, n)], start=(k == 0), stop=(k == 1))
                        last.then_inc(up_ready, 1)

            def down(g, more):
                for b in range(GB):
                    pe.wait_ge(y_ready, g * GB + (b + 1))
                    for f in range(FC):
                        if b == 0:
                            pe.wait_ge(hidden_ready, g * (2 * FC) + (2 * f + 6))
                        last = nc.tensor.matmul(P_y[b % 2][0:BN, 0:DIM], hidden[:, f, b * BN:(b + 1) * BN], w2_sb[:, f, :], start=(f == 0), stop=(f == FC - 1))
                    last.then_inc(down_ready, 1)
                    if more and b in (1, 3):
                        transpose(g + 1, b // 2)

            transpose(0, 0)
            transpose(0, 1)
            pe.wait_ge(loaded, 96)
            up(0)
            down(0, True)
            pe.wait_ge(route_ready, NG)
            pe.wait_ge(normed_t_ready, 5)
            nc.tensor.transpose(P_r[0:NB, 0:BN], route[:], ident[0:BN, 0:BN]).then_inc(route_transposed, 1)
            with pe.Fori(0, NG - 2) as t:
                pe.wait_ge(route_t_ready, 1)
                up(t + 1)
                down(t + 1, True)
            up(NG - 1)
            down(NG - 1, False)


_INS = ["x", "src", "dst", "edge_attr_18", "L0_gnn_Wqkv", "L0_gnn_bqkv", "L0_gnn_Wk_rpe", "L0_gnn_bk_rpe", "L0_gnn_Wq_rpe", "L0_gnn_bq_rpe",
        "L0_ffn_attention_mask", "L0_ffn_wr", "L0_ffn_br", "L0_ffn_w1", "L0_ffn_b1", "L0_ffn_w2", "L0_ffn_b2"]
_OUTS = [((NODES, DIM), "float32")]


def kernel(**inputs):
    import numpy as _np
    import concourse.bacc as _bacc
    from concourse import mybir as _mybir
    from concourse.bass_utils import run_bass_kernel_spmd as _run

    nc = _bacc.Bacc("TRN2", target_bir_lowering=False, num_devices=1)
    arrays, args = {}, []
    for name in _INS:
        a = _np.ascontiguousarray(inputs[name])
        arrays[f"in_{name}_dram"] = a
        args.append(nc.dram_tensor(f"in_{name}_dram", a.shape, _mybir.dt.from_np(a.dtype), kind="ExternalInput").ap())
    for i, (shape, dtype) in enumerate(_OUTS):
        dt = _mybir.dt.from_np(_np.dtype(dtype))
        args.append(nc.dram_tensor(f"out_{i}_dram", shape, dt, kind="ExternalOutput").ap())
    gnn_ffn_kernel(nc, *args)
    r = _run(nc, [arrays], core_ids=[0])
    return r.results[0]["out_0_dram"]
```
